# Optimizing a Trainium2 kernel written in Bass

```python
import numpy as np
import jax
import jax.numpy as jnp

def _softmax(x, axis=-1):
    return jax.nn.softmax(x, axis=axis)

def _gelu(x):
    return jax.nn.gelu(x, approximate=True)

def _silu(x):
    return jax.nn.silu(x)

def _sigmoid(x):
    return jax.nn.sigmoid(x)

def _layernorm(x, axis=-1, eps=1e-05):
    m = jnp.mean(x, axis=axis, keepdims=True)
    v = jnp.var(x, axis=axis, keepdims=True)
    return (x - m) / jnp.sqrt(v + eps)

def _scatter_add(tgt, idx, src, axis=0):
    return tgt.at[idx].add(src)

def _segment_sum(src, seg, n):
    return jax.ops.segment_sum(src, seg, n)
kernel_name = 'mk_decoder_preln_d2_seqx_r8_edceaf'

def setup_inputs(seed: int=0):
    np.random.seed(seed)
    _w = jnp.asarray

    def _rec_inputs():
        import jax
        import jax.numpy as jnp
        _rk = jax.random.key(seed)
        x = 7.22e-05 + 1 * jax.random.normal(jax.random.fold_in(_rk, 1), (16, 64, 256), jnp.float32)
        _lenS = 64 - jax.random.randint(jax.random.fold_in(_rk, 7), (16,), 0, max(1, 64 // 4) + 1, jnp.int32)
        _lenS2 = 64 - jax.random.randint(jax.random.fold_in(_rk, 8), (16,), 0, max(1, 64 // 4) + 1, jnp.int32)
        _ctx_1024P = jax.random.normal(jax.random.fold_in(_rk, 11), (16, 16, 128), jnp.float32)
        _ctx_1024c = jax.random.dirichlet(jax.random.fold_in(_rk, 511), 0.3 * jnp.ones((16,), jnp.float32), (16, 64))
        _ctx_1024t = jnp.einsum('bsk,bkd->bsd', _ctx_1024c, _ctx_1024P)
        _ctx_1024t = _ctx_1024t * jax.lax.rsqrt(jnp.mean(jnp.square(_ctx_1024t)) + 1e-12) * 0.953939
        ctx_1024 = -1.39393e-06 + 0.999914 * (_ctx_1024t + 0.3 * jax.random.normal(jax.random.fold_in(_rk, 611), (16, 64, 128), jnp.float32))
        fside_BxSx2_0 = jax.random.uniform(jax.random.fold_in(_rk, 12), (16, 64, 2), jnp.float32, 0.0, 0.999707)
        _validS = jnp.arange(64)[None, :] < _lenS[:, None]
        _validS2 = jnp.arange(64)[None, :] < _lenS2[:, None]
        _causal = jnp.tril(jnp.ones((64, 64), dtype=bool))
        mask_BxS2_bf1 = jnp.ones((16, 64), dtype=bool)
        return (x, ctx_1024, fside_BxSx2_0, mask_BxS2_bf1)
    x, ctx_1024, fside_BxSx2_0, mask_BxS2_bf1 = _rec_inputs()

    def _L0_attn_setup():
        import jax, jax.numpy as jnp
        import numpy as np
        HIDDEN = 256
        NUM_HEADS = 16
        HEAD_DIM = HIDDEN // NUM_HEADS
        WORLD_SIZE = 4
        BATCH = 1
        SEQ_SHARD = 256

        def _ring_attention(q, k, v):
            B, H, S, D = q.shape
            scale = 1.0 / np.sqrt(D)
            output_acc = jnp.zeros_like(q)
            max_score = jnp.full((B, H, S, 1), -jnp.inf, dtype=q.dtype)
            sum_exp = jnp.zeros((B, H, S, 1), dtype=q.dtype)
            for _ in range(WORLD_SIZE):
                scores = jnp.einsum('bhsd,bhtd->bhst', q, k) * scale
                new_max = jnp.max(scores, axis=-1, keepdims=True)
                combined_max = jnp.maximum(max_score, new_max)
                old_scale = jnp.exp(max_score - combined_max)
                new_scale = jnp.exp(new_max - combined_max)
                new_exp = jnp.exp(scores - new_max)
                sum_exp = sum_exp * old_scale + jnp.sum(new_exp, axis=-1, keepdims=True) * new_scale
                output_acc = output_acc * old_scale + jnp.einsum('bhst,bhtd->bhsd', new_exp, v) * new_scale
                max_score = combined_max
            return output_acc / sum_exp
        key = jax.random.key(seed)
        ks = jax.random.split(key, 9)
        s = 1.0 / np.sqrt(HIDDEN)
        return {'hidden_states': jax.random.normal(ks[0], (BATCH, SEQ_SHARD, HIDDEN), jnp.float32), 'wq': jax.random.normal(ks[1], (HIDDEN, HIDDEN), jnp.float32) * s, 'bq': jax.random.normal(ks[2], (HIDDEN,), jnp.float32) * s, 'wk': jax.random.normal(ks[3], (HIDDEN, HIDDEN), jnp.float32) * s, 'bk': jax.random.normal(ks[4], (HIDDEN,), jnp.float32) * s, 'wv': jax.random.normal(ks[5], (HIDDEN, HIDDEN), jnp.float32) * s, 'bv': jax.random.normal(ks[6], (HIDDEN,), jnp.float32) * s, 'wo': jax.random.normal(ks[7], (HIDDEN, HIDDEN), jnp.float32) * s, 'bo': jax.random.normal(ks[8], (HIDDEN,), jnp.float32) * s}
    _L0_attn_all = _L0_attn_setup()
    _L0_attn_in = {k: v for k, v in _L0_attn_all.items() if k in ('wq', 'bq', 'wk', 'bk', 'wv', 'bv', 'wo', 'bo')}
    del _L0_attn_all

    def _L0_xattn_setup():
        import jax, jax.numpy as jnp
        import numpy as np
        DIM = 256
        CTX_DIM = 128
        N_HEADS = 32
        HEAD_DIM = DIM // N_HEADS
        POS_DIM = 2
        B, N, CTXN = (2, 256, 256)
        ROPE_BASE = 10000.0

        def apply_axial_rope(x, pos):
            b, n, h, d = x.shape
            p = pos.shape[-1]
            dpa = d // p
            half = dpa // 2
            freqs = ROPE_BASE ** (-jnp.arange(half, dtype=x.dtype) / half)
            ang = pos[..., :, None] * freqs
            cos = jnp.cos(ang)[:, :, None, :, :]
            sin = jnp.sin(ang)[:, :, None, :, :]
            xr = x.reshape(b, n, h, p, half, 2)
            x1, x2 = (xr[..., 0], xr[..., 1])
            out = jnp.stack([x1 * cos - x2 * sin, x1 * sin + x2 * cos], axis=-1)
            return out.reshape(b, n, h, d)
        key = jax.random.key(seed)
        ks = jax.random.split(key, 8)
        x = jax.random.normal(ks[0], (B, N, DIM), jnp.float32)
        ctx = jax.random.normal(ks[1], (B, CTXN, CTX_DIM), jnp.float32)
        pos_map = jax.random.uniform(ks[2], (B, N, POS_DIM), jnp.float32)
        ctx_pos_map = jax.random.uniform(ks[3], (B, CTXN, POS_DIM), jnp.float32)
        Wq = jax.random.normal(ks[4], (DIM, DIM), jnp.float32) / np.sqrt(DIM)
        Wkv = jax.random.normal(ks[5], (CTX_DIM, 2 * DIM), jnp.float32) / np.sqrt(CTX_DIM)
        Wout = jax.random.normal(ks[6], (DIM, DIM), jnp.float32) / np.sqrt(DIM)
        bout = jnp.zeros((DIM,), jnp.float32)
        return {'x': x, 'ctx': ctx, 'pos_map': pos_map, 'ctx_pos_map': ctx_pos_map, 'Wq': Wq, 'Wkv': Wkv, 'Wout': Wout, 'bout': bout}
    _L0_xattn_all = _L0_xattn_setup()
    _L0_xattn_in = {k: v for k, v in _L0_xattn_all.items() if k in ('Wq', 'Wkv', 'Wout', 'bout')}
    del _L0_xattn_all

    def _L0_ffn_setup():
        import jax, jax.numpy as jnp
        import numpy as np
        H = 256
        I = 128
        K = 8
        E = 128
        TOPK = 4
        EPS = 1e-08
        key = jax.random.key(seed)
        ks = jax.random.split(key, 10)
        s = 0.02
        return {'x': jax.random.normal(ks[0], (4, 256, H), jnp.float32), 'w_router': jax.random.normal(ks[1], (H, E), jnp.float32) * s, 'w_gate': jax.random.normal(ks[2], (H, K * I), jnp.float32) * s, 'w_up': jax.random.normal(ks[3], (H, K * I), jnp.float32) * s, 'w_down': jax.random.normal(ks[4], (I, H), jnp.float32) * s, 'amplitudes': jax.random.normal(ks[5], (E, K, 2), jnp.float32) * 0.1, 'expert_scale': jnp.ones((E,), jnp.float32), 'shared_w_gate': jax.random.normal(ks[6], (H, 2 * I), jnp.float32) * s, 'shared_w_up': jax.random.normal(ks[7], (H, 2 * I), jnp.float32) * s, 'shared_w_down': jax.random.normal(ks[8], (2 * I, H), jnp.float32) * s}
    _L0_ffn_all = _L0_ffn_setup()
    _L0_ffn_in = {k: v for k, v in _L0_ffn_all.items() if k in ('w_router', 'w_gate', 'w_up', 'w_down', 'amplitudes', 'expert_scale', 'shared_w_gate', 'shared_w_up', 'shared_w_down')}
    del _L0_ffn_all

    def _L1_attn_setup():
        import jax, jax.numpy as jnp
        import numpy as np
        B, S, H_DIM = (2, 256, 256)
        N_HEADS, D_HEAD = (16, 128)
        key = jax.random.key(seed)
        k1, k2, k3 = jax.random.split(key, 3)
        x = jax.random.normal(k1, (B, S, H_DIM), dtype=jnp.float32)
        w_qkv = jax.random.normal(k2, (H_DIM, 3 * N_HEADS * D_HEAD), dtype=jnp.float32) * 0.02
        w_o = jax.random.normal(k3, (N_HEADS * D_HEAD, H_DIM), dtype=jnp.float32) * 0.02
        return {'x': x, 'w_qkv': w_qkv, 'w_o': w_o}
    _L1_attn_all = _L1_attn_setup()
    _L1_attn_in = {k: v for k, v in _L1_attn_all.items() if k in ('w_qkv', 'w_o')}
    del _L1_attn_all

    def _L1_xattn_setup():
        import jax, jax.numpy as jnp
        import numpy as np
        N_HEADS = 16
        N_KV_HEADS = 8
        HEAD_DIM = 128
        D_TEXT = 256
        D_VISION = 128
        GROUPS = N_HEADS // N_KV_HEADS
        key = jax.random.key(seed)
        ks = jax.random.split(key, 6)
        B, T_text, T_vis = (4, 256, 72)
        text_hidden = jax.random.normal(ks[0], (B, T_text, D_TEXT), dtype=jnp.float32)
        vision_tokens = jax.random.normal(ks[1], (B, T_vis, D_VISION), dtype=jnp.float32)
        vision_mask = jnp.ones((B, T_vis), dtype=bool)
        s = 0.02
        Wq = jax.random.normal(ks[2], (D_TEXT, N_HEADS * HEAD_DIM), dtype=jnp.float32) * s
        Wk = jax.random.normal(ks[3], (D_VISION, N_KV_HEADS * HEAD_DIM), dtype=jnp.float32) * s
        Wv = jax.random.normal(ks[4], (D_VISION, N_KV_HEADS * HEAD_DIM), dtype=jnp.float32) * s
        Wo = jax.random.normal(ks[5], (N_HEADS * HEAD_DIM, D_TEXT), dtype=jnp.float32) * s
        return {'text_hidden': text_hidden, 'vision_tokens': vision_tokens, 'vision_mask': vision_mask, 'Wq': Wq, 'Wk': Wk, 'Wv': Wv, 'Wo': Wo}
    _L1_xattn_all = _L1_xattn_setup()
    _L1_xattn_in = {k: v for k, v in _L1_xattn_all.items() if k in ('Wq', 'Wk', 'Wv', 'Wo')}
    del _L1_xattn_all

    def _L1_ffn_setup():
        import jax, jax.numpy as jnp
        import numpy as np
        N_GROUPS = 4
        TOPK_GROUPS = 2
        TOPK = 4
        ROUTE_SCALE = 1.0

        def _gate(xt, gate_w):
            T = xt.shape[0]
            E = gate_w.shape[0]
            scores = jax.nn.sigmoid(xt @ gate_w.T)
            original_scores = scores
            sg = scores.reshape(T, N_GROUPS, E // N_GROUPS)
            group_scores = sg.max(axis=-1)
            _, gidx = jax.lax.top_k(group_scores, TOPK_GROUPS)
            gmask = jax.nn.one_hot(gidx, N_GROUPS, dtype=scores.dtype).sum(axis=1)
            masked = (sg * gmask[:, :, None]).reshape(T, E)
            _, idx = jax.lax.top_k(masked, TOPK)
            w = jnp.take_along_axis(original_scores, idx, axis=-1)
            w = w / w.sum(axis=-1, keepdims=True) * ROUTE_SCALE
            return (w, idx)
        key = jax.random.key(seed)
        ks = jax.random.split(key, 8)
        B, S, D = (1, 256, 256)
        E, I = (16, 176)
        SH = 2 * I
        s = 0.02
        return {'x': jax.random.normal(ks[0], (B, S, D), dtype=jnp.float32), 'gate_w': jax.random.normal(ks[1], (E, D), dtype=jnp.float32) * s, 'W1': jax.random.normal(ks[2], (E, I, D), dtype=jnp.float32) * s, 'W2': jax.random.normal(ks[3], (E, D, I), dtype=jnp.float32) * s, 'W3': jax.random.normal(ks[4], (E, I, D), dtype=jnp.float32) * s, 'Ws1': jax.random.normal(ks[5], (SH, D), dtype=jnp.float32) * s, 'Ws2': jax.random.normal(ks[6], (D, SH), dtype=jnp.float32) * s, 'Ws3': jax.random.normal(ks[7], (SH, D), dtype=jnp.float32) * s}
    _L1_ffn_all = _L1_ffn_setup()
    _L1_ffn_in = {k: v for k, v in _L1_ffn_all.items() if k in ('gate_w', 'W1', 'W2', 'W3', 'Ws1', 'Ws2', 'Ws3')}
    del _L1_ffn_all
    return {'x': x, 'ctx_1024': ctx_1024, 'fside_BxSx2_0': fside_BxSx2_0, 'mask_BxS2_bf1': mask_BxS2_bf1, 'L0_attn_wq': _L0_attn_in['wq'], 'L0_attn_bq': _L0_attn_in['bq'], 'L0_attn_wk': _L0_attn_in['wk'], 'L0_attn_bk': _L0_attn_in['bk'], 'L0_attn_wv': _L0_attn_in['wv'], 'L0_attn_bv': _L0_attn_in['bv'], 'L0_attn_wo': _L0_attn_in['wo'], 'L0_attn_bo': _L0_attn_in['bo'], 'L0_xattn_Wq': _L0_xattn_in['Wq'], 'L0_xattn_Wkv': _L0_xattn_in['Wkv'], 'L0_xattn_Wout': _L0_xattn_in['Wout'], 'L0_xattn_bout': _L0_xattn_in['bout'], 'L0_ffn_w_router': _L0_ffn_in['w_router'], 'L0_ffn_w_gate': _L0_ffn_in['w_gate'], 'L0_ffn_w_up': _L0_ffn_in['w_up'], 'L0_ffn_w_down': _L0_ffn_in['w_down'], 'L0_ffn_amplitudes': _L0_ffn_in['amplitudes'], 'L0_ffn_expert_scale': _L0_ffn_in['expert_scale'], 'L0_ffn_shared_w_gate': _L0_ffn_in['shared_w_gate'], 'L0_ffn_shared_w_up': _L0_ffn_in['shared_w_up'], 'L0_ffn_shared_w_down': _L0_ffn_in['shared_w_down'], 'L1_attn_w_qkv': _L1_attn_in['w_qkv'], 'L1_attn_w_o': _L1_attn_in['w_o'], 'L1_xattn_Wq': _L1_xattn_in['Wq'], 'L1_xattn_Wk': _L1_xattn_in['Wk'], 'L1_xattn_Wv': _L1_xattn_in['Wv'], 'L1_xattn_Wo': _L1_xattn_in['Wo'], 'L1_ffn_gate_w': _L1_ffn_in['gate_w'], 'L1_ffn_W1': _L1_ffn_in['W1'], 'L1_ffn_W2': _L1_ffn_in['W2'], 'L1_ffn_W3': _L1_ffn_in['W3'], 'L1_ffn_Ws1': _L1_ffn_in['Ws1'], 'L1_ffn_Ws2': _L1_ffn_in['Ws2'], 'L1_ffn_Ws3': _L1_ffn_in['Ws3']}

def reference(x, ctx_1024, fside_BxSx2_0, mask_BxS2_bf1, L0_attn_wq, L0_attn_bq, L0_attn_wk, L0_attn_bk, L0_attn_wv, L0_attn_bv, L0_attn_wo, L0_attn_bo, L0_xattn_Wq, L0_xattn_Wkv, L0_xattn_Wout, L0_xattn_bout, L0_ffn_w_router, L0_ffn_w_gate, L0_ffn_w_up, L0_ffn_w_down, L0_ffn_amplitudes, L0_ffn_expert_scale, L0_ffn_shared_w_gate, L0_ffn_shared_w_up, L0_ffn_shared_w_down, L1_attn_w_qkv, L1_attn_w_o, L1_xattn_Wq, L1_xattn_Wk, L1_xattn_Wv, L1_xattn_Wo, L1_ffn_gate_w, L1_ffn_W1, L1_ffn_W2, L1_ffn_W3, L1_ffn_Ws1, L1_ffn_Ws2, L1_ffn_Ws3):
    import jax
    import jax.numpy as jnp

    def _L0_attn_ref(hidden_states, wq, bq, wk, bk, wv, bv, wo, bo):
        import jax, jax.numpy as jnp
        import numpy as np
        HIDDEN = 256
        NUM_HEADS = 16
        HEAD_DIM = HIDDEN // NUM_HEADS
        WORLD_SIZE = 4
        BATCH = 1
        SEQ_SHARD = 256

        def _ring_attention(q, k, v):
            B, H, S, D = q.shape
            scale = 1.0 / np.sqrt(D)
            output_acc = jnp.zeros_like(q)
            max_score = jnp.full((B, H, S, 1), -jnp.inf, dtype=q.dtype)
            sum_exp = jnp.zeros((B, H, S, 1), dtype=q.dtype)
            for _ in range(WORLD_SIZE):
                scores = jnp.einsum('bhsd,bhtd->bhst', q, k) * scale
                new_max = jnp.max(scores, axis=-1, keepdims=True)
                combined_max = jnp.maximum(max_score, new_max)
                old_scale = jnp.exp(max_score - combined_max)
                new_scale = jnp.exp(new_max - combined_max)
                new_exp = jnp.exp(scores - new_max)
                sum_exp = sum_exp * old_scale + jnp.sum(new_exp, axis=-1, keepdims=True) * new_scale
                output_acc = output_acc * old_scale + jnp.einsum('bhst,bhtd->bhsd', new_exp, v) * new_scale
                max_score = combined_max
            return output_acc / sum_exp
        B, S, _ = hidden_states.shape
        q = hidden_states @ wq.T + bq
        k = hidden_states @ wk.T + bk
        v = hidden_states @ wv.T + bv
        split = lambda t: t.reshape(B, S, NUM_HEADS, HEAD_DIM).transpose(0, 2, 1, 3)
        attn = _ring_attention(split(q), split(k), split(v))
        attn = attn.transpose(0, 2, 1, 3).reshape(B, S, HIDDEN)
        return attn @ wo.T + bo

    def _L0_xattn_ref(x, ctx, pos_map, ctx_pos_map, Wq, Wkv, Wout, bout):
        import jax, jax.numpy as jnp
        import numpy as np
        DIM = 256
        CTX_DIM = 128
        N_HEADS = 32
        HEAD_DIM = DIM // N_HEADS
        POS_DIM = 2
        B, N, CTXN = (2, 256, 256)
        ROPE_BASE = 10000.0

        def apply_axial_rope(x, pos):
            b, n, h, d = x.shape
            p = pos.shape[-1]
            dpa = d // p
            half = dpa // 2
            freqs = ROPE_BASE ** (-jnp.arange(half, dtype=x.dtype) / half)
            ang = pos[..., :, None] * freqs
            cos = jnp.cos(ang)[:, :, None, :, :]
            sin = jnp.sin(ang)[:, :, None, :, :]
            xr = x.reshape(b, n, h, p, half, 2)
            x1, x2 = (xr[..., 0], xr[..., 1])
            out = jnp.stack([x1 * cos - x2 * sin, x1 * sin + x2 * cos], axis=-1)
            return out.reshape(b, n, h, d)
        b, n, _ = x.shape
        ctx_n = ctx.shape[1]
        q = (x @ Wq).reshape(b, n, N_HEADS, HEAD_DIM)
        k, v = jnp.split(ctx @ Wkv, 2, axis=-1)
        k = k.reshape(b, ctx_n, N_HEADS, HEAD_DIM)
        v = v.reshape(b, ctx_n, N_HEADS, HEAD_DIM)
        q = apply_axial_rope(q, pos_map)
        k = apply_axial_rope(k, ctx_pos_map)
        scale = 1.0 / np.sqrt(HEAD_DIM).astype(np.float32)
        logits = jnp.einsum('bqhd,bkhd->bhqk', q, k) * scale
        w = jax.nn.softmax(logits, axis=-1)
        attn = jnp.einsum('bhqk,bkhd->bqhd', w, v)
        attn = attn.reshape(b, n, N_HEADS * HEAD_DIM)
        return attn @ Wout + bout

    def _L0_ffn_ref(x, w_router, w_gate, w_up, w_down, amplitudes, expert_scale, shared_w_gate, shared_w_up, shared_w_down):
        import jax, jax.numpy as jnp
        import numpy as np
        H = 256
        I = 128
        K = 8
        E = 128
        TOPK = 4
        EPS = 1e-08
        B, S, _ = x.shape
        T = B * S
        xt = x.reshape(T, H)
        probs = jax.nn.softmax(xt @ w_router, axis=-1)
        topk_p, topk_idx = jax.lax.top_k(probs, TOPK)
        topk_w = topk_p / (jnp.sum(topk_p, axis=-1, keepdims=True) + EPS)
        gate = (xt @ w_gate).reshape(T, K, I)
        up = (xt @ w_up).reshape(T, K, I)
        basis = jax.nn.silu(gate) * up
        p = amplitudes[..., 0] ** 2 + amplitudes[..., 1] ** 2
        mix = p / (jnp.sum(p, axis=-1, keepdims=True) + EPS)
        mix_sel = mix[topk_idx]
        mixed = jnp.einsum('tek,tki->tei', mix_sel, basis)
        down = jnp.einsum('tei,ih->teh', mixed, w_down)
        coeff = topk_w * expert_scale[topk_idx]
        out = jnp.einsum('teh,te->th', down, coeff)
        shared = jax.nn.silu(xt @ shared_w_gate) * (xt @ shared_w_up) @ shared_w_down
        out = out + shared
        return out.reshape(B, S, H)

    def _L1_attn_ref(x, w_qkv, w_o):
        import jax, jax.numpy as jnp
        import numpy as np
        B, S, H_DIM = (2, 256, 256)
        N_HEADS, D_HEAD = (16, 128)
        b, s, _ = x.shape
        qkv = jnp.einsum('bsh,hf->bsf', x, w_qkv)
        qkv = qkv.reshape(b, s, 3, N_HEADS, D_HEAD)
        q, k, v = (qkv[:, :, 0], qkv[:, :, 1], qkv[:, :, 2])
        q = q.transpose(0, 2, 1, 3)
        k = k.transpose(0, 2, 1, 3)
        v = v.transpose(0, 2, 1, 3)
        scores = jnp.einsum('bhqd,bhkd->bhqk', q, k) / jnp.sqrt(jnp.float32(D_HEAD))
        probs = jax.nn.softmax(scores, axis=-1)
        values = jnp.einsum('bhqk,bhkd->bhkd', probs, v)
        values = values.transpose(0, 2, 1, 3).reshape(b, s, N_HEADS * D_HEAD)
        out = jnp.einsum('bsf,fh->bsh', values, w_o)
        return out

    def _L1_xattn_ref(text_hidden, vision_tokens, vision_mask, Wq, Wk, Wv, Wo):
        import jax, jax.numpy as jnp
        import numpy as np
        N_HEADS = 16
        N_KV_HEADS = 8
        HEAD_DIM = 128
        D_TEXT = 256
        D_VISION = 128
        GROUPS = N_HEADS // N_KV_HEADS
        B, T_text, _ = text_hidden.shape
        T_vis = vision_tokens.shape[1]
        scale = jnp.float32(np.sqrt(HEAD_DIM))
        q = (text_hidden @ Wq).reshape(B, T_text, N_HEADS, HEAD_DIM).transpose(0, 2, 1, 3)
        k = (vision_tokens @ Wk).reshape(B, T_vis, N_KV_HEADS, HEAD_DIM).transpose(0, 2, 1, 3)
        v = (vision_tokens @ Wv).reshape(B, T_vis, N_KV_HEADS, HEAD_DIM).transpose(0, 2, 1, 3)
        k = jnp.repeat(k, GROUPS, axis=1)
        v = jnp.repeat(v, GROUPS, axis=1)
        scores = jnp.einsum('bhtd,bhsd->bhts', q, k) / scale
        mask = vision_mask[:, None, None, :]
        scores = jnp.where(mask, scores, -jnp.inf)
        attn = jax.nn.softmax(scores, axis=-1)
        attn = jnp.nan_to_num(attn, nan=0.0)
        out = jnp.einsum('bhts,bhsd->bhtd', attn, v)
        out = out.transpose(0, 2, 1, 3).reshape(B, T_text, N_HEADS * HEAD_DIM)
        return out @ Wo

    def _L1_ffn_ref(x, gate_w, W1, W2, W3, Ws1, Ws2, Ws3):
        import jax, jax.numpy as jnp
        import numpy as np
        N_GROUPS = 4
        TOPK_GROUPS = 2
        TOPK = 4
        ROUTE_SCALE = 1.0

        def _gate(xt, gate_w):
            T = xt.shape[0]
            E = gate_w.shape[0]
            scores = jax.nn.sigmoid(xt @ gate_w.T)
            original_scores = scores
            sg = scores.reshape(T, N_GROUPS, E // N_GROUPS)
            group_scores = sg.max(axis=-1)
            _, gidx = jax.lax.top_k(group_scores, TOPK_GROUPS)
            gmask = jax.nn.one_hot(gidx, N_GROUPS, dtype=scores.dtype).sum(axis=1)
            masked = (sg * gmask[:, :, None]).reshape(T, E)
            _, idx = jax.lax.top_k(masked, TOPK)
            w = jnp.take_along_axis(original_scores, idx, axis=-1)
            w = w / w.sum(axis=-1, keepdims=True) * ROUTE_SCALE
            return (w, idx)
        shape = x.shape
        D = shape[-1]
        xt = x.reshape(-1, D)
        E = W1.shape[0]
        weights, indices = _gate(xt, gate_w)
        combine = jnp.einsum('tk,tke->te', weights, jax.nn.one_hot(indices, E, dtype=weights.dtype))
        h1 = jnp.einsum('td,eid->tei', xt, W1)
        h3 = jnp.einsum('td,eid->tei', xt, W3)
        g = jax.nn.silu(h1) * h3 * combine[:, :, None]
        y = jnp.einsum('tei,edi->td', g, W2)
        z = jax.nn.silu(xt @ Ws1.T) * (xt @ Ws3.T) @ Ws2.T
        return (y + z).reshape(shape)
    x = x + _L0_attn_ref(_layernorm(x, axis=-1), L0_attn_wq, L0_attn_bq, L0_attn_wk, L0_attn_bk, L0_attn_wv, L0_attn_bv, L0_attn_wo, L0_attn_bo)
    x = x + _L0_xattn_ref(_layernorm(x, axis=-1), ctx_1024, fside_BxSx2_0, fside_BxSx2_0, L0_xattn_Wq, L0_xattn_Wkv, L0_xattn_Wout, L0_xattn_bout)
    x = x + _L0_ffn_ref(_layernorm(x, axis=-1), L0_ffn_w_router, L0_ffn_w_gate, L0_ffn_w_up, L0_ffn_w_down, L0_ffn_amplitudes, L0_ffn_expert_scale, L0_ffn_shared_w_gate, L0_ffn_shared_w_up, L0_ffn_shared_w_down)
    x = x + _L1_attn_ref(_layernorm(x, axis=-1), L1_attn_w_qkv, L1_attn_w_o)
    x = x + _L1_xattn_ref(_layernorm(x, axis=-1), ctx_1024, mask_BxS2_bf1, L1_xattn_Wq, L1_xattn_Wk, L1_xattn_Wv, L1_xattn_Wo)
    x = x + _L1_ffn_ref(_layernorm(x, axis=-1), L1_ffn_gate_w, L1_ffn_W1, L1_ffn_W2, L1_ffn_W3, L1_ffn_Ws1, L1_ffn_Ws2, L1_ffn_Ws3)
    return x

_drawn_inputs = setup_inputs


def setup_inputs(seed=0):
    import zlib

    import numpy as np

    out = dict(_drawn_inputs(seed))
    spreads = {'L0_xattn_bout': (0.0, 0.1), 'L0_ffn_expert_scale': (1.0, 0.6)}
    factors = {'L0_attn_bq': 5.247,
     'L0_attn_bk': 8.0,
     'L0_ffn_w_router': 8.0,
     'L0_ffn_w_gate': 8.0,
     'L0_ffn_w_up': 8.0,
     'L0_ffn_w_down': 8.0,
     'L0_ffn_amplitudes': 8.0,
     'L0_ffn_shared_w_gate': 3.911,
     'L0_ffn_shared_w_up': 3.9,
     'L0_ffn_shared_w_down': 3.837,
     'L1_xattn_Wq': 8.0,
     'L1_xattn_Wk': 8.0,
     'L1_ffn_gate_w': 8.0,
     'L1_ffn_W1': 8.0,
     'L1_ffn_W2': 8.0,
     'L1_ffn_W3': 8.0,
     'L1_ffn_Ws1': 3.489,
     'L1_ffn_Ws2': 3.46,
     'L1_ffn_Ws3': 3.455}
    for name, (base, spread) in spreads.items():
        noise = np.random.default_rng([zlib.crc32(name.encode()), seed]).standard_normal(out[name].shape)
        drawn = base * np.exp(spread * noise) if base else spread * noise
        out[name] = jnp.asarray(drawn.astype(out[name].dtype))
    for name, factor in factors.items():
        out[name] = (out[name] * factor).astype(out[name].dtype)
    return out
```

```python
from contextlib import ExitStack

import concourse.bass as bass
from concourse import mybir

F32 = mybir.dt.float32
F32R = mybir.dt.float32r
BF16 = mybir.dt.bfloat16
I32 = mybir.dt.int32
U32 = mybir.dt.uint32
U8 = mybir.dt.uint8
U16 = mybir.dt.uint16
ALU = mybir.AluOpType
ACT = mybir.ActivationFunctionType
AX_X = mybir.AxisListType.X

P = 128
B, S, D = 16, 64, 256
T = B * S
NT = T // P
KC = D // P
HALF = T // 2
PAIRS = HALF // P
EPS_LN = 1e-5
EPS_MIX = 1e-8
HEADS_D, GROUPS_E = 16, 8
STEPS_D, STEPS_E = 2 * HEADS_D, 2 * GROUPS_E
K_MIX, E_MIX, TOPK = 8, 128, 4
E_MOE = 16
CHUNKS_F = 25
STEPS_F = 2 * CHUNKS_F
STAGES = 4
SLOTS = 6
WORDS = 1280
PI = 3.141592653589793
TWO_PI_A = 6.28125
TWO_PI_B = 2 * PI - TWO_PI_A
PI_BELOW = 3.1415925
ROUND = 12582912.0
RSQRT_SEED = float(0x5F3759DF)

BLOCKS_ABC = [
    ("a_qk", 0, 1024), ("a_vo", 1, 1024), ("ctx", None, T), ("b_q", 2, 1024), ("b_kv", 3, 768), ("b_o", 4, 512),
    ("c_router_down", 5, 1024), ("c_shared", 0, 1024), ("c_mix0", 1, 1024), ("c_mix1", 2, 1024),
    ("c_mix2", 3, 1024), ("c_mix3", 4, 1024),
]
BLOCK = {name: n for n, (name, _, _) in enumerate(BLOCKS_ABC)}
NB_ABC = len(BLOCKS_ABC)
PART_D = NB_ABC
PART_E = PART_D + 2 * HEADS_D
PART_F = PART_E + 2 * GROUPS_E


class Heads:

    def __init__(self, name, width):
        self.name, self.width = name, width
        self.variants = 32 // width
        self.pairs = self.variants // 2
        self.batches = 4 // self.pairs
        self.units = B // self.batches
        self.steps = 4 * self.units
        self.order = []
        for n in range(self.steps + 6):
            if 0 <= n - 2 < self.steps:
                self.order.append(("probs", n - 2))
            if n >= 7 and (n - 7) % 4 == 0 and (n - 7) // 4 < self.units:
                self.order.append(("outs", (n - 7) // 4))
        self.turn = {use: k for k, use in enumerate(self.order)}

    def slot(self, c, vh, bl):
        return (c * self.pairs + vh) * self.batches + bl


HA, HB = Heads("a", 16), Heads("b", 8)

USES_A = [(kind, i, half) for half in range(2) for kind, i in
          [("q", 0), ("q", 1), ("k", 0), ("k", 1), ("v", 0), ("v", 1)]]
USES_B = ([(kind, c, half) for half in range(2) for c in range(2) for kind in ("k", "kr")]
          + [("v", i, half) for half in range(2) for i in range(2)]
          + [(kind, c, half) for half in range(2) for c in range(2) for kind in ("q", "qr")])


def steps(eng, count, unroll, lag, body, peel_last=False):
    for s in range(unroll):
        body(s, s)
    turns = count // unroll - int(peel_last)
    with eng.Fori(1, turns) as i:
        for u in range(unroll):
            body(i * unroll + u, u)
    for s in range(turns * unroll, count + lag):
        body(s, s % unroll)


def has(s, lag, count):
    return not isinstance(s, int) or 0 <= s - lag < count


def at_least(eng, semaphore, value):
    if not isinstance(value, int) or value > 0:
        eng.wait_ge(semaphore, value)


def decoder(nc, A, out):
    ctx = ExitStack()
    with ctx:
        def sb(name, shape, dt=F32):
            return ctx.enter_context(nc.sbuf_tensor(name, shape, dt))

        def sem(name):
            return ctx.enter_context(nc.semaphore(name))

        ps = ctx.enter_context(nc.psum_tensor("ps", [P, 8, 512], F32))

        x = sb("x_sb", [P, NT, D])
        normed = sb("normed", [P, NT, D])
        nT_hi, nT_lo = sb("nT_hi", [P, KC, T], F32R), sb("nT_lo", [P, KC, T], F32R)
        ctx_hi, ctx_lo = sb("ctx_hi", [P, T], F32R), sb("ctx_lo", [P, T], F32R)
        ident, ones, iota = sb("ident", [P, P]), sb("ones", [P, P]), sb("iota", [P, P])
        stage = sb("stage", [P, STAGES, WORDS])
        w_hi, w_lo = sb("w_hi", [P, SLOTS, WORDS], F32R), sb("w_lo", [P, SLOTS, WORDS], F32R)
        stats, mean_var = sb("stats", [P, NT, 6]), sb("mean_var", [P, NT, 2])
        var, rstd, newton = sb("var", [P, NT]), sb("rstd", [P, NT]), sb("newton", [P, NT])
        gate_raw = sb("gate_raw", [P, KC * E_MOE])
        gate_hi, gate_lo = sb("gate_hi", [P, KC * E_MOE], F32R), sb("gate_lo", [P, KC * E_MOE], F32R)
        amps, amp_sq = sb("amps", [P, K_MIX, 2]), sb("amp_sq", [P, K_MIX, 2])
        mix, mix_sum, e_scale = sb("mix", [P, K_MIX]), sb("mix_sum", [P, 2]), sb("e_scale", [P, 1])
        mix_rows = sb("mix_rows", [P, K_MIX, P])
        lower = sb("lower", [P, 4, 4])

        areas = ExitStack()

        def ar(name, shape, dt=F32):
            return areas.enter_context(nc.sbuf_tensor(name, shape, dt))

        q_var = ar("q_var", [P, KC, B, HB.variants * S])
        kT, v_tok = ar("kT", [P, KC, T]), ar("v_tok", [P, NT, D])
        probs, probsT = ar("probs", [P, 3, 512]), ar("probsT", [P, 2, 512])
        outs = ar("outs", [P, 2, 4, P])
        sin_t, cos_t, turns_k = ar("sin_t", [P, T]), ar("cos_t", [P, T]), ar("turns_k", [P, 512])
        rot_sum = ar("rot_sum", [P, 2, 512])
        smax, ssum, srec = ar("smax", [P, 2, 8]), ar("ssum", [P, 2, 32]), ar("srec", [P, 2, 32])
        head_mask, bias_col = ar("head_mask", [P, 6]), ar("bias_col", [P, 4])
        bias_rows = ar("bias_rows", [P, 3, D])
        areas.close()
        probs_flat = probs[:, :, :].rearrange("p a n -> p (a n)")
        pos, freqs = probs_flat[0:2, 0:T], probs_flat[0:2, T:T + 2 * P]
        rot = normed[:, :, :].rearrange("p (a b c) n -> p a b (c n)", a=2, b=2)

        c_silu, c_t1, c_t2 = ar("c_silu", [P, 2, 512]), ar("c_t1", [P, 2, 512]), ar("c_t2", [P, 2, 512])
        basis = ar("basis", [P, T])
        basis_hi, basis_lo = ar("basis_hi", [P, T], F32R), ar("basis_lo", [P, T], F32R)
        sh_hi, sh_lo = ar("sh_hi", [P, 2, T], F32R), ar("sh_lo", [P, 2, T], F32R)
        r_exp, r_pick = ar("r_exp", [P, NT, E_MIX]), ar("r_pick", [P, NT, E_MIX])
        coefT = ar("coefT", [P, T])
        top8, top_idx, top_idx_f = ar("top8", [P, NT, 8]), ar("top_idx", [P, NT, 8], U32), ar("top_idx_f", [P, NT, 8])
        z_all, z_top, z_rec = ar("z_all", [P, NT]), ar("z_top", [P, NT]), ar("z_rec", [P, NT])
        areas.close()

        dq, dk, d_p = ar("dq", [P, 2, 512]), ar("dk", [P, 2, 512]), ar("d_p", [P, 2, 256])
        d_max, d_sum, d_rec = ar("d_max", [P, 2, 4]), ar("d_sum", [P, 2, 4]), ar("d_rec", [P, 2, 4])
        d_cs, d_val = ar("d_cs", [P, 2, 512]), ar("d_val", [P, 2, 512])
        d_vhi, d_vlo = ar("d_vhi", [P, 2, 512], F32R), ar("d_vlo", [P, 2, 512], F32R)
        areas.close()

        eq = ar("eq", [P, 2, 8, 2 * S])
        ek, ev = ar("ek", [P, 2, 512]), ar("ev", [P, 2, 512])
        e_p, e_pT = ar("e_p", [P, 2, 512]), ar("e_pT", [P, 512])
        e_max, e_sum, e_rec = ar("e_max", [P, 2, 8]), ar("e_sum", [P, 2, 8]), ar("e_rec", [P, 2, 8])
        ea_hi, ea_lo = ar("ea_hi", [P, 2, 2, 512], F32R), ar("ea_lo", [P, 2, 2, 512], F32R)
        mask_u8, mask_bias, any_key = ar("mask_u8", [P, T], U8), ar("mask_bias", [P, T]), ar("any_key", [P, B])
        areas.close()

        f_silu, f_t1, f_t2 = ar("f_silu", [P, 2, 512]), ar("f_t1", [P, 2, 512]), ar("f_t2", [P, 2, 512])
        g_hi, g_lo = ar("g_hi", [P, 2, 512], F32R), ar("g_lo", [P, 2, 512], F32R)
        g_score, g_mask, g_pick = (ar(n, [P, NT, E_MOE]) for n in ("g_score", "g_mask", "g_pick"))
        g_top, g_rank = ar("g_top", [P, NT, 4]), ar("g_rank", [P, NT, 4])
        g_cmp, g_eq = ar("g_cmp", [P, NT, 4, 4]), ar("g_eq", [P, NT, 4, 4])
        g_top8, g_idx, g_idx_f = ar("g_top8", [P, NT, 8]), ar("g_idx", [P, NT, 8], U32), ar("g_idx_f", [P, NT, 8])
        g_sum, g_rec = ar("g_sum", [P, NT]), ar("g_rec", [P, NT])
        comb, comb_b = ar("comb", [P, NT, 96]), ar("comb_b", [P, NT, E_MOE], BF16)
        combT, select = ar("combT", [96, T], BF16), ar("select", [96, CHUNKS_F, P], BF16)
        areas.close()

        loaded = sem("loaded")
        x_in = sem("x_in")
        late_in = sem("late_in")
        gate_in = sem("gate_in")
        w_in = [sem(f"w_in{i}") for i in range(STAGES)]
        wd_in = [sem(f"wd_in{i}") for i in range(2)]
        w_hi_done, w_lo_done = sem("w_hi_done"), sem("w_lo_done")
        gate_split = sem("gate_split")
        resid = sem("resid")
        ln_chain = sem("ln_chain")
        normed_done = sem("normed_done")
        ln_tr = sem("ln_tr")
        nT_hi_done, nT_done = sem("nT_hi_done"), sem("nT_done")
        y_full = sem("y_full")
        pool_x = sem("pool_x")
        stored = sem("stored")
        consts = sem("consts")

        ang = sem("ang")
        ang_out = sem("ang_out")
        ang_chain = sem("ang_chain")
        sins = sem("sins")
        a_mm, b_mm = sem("a_mm"), sem("b_mm")
        a_q, a_k, a_v = sem("a_q"), sem("a_k"), sem("a_v")
        b_rot, b_v = sem("b_rot"), sem("b_v")
        b_sum, b_var = sem("b_sum"), sem("b_var")
        hs = {h.name: {k: sem(f"heads_{h.name}_{k}") for k in
                       ("score", "max", "sub", "exp", "sum", "rec", "tr", "probsT", "av", "norm", "outT", "out_hi", "out_lo")}
              for h in (HA, HB)}

        c_router, c_top, c_sub, c_exp, c_chain, c_coef, c_coefT, c_coef_out = (
            sem("c_" + n) for n in ("router", "top", "sub", "exp", "chain", "coef", "coefT", "coef_out"))
        c_gate, c_up, c_cb = sem("c_gate"), sem("c_up"), sem("c_cb")
        c_silued, c_m1, c_m2, c_acc, c_hi, c_lo = (sem("c_" + n) for n in ("silued", "m1", "m2", "acc", "hi", "lo"))

        (d_qk, d_qk_out, d_score, d_maxed, d_subbed, d_exped, d_summed, d_recd, d_pd, d_csum, d_cs_out, d_v,
         d_vd, d_vhid, d_vlod, d_o) = (sem("d_" + n) for n in
                                     ("qk", "qk_out", "score", "maxed", "subbed", "exped", "summed", "recd", "pd",
                                      "csum", "cs_out", "v", "vd", "vhid", "vlod", "o"))
        (e_q, e_kv, e_qk_out, e_v_out, e_score, e_masked, e_maxed, e_subbed, e_exped, e_summed, e_recd, e_pd, e_tr,
         e_pT_out, e_av, e_ahi, e_alo, e_o, e_mask) = (sem("e_" + n) for n in
                                               ("q", "kv", "qk_out", "v_out", "score", "masked", "maxed", "subbed",
                                                "exped", "summed", "recd", "pd", "tr", "pT_out", "av", "ahi", "alo",
                                                "o", "mask"))
        (f_gate, f_sig, f_chain, f_comb, f_combT, f_comb_out, f_h1, f_h3, f_cb, f_silued, f_m1, f_m2, f_ghi, f_glo,
         f_down) = (sem("f_" + n) for n in
                    ("gate", "sig", "chain", "comb", "combT", "comb_out", "h1", "h3", "cb", "silued", "m1", "m2",
                     "ghi", "glo", "down"))

        def f32(ap):
            return ap.bitcast(F32)

        def use_done(uses, n):
            kind = uses[n][0]
            if uses is USES_A:
                s = {"q": a_q, "k": a_k, "v": a_v}[kind]
                return s, sum(u[0] == kind for u in uses[:n + 1])
            if kind == "v":
                return b_v, sum(u[0] == "v" for u in uses[:n + 1])
            return b_rot, sum(u[0] != "v" for u in uses[:n + 1])

        def out_view(dst, h, u):
            n = h.batches * S
            return dst[:, :, u * n:(u + 1) * n].rearrange("p v (b q) -> p b v q", q=S)

        def out_src(bank):
            return bank.rearrange("p (b v q) -> p b v q", v=2, q=S)

        def ea_view(dst, buf, par):
            return dst[:, buf, :, :].rearrange("p j (i r q) -> p r i j q", r=2, q=S)[:, par]

        WORDS_D, WORDS_E, WORDS_F = [(0, 768), (768, 1024)], [(0, 768), (768, 1280)], [(0, 512), (512, 768)]

        T_BANK = [4, 4, 4, 0, 0, 0]
        Y_BANK = [0, 0, 4, 4, 4, 4]

        def y_of(block, t):
            return ps[:, Y_BANK[block] + t // 2, (t % 2) * D:(t % 2 + 1) * D]

        block = ctx.enter_context(nc.Block())

        @block.sync
        def _(sp):
            x_tiles = A["x"].rearrange("(t p) d -> p t d", p=P)
            for half in range(2):
                ts = slice(half * PAIRS, (half + 1) * PAIRS)
                sp.dma_start(x[:, ts, :], x_tiles[:, ts, :]).then_inc(x_in, 16)

            def load(n, src, words, freed=None):
                if freed is not None:
                    sp.wait_ge(w_lo_done, freed)
                i = n % STAGES if isinstance(n, int) else None
                sp.dma_start(stage[:, i, 0:words], src).then_inc(w_in[i], 16)

            def load_abc(n):
                name, _, words = BLOCKS_ABC[n]
                load(n, A["w_" + name], words, n - STAGES + 1 if n >= STAGES else None)

            load_abc(0)
            sp.dma_start(ident[:], A["ident"]).then_inc(loaded, 16)
            sp.dma_start(head_mask[:], A["head_mask"]).then_inc(loaded, 16)
            sp.dma_start(bias_col[:], A["bias_col"]).then_inc(loaded, 16)
            sp.dma_start(bias_rows[:], A["bias_rows"].rearrange("(o r) d -> o r d", o=1).to_broadcast([P, 3, D])
                         ).then_inc(loaded, 16)
            sp.dma_start(pos, A["pos"]).then_inc(loaded, 16)
            sp.dma_start(freqs, A["freqs"]).then_inc(loaded, 16)
            load_abc(1)
            sp.dma_start(amps[:], A["amps"]).then_inc(loaded, 16)
            sp.dma_start(e_scale[:], A["e_scale"]).then_inc(loaded, 16)
            sp.dma_start(iota[:], A["iota"]).then_inc(loaded, 16)
            sp.dma_start(lower[:], A["lower"]).then_inc(loaded, 16)
            sp.dma_start(gate_raw[:], A["gate"]).then_inc(gate_in, 16)
            for n in range(2, NB_ABC):
                load_abc(n)

            def load_def(src, q, i, stage_i, words):
                peeled = isinstance(q, int)
                sp.wait_ge(w_lo_done, NB_ABC - STAGES + 1 + q if peeled and q < 2 else PART_D + 2 * q - 2)
                sp.dma_start(stage[:, stage_i, 0:words], src[bass.ds(i, 1), :, :].rearrange("o p n -> p (o n)")
                             ).then_inc(wd_in[stage_i], 16)

            def load_d(h, u):
                load_def(A["w_d"], h, h, u, 1024)

            steps(sp, HEADS_D, 2, 0, load_d)

            def load_e(g, u):
                load_def(A["w_e"], HEADS_D + g, g, u, WORDS)

            for g in range(2):
                load_e(g, g)
            sp.wait_ge(resid, 4 * NT)
            sp.dma_start(mask_u8[:], A["mask"].to_broadcast([P, T])).then_inc(late_in, 16)
            with sp.Fori(1, GROUPS_E // 2) as i:
                for u in range(2):
                    load_e(i * 2 + u, u)

            def load_f(j, u):
                load_def(A["w_f"], HEADS_D + GROUPS_E + j, j, u, 768)

            for j in range(2):
                load_f(j, j)
            sp.wait_ge(resid, 5 * NT)
            sp.dma_start(select[:].bitcast(U16), A["select"]).then_inc(late_in, 16)
            with sp.Fori(1, CHUNKS_F // 2) as i:
                for u in range(2):
                    load_f(i * 2 + u, u)
            load_f(CHUNKS_F - 1, 0)

            out_tiles = out.rearrange("(t p) d -> p t d", p=P)
            for t in range(0, NT, 2):
                sp.wait_ge(resid, 5 * NT + t + 2)
                sp.dma_start(out_tiles[:, t:t + 2, :], x[:, t:t + 2, :]).then_inc(stored, 16)
            sp.wait_ge(stored, 16 * NT // 2)

        N_LOADED = 16 * 10

        @block.tensor
        def _(pe):
            def mm(o, lhsT, rhs, start, stop):
                return pe.matmul(o, lhsT, rhs, start=start, stop=stop, skip_group_check=True)

            def mm3(o, l_hi, l_lo, r_hi, r_lo, start, stop):
                mm(o, l_hi, r_hi, start, False)
                mm(o, l_hi, r_lo, False, False)
                return mm(o, l_lo, r_hi, False, stop)

            def w(slot, lo, hi):
                return w_hi[:, slot, lo:hi], w_lo[:, slot, lo:hi]

            def weights(part):
                pe.wait_ge(w_lo_done, part + 1)

            def feature_major(o, slot, at, width, c, half):
                for k in range(KC):
                    lo = at + k * width + c * P
                    cols = slice(half * HALF, (half + 1) * HALF)
                    last = mm3(o, *w(slot, lo, lo + P), nT_hi[:, k, cols], nT_lo[:, k, cols], k == 0, k == KC - 1)
                return last

            def transposes(blk, tiles):
                for t in tiles:
                    pe.wait_ge(normed_done, blk * NT + t + 1)
                    if t >= 4:
                        pe.wait_ge(nT_done, blk * NT + t - 3)
                    for k in range(KC):
                        last = pe.transpose(ps[:, T_BANK[blk] + t % 4, k * P:(k + 1) * P],
                                            normed[:, t, k * P:(k + 1) * P], ident[:])
                    last.then_inc(ln_tr, 1)

            def narrow_heads(h, blk, wo_slot, wo_at, wo_part):
                z = hs[h.name]
                d2 = 2 * h.width
                for n in range(h.steps + 6):
                    if n < h.steps:
                        u, g = divmod(n, 4)
                        rows = slice(32 * g, 32 * g + 32)
                        if n >= 4:
                            pe.wait_ge(z["sub"], n - 3)
                        for c in range(KC):
                            for vh in range(h.pairs):
                                for bl in range(h.batches):
                                    b = u * h.batches + bl
                                    at = h.slot(c, vh, bl) * S
                                    last = mm(ps[:, g, at:at + S], q_var[rows, c, b, vh * P:(vh + 1) * P],
                                              kT[rows, c, b * S:(b + 1) * S], True, True)
                        last.then_inc(z["score"], 1)
                    m = n - 2
                    if 0 <= m < h.steps:
                        pe.wait_ge(z["exp"], m + 1)
                        turn = h.turn["probs", m]
                        bank_free(h, z, turn)
                        for j in range(4):
                            last = pe.transpose(ps[:, 4 + turn % 2, j * P:(j + 1) * P],
                                                probs[:, m % 3, j * P:(j + 1) * P], ident[:])
                        last.then_inc(z["tr"], 1)
                    m = n - 3
                    if 0 <= m < h.steps:
                        u, g = divmod(m, 4)
                        pe.wait_ge(z["probsT"], m + 1)
                        if g == 0 and u > 0:
                            pe.wait_ge(z["norm"], 4 * u)
                        for c in range(KC):
                            for vh in range(h.pairs):
                                for bl in range(h.batches):
                                    bp, par = divmod(bl, 2)
                                    half_rows = slice(64 * par, 64 * par + 64)
                                    blk_at = (h.slot(c, vh, bl) // 2) * P
                                    tile = u * h.batches // 2 + bp
                                    f0 = c * P + g * 32 + vh * d2
                                    at = (((bp * KC + c) * 4 + g) * h.pairs + vh) * d2
                                    last = mm(ps[:, 6 + par, at:at + d2], probsT[half_rows, m % 2, blk_at:blk_at + P],
                                              v_tok[half_rows, tile, f0:f0 + d2], True, True)
                        last.then_inc(z["av"], 1)
                    if n >= 7 and (n - 7) % 4 == 0 and (n - 7) // 4 < h.units:
                        u = (n - 7) // 4
                        pe.wait_ge(z["norm"], 4 * (u + 1))
                        turn = h.turn["outs", u]
                        bank_free(h, z, turn)
                        for bl in range(h.batches):
                            last = pe.transpose(ps[:, 4 + turn % 2, bl * P:(bl + 1) * P], outs[:, u % 2, bl, :], ident[:])
                        last.then_inc(z["outT"], 1)
                weights(wo_part)
                pe.wait_ge(z["out_lo"], h.units)
                pe.wait_ge(z["sub"], h.steps)
                for t in range(NT):
                    cols = slice(t * P, (t + 1) * P)
                    for v in range(KC):
                        r = w(wo_slot, wo_at + v * D, wo_at + (v + 1) * D)
                        last = mm3(y_of(blk, t), nT_hi[:, v, cols], nT_lo[:, v, cols], *r, v == 0 and t % 2 == 0, v == 1)
                    if t % 2:
                        last.then_inc(y_full, 1)

            def bank_free(h, z, turn):
                if turn >= 2:
                    kind, m = h.order[turn - 2]
                    pe.wait_ge(z["probsT"] if kind == "probs" else z["out_lo"], m + 1)

            pe.wait_ge(loaded, N_LOADED)
            for i in range(4):
                table, half = divmod(i, 2)
                mm(ps[:, i, :], freqs[:, table * P:(table + 1) * P], pos[:, half * HALF:(half + 1) * HALF],
                   True, True).then_inc(ang, 1)

            n = 0
            for half in range(2):
                transposes(0, range(half * 4, half * 4 + 4))
                pe.wait_ge(nT_done, half * 4 + 4)
                for kind, i, _ in USES_A[6 * half:6 * half + 6]:
                    weights(BLOCK["a_vo"] if kind == "v" else BLOCK["a_qk"])
                    if n < 4:
                        pe.wait_ge(ang_out, n + 1)
                    else:
                        pe.wait_ge(*use_done(USES_A, n - 4))
                    bank = n % 4
                    if kind == "v":
                        for j in range(2):
                            t = half * 4 + 2 * i + j
                            for k in range(KC):
                                r = w(1, k * D, (k + 1) * D)
                                last = mm3(ps[:, bank, j * D:(j + 1) * D], nT_hi[:, k, t * P:(t + 1) * P],
                                           nT_lo[:, k, t * P:(t + 1) * P], *r, k == 0 and j == 0, k == 1)
                    else:
                        last = feature_major(ps[:, bank, :], 0, 0 if kind == "q" else 512, D, i, half)
                    last.then_inc(a_mm, 1)
                    n += 1
            for read in (a_q, a_k, a_v):
                pe.wait_ge(read, 4)
            narrow_heads(HA, 0, 1, 512, BLOCK["a_vo"])

            transposes(1, range(NT))
            pe.wait_ge(nT_done, 2 * NT)
            weights(BLOCK["ctx"])
            weights(BLOCK["b_kv"])
            for n, (kind, i, half) in enumerate(USES_B):
                if n >= 4:
                    pe.wait_ge(*use_done(USES_B, n - 4))
                bank, cols = n % 4, slice(half * HALF, (half + 1) * HALF)
                if kind == "v":
                    for j in range(2):
                        t = half * 4 + 2 * i + j
                        last = mm3(ps[:, bank, j * D:(j + 1) * D], ctx_hi[:, t * P:(t + 1) * P],
                                   ctx_lo[:, t * P:(t + 1) * P], *w(3, 512, 768), j == 0, True)
                elif kind in ("k", "kr"):
                    lo = (D if kind == "kr" else 0) + i * P
                    last = mm3(ps[:, bank, :], *w(3, lo, lo + P), ctx_hi[:, cols], ctx_lo[:, cols], True, True)
                else:
                    last = feature_major(ps[:, bank, :], 2, 512 if kind == "qr" else 0, D, i, half)
                last.then_inc(b_mm, 1)
            pe.wait_ge(b_var, 4)
            pe.wait_ge(b_sum, 8)
            pe.wait_ge(b_v, 4)
            narrow_heads(HB, 1, 4, 0, BLOCK["b_o"])

            transposes(2, range(NT))
            weights(BLOCK["c_router_down"])
            for t in range(NT):
                pe.wait_ge(nT_done, 2 * NT + t + 1)
                if t % 4 == 0:
                    pe.wait_ge(nT_done, 3 * NT)
                for k in range(KC):
                    last = mm3(ps[:, 4 + t // 4, (t % 4) * P:(t % 4 + 1) * P], nT_hi[:, k, t * P:(t + 1) * P],
                               nT_lo[:, k, t * P:(t + 1) * P], *w(5, k * P, (k + 1) * P), k == 0 and t % 4 == 0, k == 1)
                if t % 4 == 3:
                    last.then_inc(c_router, 1)
            readers = []

            def c_bank(reader):
                if len(readers) >= 4:
                    pe.wait_ge(*readers[-4])
                readers.append(reader)
                return ps[:, (len(readers) - 1) % 4, :]

            for s in range(20):
                if s < 4:
                    j, half = divmod(s, 2)
                    slot, at = 0, 512 * j
                    weights(BLOCK["c_shared"])
                else:
                    k_mix, half = divmod(s - 4, 2)
                    slot, at = 1 + k_mix // 2, 512 * (k_mix % 2)
                    weights(BLOCK["c_mix0"] + k_mix // 2)
                feature_major(c_bank((c_silued, s + 1)), slot, at, P, 0, half).then_inc(c_gate, 1)
                feature_major(c_bank((c_m1, s + 1)), slot, at + D, P, 0, half).then_inc(c_up, 1)
                if s == 3:
                    for t in range(NT):
                        if t % 4 == 0:
                            pe.wait_ge(c_coef, t // 4 + 1)
                        last = pe.transpose(ps[:, 6 + t // 4, (t % 4) * P:(t % 4 + 1) * P], r_pick[:, t, :], ident[:])
                        if t % 4 == 3:
                            last.then_inc(c_coefT, 1)
                if s >= 4:
                    pe.wait_ge(c_coef_out, half + 1)
                    mm(c_bank((c_m2, s - 3)), mix_rows[:, k_mix, :], coefT[:, half * HALF:(half + 1) * HALF],
                       True, True).then_inc(c_cb, 1)
            pe.wait_ge(c_lo, 6)
            for t in range(NT):
                cols = slice(t * P, (t + 1) * P)
                mm3(y_of(2, t), basis_hi[:, cols], basis_lo[:, cols], *w(5, 768, 1024), t % 2 == 0, False)
                for j in range(2):
                    last = mm3(y_of(2, t), sh_hi[:, j, cols], sh_lo[:, j, cols],
                               *w(5, 256 + j * D, 256 + (j + 1) * D), False, j == 1)
                if t % 2:
                    last.then_inc(y_full, 1)

            transposes(3, range(NT))
            pe.wait_ge(nT_done, 4 * NT)

            def step_d(s, u):
                half, hp = u % 2, u // 2
                base = 0 if u % 2 == 0 else 2
                if has(s, 0, STEPS_D):
                    if half == 0:
                        pe.wait_ge(w_lo_done, PART_D + s + 1)
                    at_least(pe, d_cs_out, 2 * s - 3)
                    feature_major(ps[:, base, :], hp, 0, P, 0, half).then_inc(d_qk, 1)
                    at_least(pe, d_cs_out, 2 * s - 2)
                    feature_major(ps[:, base + 1, :], hp, 256, P, 0, half).then_inc(d_qk, 1)
                if has(s, 1, STEPS_D):
                    pe.wait_ge(d_pd, s)
                    p_half, p_head, p_buf = (u + 1) % 2, ((u - 1) % 4) // 2, (u - 1) % 2
                    at_least(pe, d_vd, s - 1)
                    for par in range(2):
                        rows = slice(64 * par, 64 * par + 64)
                        last = mm(ps[:, (base + 2 + par) % 4, 0:256], ones[rows, :], d_p[rows, p_buf, :], True, True)
                    last.then_inc(d_csum, 1)
                    if has(s, 0, STEPS_D):
                        pe.wait_ge(d_qk_out, 2 * s + 1)
                    feature_major(ps[:, base, :], p_head, 512, P, 0, p_half).then_inc(d_v, 1)
                if has(s, 0, STEPS_D):
                    pe.wait_ge(d_qk_out, 2 * s + 2)
                    buf = u % 2
                    for b in range(8):
                        pair, par = divmod(b, 2)
                        last = mm(ps[64 * par:64 * par + 64, base + 1, pair * S:(pair + 1) * S],
                                  dq[:, buf, b * S:(b + 1) * S], dk[:, buf, b * S:(b + 1) * S], True, True)
                    last.then_inc(d_score, 1)
                if has(s, 2, STEPS_D):
                    o_head = ((u - 2) % 4) // 2
                    pe.wait_ge(d_vlod, s - 1)
                    if half == 0:
                        pe.wait_ge(w_lo_done, PART_D + s)
                    for i in range(PAIRS):
                        t = half * PAIRS + i
                        last = mm3(y_of(3, t), d_vhi[:, u % 2, i * P:(i + 1) * P], d_vlo[:, u % 2, i * P:(i + 1) * P],
                                   *w(o_head, 768, 1024), isinstance(s, int) and s < 4 and t % 2 == 0,
                                   isinstance(s, int) and s >= STEPS_D)
                        if isinstance(s, int) and s >= STEPS_D and i % 2:
                            last.then_inc(y_full, 1)
                    if not (isinstance(s, int) and s >= STEPS_D):
                        last.then_inc(d_o, 1)

            pe.wait_ge(consts, 1)
            steps(pe, STEPS_D, 4, 2, step_d)

            transposes(4, range(NT))
            pe.wait_ge(nT_done, 5 * NT)

            def step_e(s, u):
                half, slot, buf = u % 2, 2 + u // 2, u % 2
                prev = (u - 1) % 2
                if has(s, 0, STEPS_E):
                    if half == 0:
                        pe.wait_ge(w_lo_done, PART_E + s + 1)
                    at_least(pe, e_pT_out, s - 1)
                    feature_major(ps[:, 0, :], slot, 0, P, 0, half).then_inc(e_q, 1)
                    at_least(pe, e_alo, 2 * s - 3)
                    feature_major(ps[:, 1, :], slot, 256, P, 0, half).then_inc(e_q, 1)
                    at_least(pe, e_alo, 2 * s - 2)
                    cols = slice(half * HALF, (half + 1) * HALF)
                    mm3(ps[:, 2, :], *w(slot, 512, 640), ctx_hi[:, cols], ctx_lo[:, cols], True, True).then_inc(e_q, 1)
                    at_least(pe, e_masked, s)
                    for i in range(PAIRS):
                        t = half * PAIRS + i
                        last = mm3(ps[:, 3, i * P:(i + 1) * P], ctx_hi[:, t * P:(t + 1) * P],
                                   ctx_lo[:, t * P:(t + 1) * P], *w(slot, 640, 768), i == 0, True)
                    last.then_inc(e_kv, 1)
                if has(s, 1, STEPS_E):
                    if has(s, 0, STEPS_E):
                        pe.wait_ge(e_qk_out, 3 * s + 1)
                    else:
                        pe.wait_ge(e_pT_out, s - 1)
                    pe.wait_ge(e_pd, s)
                    for i in range(PAIRS):
                        last = pe.transpose(ps[:, 0, i * P:(i + 1) * P], e_p[:, prev, i * P:(i + 1) * P], ident[:])
                    last.then_inc(e_tr, 1)
                if has(s, 2, STEPS_E):
                    o_slot = 2 + ((u - 2) % 4) // 2
                    pe.wait_ge(e_alo, 2 * s - 2)
                    if half == 0:
                        pe.wait_ge(w_lo_done, PART_E + s)
                    final = isinstance(s, int) and s >= STEPS_E
                    for i in range(PAIRS):
                        t = half * PAIRS + i
                        for j in range(2):
                            last = mm3(y_of(4, t), ea_hi[:, buf, j, i * P:(i + 1) * P], ea_lo[:, buf, j, i * P:(i + 1) * P],
                                       *w(o_slot, 768 + j * D, 768 + (j + 1) * D),
                                       isinstance(s, int) and s < 4 and t % 2 == 0 and j == 0, final and j == 1)
                        if final and i % 2:
                            last.then_inc(y_full, 1)
                    if not final:
                        last.then_inc(e_o, 1)
                if has(s, 0, STEPS_E):
                    pe.wait_ge(e_qk_out, 3 * s + 3)
                    pe.wait_ge(e_v_out, s + 1)
                    for b in range(8):
                        last = mm(ps[:, 3, b * S:(b + 1) * S], eq[:, buf, b, :], ek[:, buf, b * S:(b + 1) * S], True, True)
                    last.then_inc(e_score, 1)
                if has(s, 1, STEPS_E):
                    if not has(s, 0, STEPS_E):
                        pe.wait_ge(e_alo, 2 * s - 2)
                    pe.wait_ge(e_pT_out, s)
                    for par in range(2):
                        rows = slice(64 * par, 64 * par + 64)
                        for i in range(PAIRS):
                            last = mm(ps[:, 1 + par, i * P:(i + 1) * P], ev[rows, prev, i * P:(i + 1) * P],
                                      e_pT[rows, i * P:(i + 1) * P], True, True)
                        last.then_inc(e_av, 1)

            steps(pe, STEPS_E, 4, 2, step_e)

            transposes(5, range(NT))
            pe.wait_ge(nT_done, 6 * NT)
            pe.wait_ge(gate_split, 2)
            for t in range(NT):
                for k in range(KC):
                    last = mm3(ps[:, 2, t * E_MOE:(t + 1) * E_MOE], nT_hi[:, k, t * P:(t + 1) * P],
                               nT_lo[:, k, t * P:(t + 1) * P], gate_hi[:, k * E_MOE:(k + 1) * E_MOE],
                               gate_lo[:, k * E_MOE:(k + 1) * E_MOE], k == 0 and t == 0, k == 1)
            last.then_inc(f_gate, 1)

            def step_f(s, u):
                half, slot, buf = u % 2, 4 + u // 2, u % 2
                peeled = isinstance(s, int)
                if has(s, 0, STEPS_F):
                    if half == 0:
                        pe.wait_ge(w_lo_done, PART_F + s + 1)
                    at_least(pe, f_m2, s - 1)
                    feature_major(ps[:, (3 * u) % 4, :], slot, 0, P, 0, half).then_inc(f_h1, 1)
                if has(s, 2, STEPS_F):
                    d_slot = 4 + ((u - 2) % 4) // 2
                    pe.wait_ge(f_glo, s - 1)
                    if half == 0:
                        pe.wait_ge(w_lo_done, PART_F + s)
                    final = peeled and s >= STEPS_F
                    for i in range(PAIRS):
                        t = half * PAIRS + i
                        last = mm3(y_of(5, t), g_hi[:, buf, i * P:(i + 1) * P], g_lo[:, buf, i * P:(i + 1) * P],
                                   *w(d_slot, 512, 768), peeled and s < 4 and t % 2 == 0, final)
                        if final and i % 2:
                            last.then_inc(y_full, 1)
                    if not final:
                        last.then_inc(f_down, 1)
                if has(s, 0, STEPS_F):
                    at_least(pe, f_silued, s)
                    feature_major(ps[:, (3 * u + 1) % 4, :], slot, 256, P, 0, half).then_inc(f_h3, 1)
                    if peeled and s == 0:
                        for t in range(NT):
                            if t % 4 == 0:
                                pe.wait_ge(f_comb, 1)
                            last = pe.transpose(ps[0:96, 4 + t // 4, (t % 4) * P:(t % 4 + 1) * P], comb[:, t, :], ident[:])
                        last.then_inc(f_combT, 1)
                        pe.wait_ge(f_comb_out, 2)
                        pe.wait_ge(late_in, 32)
                    at_least(pe, f_m1, s)
                    chunk = (s // 2) if peeled else None
                    cols = slice(half * HALF, (half + 1) * HALF)
                    sel = select[:, chunk, :] if peeled else sel_view(s, u)
                    mm(ps[:, (3 * u + 2) % 4, :], sel, combT[:, cols], True, True).then_inc(f_cb, 1)

            def sel_view(s, u):
                return select[:, :, :].rearrange("p c m -> p (c m)")[:, bass.ds((s - u) * (P // 2) + (u // 2) * P, P)]

            steps(pe, STEPS_F, 4, 2, step_f)

        @block.scalar
        def _(act):
            def split_hi(part, src_block, slot, lo, hi, dst=None, stage_i=None, value=None):
                act.wait_ge(w_in[stage_i], value)
                d = w_hi[:, slot, lo:hi] if dst is None else dst
                act.activation(d, stage[:, stage_i, lo:hi], ACT.Copy).then_inc(w_hi_done, 1)

            def split_abc(name):
                n = BLOCK[name]
                _, slot, words = BLOCKS_ABC[n]
                if slot is None:
                    split_hi(n, n, 0, 0, T, ctx_hi[:], n % STAGES, 16 * (n // STAGES + 1))
                else:
                    split_hi(n, n, slot, 0, words, None, n % STAGES, 16 * (n // STAGES + 1))

            def round_nT(blk, tiles):
                for t in tiles:
                    act.wait_ge(ln_tr, blk * NT + t + 1)
                    act.activation(nT_hi[:, :, t * P:(t + 1) * P],
                                   ps[:, T_BANK[blk] + t % 4, 0:D].rearrange("p (k n) -> p k n", k=KC),
                                   ACT.Copy).then_inc(nT_hi_done, 1)

            def narrow_heads(h):
                z = hs[h.name]
                scale = float(h.width) ** -0.5
                for n in range(h.steps + 6):
                    if n < h.steps:
                        act.wait_ge(z["sub"], n + 1)
                        act.activation(probs[:, n % 3, :], probs[:, n % 3, :], ACT.Exp, scale=scale).then_inc(z["exp"], 1)
                    m = n - 2
                    if 0 <= m < h.steps:
                        act.wait_ge(z["tr"], m + 1)
                        if m >= 2:
                            act.wait_ge(z["av"], m - 1)
                        act.activation(probsT[:, m % 2, :], ps[:, 4 + h.turn["probs", m] % 2, :],
                                       ACT.Copy).then_inc(z["probsT"], 1)
                    if n >= 7 and (n - 7) % 4 == 0 and (n - 7) // 4 < h.units:
                        u = (n - 7) // 4
                        act.wait_ge(z["outT"], u + 1)
                        src = ps[:, 4 + h.turn["outs", u] % 2, 0:h.batches * P]
                        act.activation(out_view(nT_hi, h, u), out_src(src), ACT.Copy).then_inc(z["out_hi"], 1)

            act.wait_ge(loaded, N_LOADED)
            for i in range(4):
                table, half = divmod(i, 2)
                act.wait_ge(ang, i + 1)
                dst = (sin_t, cos_t)[table][:, half * HALF:(half + 1) * HALF]
                act.activation(dst, ps[:, i, :], ACT.Copy, bias=PI / 2 if table else 0.0).then_inc(ang_out, 1)
            split_abc("a_qk")
            split_abc("a_vo")
            for half in range(2):
                round_nT(0, range(half * 4, half * 4 + 4))
                for c in range(KC):
                    n = 6 * half + 2 + c
                    act.wait_ge(a_mm, n + 1)
                    act.activation(kT[:, c, half * HALF:(half + 1) * HALF], ps[:, n % 4, :], ACT.Identity,
                                   bias=bias_col[:, 2 + c:3 + c]).then_inc(a_k, 1)
            for name in ("ctx", "b_q", "b_kv", "b_o", "c_router_down"):
                split_abc(name)
            act.wait_ge(gate_in, 16)
            act.activation(gate_hi[:], gate_raw[:], ACT.Copy).then_inc(gate_split, 1)
            narrow_heads(HA)
            for i in range(4):
                table, half = divmod(i, 2)
                act.wait_ge(ang_chain, 7 * (i + 1))
                dst = (sin_t, cos_t)[table][:, half * HALF:(half + 1) * HALF]
                act.activation(dst, dst, ACT.Sin).then_inc(sins, 1)
            round_nT(1, range(NT))
            for n, (kind, i, half) in enumerate(USES_B):
                if kind == "v":
                    act.wait_ge(b_mm, n + 1)
                    t = half * 4 + 2 * i
                    act.activation(v_tok[:, t:t + 2, :], ps[:, n % 4, :].rearrange("p (t d) -> p t d", t=2),
                                   ACT.Copy).then_inc(b_v, 1)
            act.wait_ge(y_full, 4)
            split_abc("c_shared")
            split_abc("c_mix0")
            narrow_heads(HB)
            round_nT(2, range(NT))
            act.wait_ge(b_mm, len(USES_B))
            split_abc("c_mix1")
            split_abc("c_mix2")
            act.wait_ge(y_full, 8)
            split_abc("c_mix3")
            for half in range(2):
                act.wait_ge(c_sub, half + 1)
                v = r_exp[:, half * 4:half * 4 + 4, :]
                act.activation(v, v, ACT.Exp).then_inc(c_exp, 1)
            for s in range(20):
                half = s % 2
                act.wait_ge(c_gate, s + 1)
                if s >= 2:
                    act.wait_ge(c_m1, s - 1)
                use = 2 * s if s < 4 else 8 + 3 * (s - 4)
                act.activation(c_silu[:, s % 2, :], ps[:, use % 4, :], ACT.Silu).then_inc(c_silued, 1)
                if 1 <= s <= 4:
                    j, h2 = divmod(s - 1, 2)
                    act.wait_ge(c_m1, s)
                    act.activation(sh_hi[:, j, h2 * HALF:(h2 + 1) * HALF], c_t1[:, (s - 1) % 2, :],
                                   ACT.Copy).then_inc(c_hi, 1)
                if s == 3:
                    for h2 in range(2):
                        act.wait_ge(c_coefT, h2 + 1)
                        act.activation(coefT[:, h2 * HALF:(h2 + 1) * HALF], ps[:, 6 + h2, :], ACT.Copy).then_inc(c_coef_out, 1)
            for half in range(2):
                act.wait_ge(c_acc, 13 + half)
                cols = slice(half * HALF, (half + 1) * HALF)
                act.activation(basis_hi[:, cols], basis[:, cols], ACT.Copy).then_inc(c_hi, 1)

            def split_next(s, u, count, q0, slot0, words, used):
                odd = u % 2
                if not has(s, 2 + odd, count - 4):
                    return
                if odd:
                    act.wait_ge(used, s - 1)
                stage_i = (u // 2 + 1) % 2
                act.wait_ge(wd_in[stage_i], 16 * (q0 // 2 + (u // 2 + 1) // 2 + 1) + 4 * (s - u))
                lo, hi = words[odd]
                slot = slot0 + stage_i
                act.activation(w_hi[:, slot, lo:hi], stage[:, stage_i, lo:hi], ACT.Copy).then_inc(w_hi_done, 1)

            def split_first(q, slot, words):
                act.wait_ge(wd_in[q % 2], 16 * (q // 2 + 1))
                for lo, hi in words:
                    act.activation(w_hi[:, slot, lo:hi], stage[:, q % 2, lo:hi], ACT.Copy).then_inc(w_hi_done, 1)

            act.wait_ge(c_up, 8)
            for q in range(2):
                split_first(q, q, WORDS_D)
            round_nT(3, range(NT))

            def step_d(s, u):
                buf = u % 2
                base = 2 * (u % 2)
                if has(s, 0, STEPS_D):
                    for i, dst in enumerate((dq, dk)):
                        act.wait_ge(d_qk, 2 * s + i + 1)
                        at_least(act, d_score, s - 1)
                        act.activation(dst[:, buf, :], ps[:, base + i, :], ACT.Copy).then_inc(d_qk_out, 1)
                if has(s, 1, STEPS_D):
                    prev = (u - 1) % 2
                    act.wait_ge(d_csum, s)
                    at_least(act, d_vd, s - 2)
                    cs = d_cs[:, prev, :].rearrange("p (i r k) -> p r i k", r=2, k=S)
                    for par in range(2):
                        act.activation(cs[:, par], ps[:, (base + 2 + par) % 4, 0:256].rearrange("p (i k) -> p i k", k=S),
                                       ACT.Copy).then_inc(d_cs_out, 1)
                if has(s, 0, STEPS_D):
                    act.wait_ge(d_subbed, s + 1)
                    act.activation(d_p[:, buf, :], d_p[:, buf, :], ACT.Exp, scale=float(P) ** -0.5).then_inc(d_exped, 1)
                if has(s, 1, STEPS_D):
                    act.wait_ge(d_vd, s)
                    at_least(act, d_o, s - 2)
                    act.activation(d_vhi[:, prev, :], d_val[:, prev, :], ACT.Copy).then_inc(d_vhid, 1)
                split_next(s, u, STEPS_D, 0, 0, WORDS_D, d_o)
                if isinstance(s, int) and s >= STEPS_D - 2 and s < STEPS_D:
                    q = HEADS_D + s - STEPS_D + 2
                    split_first(q, 2 + q % 2, WORDS_E)

            steps(act, STEPS_D, 4, 2, step_d, peel_last=True)

            round_nT(4, range(NT))

            def step_e(s, u):
                buf, prev = u % 2, (u - 1) % 2
                if has(s, 0, STEPS_E):
                    at_least(act, e_score, s - 1)
                    for j in range(2):
                        act.wait_ge(e_q, 3 * s + j + 1)
                        act.activation(eq[:, buf, :, j * S:(j + 1) * S], ps[:, j, :].rearrange("p (b n) -> p b n", b=8),
                                       ACT.Copy).then_inc(e_qk_out, 1)
                    act.wait_ge(e_q, 3 * s + 3)
                    act.activation(ek[:, buf, :], ps[:, 2, :], ACT.Copy).then_inc(e_qk_out, 1)
                if has(s, 1, STEPS_E):
                    act.wait_ge(e_tr, s)
                    at_least(act, e_av, 2 * s - 2)
                    act.activation(e_pT[:], ps[:, 0, :], ACT.Copy).then_inc(e_pT_out, 1)
                if u % 2 == 0:
                    split_next(s, u, STEPS_E, HEADS_D, 2, WORDS_E, e_o)
                if has(s, 0, STEPS_E):
                    act.wait_ge(e_subbed, s + 1)
                    act.activation(e_p[:, buf, :], e_p[:, buf, :], ACT.Exp, scale=float(P) ** -0.5).then_inc(e_exped, 1)
                if has(s, 1, STEPS_E):
                    at_least(act, e_o, s - 2)
                    for par in range(2):
                        act.wait_ge(e_av, 2 * s - 1 + par)
                        act.activation(ea_view(ea_hi, prev, par), ps[:, 1 + par, :].rearrange("p (i j q) -> p i j q", j=2, q=S),
                                       ACT.Copy).then_inc(e_ahi, 1)
                if u % 2:
                    split_next(s, u, STEPS_E, HEADS_D, 2, WORDS_E, e_o)
                if isinstance(s, int) and s >= STEPS_E - 2 and s < STEPS_E:
                    q = HEADS_D + GROUPS_E + s - STEPS_E + 2
                    split_first(q, 4 + q % 2, WORDS_F)

            steps(act, STEPS_E, 4, 2, step_e, peel_last=True)

            round_nT(5, range(NT))
            act.wait_ge(f_gate, 1)
            act.activation(g_score[:].rearrange("p t e -> p (t e)"), ps[:, 2, 0:NT * E_MOE], ACT.Sigmoid).then_inc(f_sig, 1)

            def step_f(s, u):
                buf, prev = u % 2, (u - 1) % 2
                if has(s, 0, STEPS_F):
                    act.wait_ge(f_h1, s + 1)
                    at_least(act, f_m1, s - 1)
                    act.activation(f_silu[:, buf, :], ps[:, (3 * u) % 4, :], ACT.Silu).then_inc(f_silued, 1)
                if has(s, 1, STEPS_F):
                    act.wait_ge(f_m2, s)
                    at_least(act, f_down, s - 2)
                    act.activation(g_hi[:, prev, :], f_t2[:, prev, :], ACT.Copy).then_inc(f_ghi, 1)
                if isinstance(s, int) and s == 0:
                    for half in range(2):
                        act.wait_ge(f_combT, 1)
                        act.activation(combT[:, half * HALF:(half + 1) * HALF], ps[0:96, 4 + half, :],
                                       ACT.Copy).then_inc(f_comb_out, 1)
                split_next(s, u, STEPS_F, HEADS_D + GROUPS_E, 4, WORDS_F, f_down)

            steps(act, STEPS_F, 4, 2, step_f)

        @block.gpsimd
        def _(pool):
            def sub_lo(part, slot, lo, hi, stage_i, dst=None, src_hi=None):
                d = w_lo[:, slot, lo:hi] if dst is None else dst
                h = w_hi[:, slot, lo:hi] if src_hi is None else src_hi
                pool.wait_ge(w_hi_done, part + 1)
                pool.tensor_tensor(d, stage[:, stage_i, lo:hi], f32(h), ALU.subtract).then_inc(w_lo_done, 1)

            def sub_abc(name):
                n = BLOCK[name]
                _, slot, words = BLOCKS_ABC[n]
                if slot is None:
                    sub_lo(n, 0, 0, T, n % STAGES, ctx_lo[:], ctx_hi[:])
                else:
                    sub_lo(n, slot, 0, words, n % STAGES)

            sub_abc("a_qk")
            sub_abc("a_vo")
            chain = 0

            def small(instruction):
                nonlocal chain
                instruction.then_inc(ang_chain, 1)
                chain += 1
                pool.wait_ge(ang_chain, chain)

            for i in range(4):
                table, half = divmod(i, 2)
                y = (sin_t, cos_t)[table][:, half * HALF:(half + 1) * HALF]
                pool.wait_ge(ang_out, i + 1)
                small(pool.tensor_scalar(turns_k[:], y, 1 / (2 * PI), ROUND, ALU.mult, ALU.add))
                small(pool.tensor_scalar(turns_k[:], turns_k[:], ROUND, None, ALU.subtract))
                for part in (TWO_PI_A, TWO_PI_B):
                    small(pool.tensor_scalar(rot_sum[:, 0, :], turns_k[:], part, None, ALU.mult))
                    small(pool.tensor_tensor(y, y, rot_sum[:, 0, :], ALU.subtract))
                small(pool.tensor_scalar(y, y, PI_BELOW, -PI_BELOW, ALU.min, ALU.max))
            for name in ("ctx", "b_q", "b_kv", "b_o", "c_router_down"):
                sub_abc(name)
            pool.wait_ge(gate_split, 1)
            pool.tensor_tensor(gate_lo[:], gate_raw[:], f32(gate_hi[:]), ALU.subtract).then_inc(gate_split, 1)

            def add_bias(blk, row):
                pool.wait_ge(normed_done, (blk + 1) * NT)
                pool.wait_ge(loaded, N_LOADED)
                bias = bias_rows[:, row:row + 1, :].to_broadcast([P, NT, D])
                pool.tensor_tensor(x[:], x[:], bias, ALU.add).then_inc(pool_x, 1)

            add_bias(0, 1)
            add_bias(1, 2)
            pieces = [("k", c, half) for half in range(2) for c in range(2)] + [("q", c, half) for half in range(2) for c in range(2)]
            for i, (kind, c, half) in enumerate(pieces):
                pool.wait_ge(b_rot, 2 * i + 2)
                if kind == "k":
                    dst = kT[:, c, half * HALF:(half + 1) * HALF]
                else:
                    dst = rot_sum[:, i % 2, :]
                    if i >= 6:
                        pool.wait_ge(b_var, i - 5)
                pool.tensor_tensor(dst, rot[:, i % 2, 0, :], rot[:, i % 2, 1, :], ALU.add).then_inc(b_sum, 1)
            sub_abc("c_shared")
            sub_abc("c_mix0")
            sub_abc("c_mix1")
            sub_abc("c_mix2")
            sub_abc("c_mix3")
            for s in range(20):
                half = s % 2
                cols = slice(half * HALF, (half + 1) * HALF)
                if s < 4:
                    j = s // 2
                    pool.wait_ge(c_hi, s + 1)
                    pool.tensor_tensor(sh_lo[:, j, cols], c_t1[:, s % 2, :], f32(sh_hi[:, j, cols]),
                                       ALU.subtract).then_inc(c_lo, 1)
                elif s >= 6:
                    pool.wait_ge(c_m2, s - 3)
                    if s >= 8:
                        pool.wait_ge(c_acc, s - 7)
                    pool.tensor_tensor(basis[:, cols], basis[:, cols], c_t2[:, s % 2, :], ALU.add).then_inc(c_acc, 1)
            for half in range(2):
                cols = slice(half * HALF, (half + 1) * HALF)
                pool.wait_ge(c_hi, 5 + half)
                pool.tensor_tensor(basis_lo[:, cols], basis[:, cols], f32(basis_hi[:, cols]), ALU.subtract).then_inc(c_lo, 1)

            def sub_next(s, u, count, part0, slot0, words):
                odd = u % 2
                if not has(s, 2 + odd, count - 4):
                    return
                stage_i = (u // 2 + 1) % 2
                sub_lo(part0 + s + 2, slot0 + stage_i, *words[odd], stage_i)

            def sub_first(q, slot, words):
                for i, (lo, hi) in enumerate(words):
                    sub_lo(PART_D + 2 * q + i, slot, lo, hi, q % 2)

            for q in range(2):
                sub_first(q, q, WORDS_D)

            def step_d(s, u):
                prev = (u - 1) % 2
                if has(s, 1, STEPS_D):
                    pool.wait_ge(d_vhid, s)
                    pool.tensor_tensor(d_vlo[:, prev, :], d_val[:, prev, :], f32(d_vhi[:, prev, :]),
                                       ALU.subtract).then_inc(d_vlod, 1)
                sub_next(s, u, STEPS_D, PART_D, 0, WORDS_D)
                if isinstance(s, int) and STEPS_D - 2 <= s < STEPS_D:
                    q = HEADS_D + s - STEPS_D + 2
                    sub_first(q, 2 + q % 2, WORDS_E)

            steps(pool, STEPS_D, 4, 2, step_d, peel_last=True)

            def step_e(s, u):
                sub_next(s, u, STEPS_E, PART_E, 2, WORDS_E)
                if isinstance(s, int) and STEPS_E - 2 <= s < STEPS_E:
                    q = HEADS_D + GROUPS_E + s - STEPS_E + 2
                    sub_first(q, 4 + q % 2, WORDS_F)

            steps(pool, STEPS_E, 4, 0, step_e, peel_last=True)

            def step_f(s, u):
                prev = (u - 1) % 2
                if has(s, 1, STEPS_F):
                    pool.wait_ge(f_ghi, s)
                    pool.tensor_tensor(g_lo[:, prev, :], f_t2[:, prev, :], f32(g_hi[:, prev, :]),
                                       ALU.subtract).then_inc(f_glo, 1)
                sub_next(s, u, STEPS_F, PART_F, 4, WORDS_F)

            steps(pool, STEPS_F, 4, 2, step_f)

        @block.vector
        def _(ve):
            chained = 0

            def small(instruction):
                nonlocal chained
                instruction.then_inc(ln_chain, 1)
                chained += 1
                ve.wait_ge(ln_chain, chained)

            def add_output(blk, tiles):
                for t in tiles:
                    ve.wait_ge(y_full, 4 * blk + t // 2 + 1)
                    if blk < 2:
                        ve.wait_ge(pool_x, blk + 1)
                    ve.tensor_tensor(x[:, t, :], x[:, t, :], y_of(blk, t), ALU.add).then_inc(resid, 1)

            def layernorm(blk, tiles):
                four = slice(tiles[0], tiles[0] + 4)
                for t in tiles:
                    if blk:
                        ve.wait_ge(resid, (blk - 1) * NT + t + 1)
                    last = ve.bn_stats(stats[:, t, :], x[:, t, :])
                small(last)
                for t in tiles:
                    last = ve.bn_aggr(mean_var[:, t, :], stats[:, t, :])
                small(last)
                v, y, a = var[:, four], rstd[:, four], newton[:, four]
                small(ve.tensor_scalar(v, mean_var[:, four, 1], EPS_LN, None, ALU.add))
                small(ve.tensor_scalar(y.bitcast(I32), v.bitcast(I32), 1, None, ALU.logical_shift_right))
                small(ve.tensor_scalar(y.bitcast(I32), y.bitcast(I32), -1.0, RSQRT_SEED, ALU.mult, ALU.add))
                for _ in range(3):
                    small(ve.tensor_tensor(a, y, y, ALU.mult))
                    small(ve.scalar_tensor_tensor(out=a, in0=a, scalar=-0.5, in1=v, op0=ALU.mult, op1=ALU.mult))
                    small(ve.scalar_tensor_tensor(out=y, in0=a, scalar=1.5, in1=y, op0=ALU.add, op1=ALU.mult))
                for t in tiles:
                    ve.tensor_scalar(normed[:, t, :], x[:, t, :], mean_var[:, t, 0:1], rstd[:, t:t + 1],
                                     ALU.subtract, ALU.mult).then_inc(normed_done, 1)

            def lo_nT(blk, tiles):
                for t in tiles:
                    ve.wait_ge(nT_hi_done, blk * NT + t + 1)
                    cols = slice(t * P, (t + 1) * P)
                    ve.tensor_tensor(nT_lo[:, :, cols], ps[:, T_BANK[blk] + t % 4, 0:D].rearrange("p (k n) -> p k n", k=KC),
                                     f32(nT_hi[:, :, cols]), ALU.subtract).then_inc(nT_done, 1)

            def next_block(blk):
                first, second = range(4), range(4, NT)
                if blk:
                    add_output(blk - 1, first)
                layernorm(blk, first)
                if blk:
                    add_output(blk - 1, second)
                layernorm(blk, second)
                lo_nT(blk, first)
                lo_nT(blk, second)

            def bcast(ap, shape):
                return ap.unsqueeze(len(ap.shape)).to_broadcast(shape)

            def narrow_heads(h):
                z = hs[h.name]
                d, G = h.width, 4 * h.pairs * KC
                for n in range(h.steps + 6):
                    if n >= 7 and (n - 7) % 4 == 0 and (n - 7) // 4 < h.units:
                        u = (n - 7) // 4
                        ve.wait_ge(z["av"], 4 * (u + 1))
                        ve.wait_ge(z["rec"], u + 1)
                        if u >= 2:
                            ve.wait_ge(z["outT"], u - 1)
                        nb = h.batches // 2
                        for par in range(2):
                            for v in range(2):
                                rows = slice(64 * v, 64 * v + 64)
                                src = ps[rows, 6 + par, 0:nb * G * 2 * d].rearrange(
                                    "p (b g d) -> p b g d", g=G, d=2 * d)[:, :, :, v * d:(v + 1) * d]
                                dst = outs[rows, u % 2, 0:h.batches, :].rearrange(
                                    "p (b r) (g d) -> p r b g d", r=2, d=d)[:, par]
                                rec = srec[rows, u % 2, :].rearrange("p (b r g) -> p r b g", r=2, g=G)[:, par]
                                ve.tensor_tensor(dst, src, bcast(rec, [64, nb, G, d]), ALU.mult).then_inc(z["norm"], 1)
                    if n < h.steps:
                        u, g = divmod(n, 4)
                        s3 = ps[:, g, :].rearrange("p (s k) -> p s k", k=S)
                        ve.wait_ge(z["score"], n + 1)
                        ve.tensor_reduce(smax[:, n % 2, :], s3, AX_X, ALU.max).then_inc(z["max"], 1)
                        ve.wait_ge(z["max"], n + 1)
                        if n >= 3:
                            ve.wait_ge(z["tr"], n - 2)
                        ve.tensor_tensor(probs[:, n % 3, :].rearrange("p (s k) -> p s k", k=S), s3,
                                         bcast(smax[:, n % 2, :], [P, 8, S]), ALU.subtract).then_inc(z["sub"], 1)
                    if 0 <= n - 1 < h.steps:
                        m = n - 1
                        u, g = divmod(m, 4)
                        ve.wait_ge(z["exp"], m + 1)
                        dst = ssum[:, u % 2, :].rearrange("p (b c g v) -> p g c v b", c=KC, g=4, v=h.pairs)[:, g]
                        ve.tensor_reduce(dst, probs[:, m % 3, :].rearrange("p (c v b k) -> p c v b k", c=KC, v=h.pairs, k=S),
                                         AX_X, ALU.add).then_inc(z["sum"], 1)
                        if g == 3:
                            ve.wait_ge(z["sum"], m + 1)
                            if u >= 2:
                                ve.wait_ge(z["norm"], 4 * (u - 1))
                            ve.reciprocal(srec[:, u % 2, :], ssum[:, u % 2, :]).then_inc(z["rec"], 1)
                    if n >= 8 and (n - 8) % 4 == 0 and (n - 8) // 4 < h.units:
                        u = (n - 8) // 4
                        ve.wait_ge(z["out_hi"], u + 1)
                        src = ps[:, 4 + h.turn["outs", u] % 2, 0:h.batches * P]
                        ve.tensor_tensor(out_view(nT_lo, h, u), out_src(src), f32(out_view(nT_hi, h, u)),
                                         ALU.subtract).then_inc(z["out_lo"], 1)

            small(ve.memset(ones[:], 1.0))
            ve.wait_ge(loaded, N_LOADED)
            small(ve.tensor_tensor(amp_sq[:], amps[:], amps[:], ALU.mult))
            small(ve.tensor_reduce(mix[:], amp_sq[:], AX_X, ALU.add))
            small(ve.tensor_reduce(mix_sum[:, 0:1], mix[:], AX_X, ALU.add))
            small(ve.tensor_scalar(mix_sum[:, 0:1], mix_sum[:, 0:1], EPS_MIX, None, ALU.add))
            small(ve.reciprocal(mix_sum[:, 1:2], mix_sum[:, 0:1]))
            small(ve.tensor_scalar(mix[:], mix[:], mix_sum[:, 1:2], e_scale[:], ALU.mult, ALU.mult))
            ve.tensor_copy(mix_rows[:], bcast(mix[:], [P, K_MIX, P])).then_inc(consts, 1)

            for half in range(2):
                tiles = range(half * 4, half * 4 + 4)
                ve.wait_ge(x_in, 16 * (half + 1))
                layernorm(0, tiles)
                lo_nT(0, tiles)
                for i in range(6):
                    kind, c, _ = USES_A[6 * half + i]
                    n = 6 * half + i
                    if kind == "k":
                        continue
                    ve.wait_ge(a_mm, n + 1)
                    if kind == "q":
                        for v in range(HA.variants):
                            last = ve.tensor_scalar(q_var[:, c, half * 8:half * 8 + 8, v * S:(v + 1) * S],
                                                    ps[:, n % 4, :].rearrange("p (b q) -> p b q", q=S),
                                                    bias_col[:, c:c + 1], head_mask[:, v:v + 1], ALU.add, ALU.mult)
                        last.then_inc(a_q, 1)
                    else:
                        t = half * 4 + 2 * c
                        ve.tensor_tensor(v_tok[:, t:t + 2, :], ps[:, n % 4, :].rearrange("p (t d) -> p t d", t=2),
                                         bias_rows[:, 0:1, :].to_broadcast([P, 2, D]), ALU.add).then_inc(a_v, 1)
            narrow_heads(HA)

            next_block(1)
            ve.wait_ge(sins, 4)
            piece = 0
            for n, (kind, c, half) in enumerate(USES_B):
                if kind == "v":
                    continue
                cols = slice(half * HALF, (half + 1) * HALF)
                turned = kind in ("kr", "qr")
                ve.wait_ge(b_mm, n + 1)
                if piece >= 2:
                    ve.wait_ge(b_sum, piece - 1)
                ve.tensor_tensor(rot[:, piece % 2, int(turned), :], ps[:, n % 4, :], (sin_t if turned else cos_t)[:, cols],
                                 ALU.mult).then_inc(b_rot, 1)
                if turned:
                    if kind == "qr":
                        ve.wait_ge(b_sum, piece + 1)
                        for v in range(HB.variants):
                            last = ve.tensor_scalar(q_var[:, c, half * 8:half * 8 + 8, v * S:(v + 1) * S],
                                                    rot_sum[:, piece % 2, :].rearrange("p (b q) -> p b q", q=S),
                                                    head_mask[:, 2 + v:3 + v], None, ALU.mult)
                        last.then_inc(b_var, 1)
                    piece += 1
            narrow_heads(HB)

            next_block(2)

            def c_step(s):
                half, use = s % 2, 2 * s + 1 if s < 4 else 9 + 3 * (s - 4)
                ve.wait_ge(c_up, s + 1)
                ve.wait_ge(c_silued, s + 1)
                if 2 <= s < 6:
                    ve.wait_ge(c_lo, s - 1)
                ve.tensor_tensor(c_t1[:, s % 2, :], c_silu[:, s % 2, :], ps[:, use % 4, :], ALU.mult).then_inc(c_m1, 1)
                if s >= 4:
                    ve.wait_ge(c_m1, s + 1)
                    ve.wait_ge(c_cb, s - 3)
                    first = s < 6
                    if s >= 8:
                        ve.wait_ge(c_acc, s - 7)
                    dst = basis[:, half * HALF:(half + 1) * HALF] if first else c_t2[:, s % 2, :]
                    ve.tensor_tensor(dst, c_t1[:, s % 2, :], ps[:, (use + 1) % 4, :], ALU.mult).then_inc(c_m2, 1)

            logits = [ps[:, 4 + half, :].rearrange("p (t e) -> p t e", e=E_MIX) for half in range(2)]
            for t in range(NT):
                ve.wait_ge(c_router, t // 4 + 1)
                last = ve.max(top8[:, t, :], logits[t // 4][:, t % 4, :])
            small(last)
            for half in range(2):
                tiles = slice(half * 4, half * 4 + 4)
                ve.tensor_tensor(r_exp[:, tiles, :], logits[half], top8[:, tiles, 0:1].to_broadcast([P, 4, E_MIX]),
                                 ALU.subtract).then_inc(c_sub, 1)
            for t in range(NT):
                last = ve.max_index(top_idx[:, t, :], top8[:, t, :], logits[t // 4][:, t % 4, :])
            small(last)
            small(ve.tensor_copy(top_idx_f[:], top_idx[:]))
            c_step(0)
            c_step(1)
            for j in range(TOPK):
                for t in range(NT):
                    idx = top_idx_f[:, t, j:j + 1]
                    if j == 0:
                        last = ve.tensor_scalar(r_pick[:, t, :], iota[:], idx, None, ALU.is_equal)
                    else:
                        last = ve.scalar_tensor_tensor(out=r_pick[:, t, :], in0=iota[:], scalar=idx, in1=r_pick[:, t, :],
                                                       op0=ALU.is_equal, op1=ALU.add)
                small(last)
            ve.wait_ge(c_exp, 2)
            small(ve.tensor_reduce(z_all[:], r_exp[:], AX_X, ALU.add))
            small(ve.tensor_tensor(r_pick[:], r_pick[:], r_exp[:], ALU.mult))
            small(ve.tensor_reduce(z_top[:], r_pick[:], AX_X, ALU.add))
            small(ve.scalar_tensor_tensor(out=z_top[:], in0=z_all[:], scalar=EPS_MIX, in1=z_top[:], op0=ALU.mult, op1=ALU.add))
            small(ve.reciprocal(z_rec[:], z_top[:]))
            for half in range(2):
                tiles = slice(half * 4, half * 4 + 4)
                ve.tensor_tensor(r_pick[:, tiles, :], r_pick[:, tiles, :], bcast(z_rec[:, tiles], [P, 4, E_MIX]),
                                 ALU.mult).then_inc(c_coef, 1)
            for s in range(2, 20):
                c_step(s)

            next_block(3)

            def step_d(s, u):
                buf, prev, base = u % 2, (u - 1) % 2, 2 * (u % 2)
                if has(s, 1, STEPS_D):
                    ve.wait_ge(d_v, s)
                    ve.wait_ge(d_cs_out, 2 * s)
                    at_least(ve, d_vlod, s - 2)
                    ve.tensor_tensor(d_val[:, prev, :], ps[:, base, :], d_cs[:, prev, :], ALU.mult).then_inc(d_vd, 1)
                if has(s, 0, STEPS_D):
                    s3 = ps[:, base + 1, 0:256].rearrange("p (i k) -> p i k", k=S)
                    p3 = d_p[:, buf, :].rearrange("p (i k) -> p i k", k=S)
                    ve.wait_ge(d_score, s + 1)
                    ve.tensor_reduce(d_max[:, buf, :], s3, AX_X, ALU.max).then_inc(d_maxed, 1)
                    ve.wait_ge(d_maxed, s + 1)
                    at_least(ve, d_csum, s - 1)
                    ve.tensor_tensor(p3, s3, bcast(d_max[:, buf, :], [P, 4, S]), ALU.subtract).then_inc(d_subbed, 1)
                    ve.wait_ge(d_exped, s + 1)
                    ve.tensor_reduce(d_sum[:, buf, :], p3, AX_X, ALU.add).then_inc(d_summed, 1)
                    ve.wait_ge(d_summed, s + 1)
                    ve.reciprocal(d_rec[:, buf, :], d_sum[:, buf, :]).then_inc(d_recd, 1)
                    ve.wait_ge(d_recd, s + 1)
                    ve.tensor_tensor(p3, p3, bcast(d_rec[:, buf, :], [P, 4, S]), ALU.mult).then_inc(d_pd, 1)

            steps(ve, STEPS_D, 4, 1, step_d)

            next_block(4)
            ve.wait_ge(late_in, 16)
            small(ve.tensor_copy(mask_bias[:], mask_u8[:]))
            small(ve.tensor_reduce(any_key[:], mask_bias[:].rearrange("p (b k) -> p b k", k=S), AX_X, ALU.max))
            small(ve.tensor_scalar(mask_bias[:], mask_bias[:], -1.0, 1e30, ALU.add, ALU.mult))

            def step_e(s, u):
                half, buf, prev = u % 2, u % 2, (u - 1) % 2
                p3 = e_p[:, buf, :].rearrange("p (b k) -> p b k", k=S)
                if has(s, 0, STEPS_E):
                    ve.wait_ge(e_kv, s + 1)
                    at_least(ve, e_av, 2 * s - 2)
                    ve.tensor_copy(ev[:, buf, :], ps[:, 3, :]).then_inc(e_v_out, 1)
                    ve.wait_ge(e_score, s + 1)
                    at_least(ve, e_tr, s - 1)
                    ve.tensor_tensor(e_p[:, buf, :], ps[:, 3, :], mask_bias[:, half * HALF:(half + 1) * HALF],
                                     ALU.add).then_inc(e_masked, 1)
                    ve.wait_ge(e_masked, s + 1)
                    ve.tensor_reduce(e_max[:, buf, :], p3, AX_X, ALU.max).then_inc(e_maxed, 1)
                    ve.wait_ge(e_maxed, s + 1)
                    ve.tensor_tensor(p3, p3, bcast(e_max[:, buf, :], [P, 8, S]), ALU.subtract).then_inc(e_subbed, 1)
                if has(s, 1, STEPS_E):
                    for par in range(2):
                        ve.wait_ge(e_ahi, 2 * s - 1 + par)
                        ve.tensor_tensor(ea_view(ea_lo, prev, par), ps[:, 1 + par, :].rearrange("p (i j q) -> p i j q", j=2, q=S),
                                         f32(ea_view(ea_hi, prev, par)), ALU.subtract).then_inc(e_alo, 1)
                if has(s, 0, STEPS_E):
                    ve.wait_ge(e_exped, s + 1)
                    ve.tensor_reduce(e_sum[:, buf, :], p3, AX_X, ALU.add).then_inc(e_summed, 1)
                    ve.wait_ge(e_summed, s + 1)
                    ve.reciprocal(e_rec[:, buf, :], e_sum[:, buf, :]).then_inc(e_recd, 1)
                    ve.wait_ge(e_recd, 2 * s + 1)
                    ve.tensor_tensor(e_rec[:, buf, :], e_rec[:, buf, :], any_key[:, half * 8:half * 8 + 8],
                                     ALU.mult).then_inc(e_recd, 1)
                    ve.wait_ge(e_recd, 2 * s + 2)
                    ve.tensor_tensor(p3, p3, bcast(e_rec[:, buf, :], [P, 8, S]), ALU.mult).then_inc(e_pd, 1)

            steps(ve, STEPS_E, 4, 1, step_e)

            next_block(5)
            small(ve.memset(comb[:], 0.0))
            ve.wait_ge(f_sig, 1)
            g4 = g_score[:].rearrange("p t (g e) -> p t g e", g=4)
            small(ve.tensor_reduce(g_top[:], g4, AX_X, ALU.max))
            top_i = g_top[:].unsqueeze(3).to_broadcast([P, NT, 4, 4])
            top_j = g_top[:].unsqueeze(2).to_broadcast([P, NT, 4, 4])
            small(ve.tensor_tensor(g_cmp[:], top_j, top_i, ALU.is_gt))
            small(ve.tensor_tensor(g_eq[:], top_j, top_i, ALU.is_equal))
            small(ve.tensor_tensor(g_eq[:], g_eq[:], lower[:].unsqueeze(1).to_broadcast([P, NT, 4, 4]), ALU.mult))
            small(ve.tensor_tensor(g_cmp[:], g_cmp[:], g_eq[:], ALU.add))
            small(ve.tensor_reduce(g_rank[:], g_cmp[:], AX_X, ALU.add))
            small(ve.tensor_scalar(g_rank[:], g_rank[:], 1.5, None, ALU.is_lt))
            small(ve.tensor_tensor(g_mask[:].rearrange("p t (g e) -> p t g e", g=4), g4,
                                   g_rank[:].unsqueeze(3).to_broadcast([P, NT, 4, 4]), ALU.mult))
            for t in range(NT):
                last = ve.max(g_top8[:, t, :], g_mask[:, t, :])
            small(last)
            for t in range(NT):
                last = ve.max_index(g_idx[:, t, :], g_top8[:, t, :], g_mask[:, t, :])
            small(last)
            small(ve.tensor_copy(g_idx_f[:], g_idx[:]))
            for j in range(TOPK):
                idx = g_idx_f[:, :, j:j + 1].to_broadcast([P, NT, E_MOE])
                ids = iota[:, 0:E_MOE].unsqueeze(1).to_broadcast([P, NT, E_MOE])
                if j == 0:
                    small(ve.tensor_tensor(g_pick[:], ids, idx, ALU.is_equal))
                else:
                    small(ve.tensor_tensor(g_mask[:], ids, idx, ALU.is_equal))
                    small(ve.tensor_tensor(g_pick[:], g_pick[:], g_mask[:], ALU.add))
            small(ve.tensor_tensor(g_pick[:], g_pick[:], g_score[:], ALU.mult))
            small(ve.tensor_reduce(g_sum[:], g_pick[:], AX_X, ALU.add))
            small(ve.reciprocal(g_rec[:], g_sum[:]))
            small(ve.tensor_tensor(g_pick[:], g_pick[:], bcast(g_rec[:], [P, NT, E_MOE]), ALU.mult))
            small(ve.memset(comb[:, :, E_MOE:E_MOE + 1], 1.0))
            for i in range(3):
                small(ve.tensor_copy(comb_b[:], g_pick[:]))
                last = ve.tensor_copy(comb[:, :, 32 * i:32 * i + E_MOE], comb_b[:])
                if i < 2:
                    small(last)
                    small(ve.tensor_tensor(g_pick[:], g_pick[:], comb[:, :, 32 * i:32 * i + E_MOE], ALU.subtract))
            last.then_inc(f_comb, 1)

            def step_f(s, u):
                buf = u % 2
                if has(s, 0, STEPS_F):
                    ve.wait_ge(f_h3, s + 1)
                    ve.wait_ge(f_silued, s + 1)
                    ve.tensor_tensor(f_t1[:, buf, :], f_silu[:, buf, :], ps[:, (3 * u + 1) % 4, :], ALU.mult).then_inc(f_m1, 1)
                    ve.wait_ge(f_m1, s + 1)
                    ve.wait_ge(f_cb, s + 1)
                    at_least(ve, f_glo, s - 1)
                    ve.tensor_tensor(f_t2[:, buf, :], f_t1[:, buf, :], ps[:, (3 * u + 2) % 4, :], ALU.mult).then_inc(f_m2, 1)

            steps(ve, STEPS_F, 4, 0, step_f)
            add_output(5, range(NT))


_OUT = (T, D)


def _chunks(w):
    k = w.shape[0] // P
    return w.reshape(k, P, w.shape[1]).transpose(1, 0, 2).reshape(P, -1)


def _out_rows(h):
    import numpy as np
    n = np.arange(D).reshape(KC, 4, h.pairs, 2, h.width)
    return n.transpose(3, 0, 1, 2, 4).reshape(-1)


def _layouts(i):
    import numpy as np

    def cat(*a):
        return np.ascontiguousarray(np.concatenate(a, axis=1))

    g = {}
    g["x"] = i["x"].reshape(T, D)
    g["w_a_qk"] = cat(_chunks(i["L0_attn_wq"].T), _chunks(i["L0_attn_wk"].T))
    g["w_a_vo"] = cat(_chunks(i["L0_attn_wv"].T), _chunks(i["L0_attn_wo"].T[_out_rows(HA)]))
    g["w_ctx"] = i["ctx_1024"].reshape(T, P).T
    swap = np.arange(D).reshape(-1, 2)[:, ::-1].reshape(-1)
    wq, wk, wv = i["L0_xattn_Wq"], i["L0_xattn_Wkv"][:, :D], i["L0_xattn_Wkv"][:, D:]
    g["w_b_q"] = cat(_chunks(wq), _chunks(wq[:, swap]))
    g["w_b_kv"] = cat(wk, wk[:, swap], wv)
    g["w_b_o"] = _chunks(i["L0_xattn_Wout"][_out_rows(HB)])
    g["w_c_router_down"] = cat(_chunks(i["L0_ffn_w_router"]), _chunks(i["L0_ffn_shared_w_down"]), i["L0_ffn_w_down"])

    def gate_up(gate, up, js):
        return cat(*[_chunks(w[:, j * P:(j + 1) * P]) for j in js for w in (gate, up)])

    g["w_c_shared"] = gate_up(i["L0_ffn_shared_w_gate"], i["L0_ffn_shared_w_up"], range(2))
    for r in range(4):
        g[f"w_c_mix{r}"] = gate_up(i["L0_ffn_w_gate"], i["L0_ffn_w_up"], (2 * r, 2 * r + 1))
    qkv, wo = i["L1_attn_w_qkv"], i["L1_attn_w_o"]
    F = HEADS_D * P
    g["w_d"] = np.stack([cat(*[_chunks(qkv[:, n * F + h * P:n * F + (h + 1) * P]) for n in range(3)],
                             wo[h * P:(h + 1) * P]) for h in range(HEADS_D)])
    q, k, v, o = (i["L1_xattn_W" + n] for n in "qkvo")
    g["w_e"] = np.stack([cat(*[_chunks(q[:, h * P:(h + 1) * P]) for h in (2 * n, 2 * n + 1)],
                             k[:, n * P:(n + 1) * P], v[:, n * P:(n + 1) * P],
                             o[2 * n * P:(2 * n + 1) * P], o[(2 * n + 1) * P:(2 * n + 2) * P]) for n in range(GROUPS_E)])

    def rows(expert, shared):
        a = np.concatenate([expert, shared])
        return np.concatenate([a, np.zeros((CHUNKS_F * P - len(a), D), np.float32)])

    w1 = rows(i["L1_ffn_W1"].reshape(-1, D), i["L1_ffn_Ws1"])
    w3 = rows(i["L1_ffn_W3"].reshape(-1, D), i["L1_ffn_Ws3"])
    w2 = rows(i["L1_ffn_W2"].transpose(0, 2, 1).reshape(-1, D), i["L1_ffn_Ws2"].T)
    g["w_f"] = np.stack([cat(_chunks(w1[n * P:(n + 1) * P].T), _chunks(w3[n * P:(n + 1) * P].T),
                             w2[n * P:(n + 1) * P]) for n in range(CHUNKS_F)])
    g["gate"] = _chunks(i["L1_ffn_gate_w"].T)
    g["bias_col"] = cat(i["L0_attn_bq"].reshape(KC, P).T, i["L0_attn_bk"].reshape(KC, P).T)
    g["bias_rows"] = np.stack([i["L0_attn_bv"], i["L0_attn_bo"], i["L0_xattn_bout"]])
    g["pos"] = i["fside_BxSx2_0"].reshape(T, 2).T
    g["mask"] = i["mask_BxS2_bf1"].reshape(1, T).view(np.uint8)
    g["amps"] = i["L0_ffn_amplitudes"]
    g["e_scale"] = i["L0_ffn_expert_scale"].reshape(P, 1)

    p = np.arange(P)
    g["ident"] = np.eye(P, dtype=np.float32)
    g["iota"] = np.tile(p.astype(np.float32), (P, 1))
    g["head_mask"] = np.stack([(p // 16) % 2 == v for v in range(2)] + [(p // 8) % 4 == v for v in range(4)],
                              axis=1).astype(np.float32)
    g["lower"] = np.tile((np.arange(4)[None, :] < np.arange(4)[:, None]).astype(np.float32), (P, 1, 1))
    freq = np.array([1.0, np.float32(10000.0) ** np.float32(-0.5)], np.float32)[(p % 4) // 2]
    axis = (p % 8) // 4 == np.arange(2)[:, None]
    sign = np.where(p % 2 == 0, -1.0, 1.0)
    g["freqs"] = np.concatenate([axis * freq * sign, axis * freq], axis=1).astype(np.float32)
    hidden = np.arange(CHUNKS_F * P)
    owner = np.where(hidden < 16 * 176, hidden // 176, 16)
    sel = np.zeros((96, CHUNKS_F * P), np.float32)
    for r in range(96):
        if r % 32 < 16 or r == 16:
            sel[r] = owner == r % 32
    g["select"] = (sel.reshape(96, CHUNKS_F, P) * 0x3F80).astype(np.uint16)
    return g


_INS = ['x', 'ctx_1024', 'fside_BxSx2_0', 'mask_BxS2_bf1', 'L0_attn_wq', 'L0_attn_bq', 'L0_attn_wk', 'L0_attn_bk',
        'L0_attn_wv', 'L0_attn_bv', 'L0_attn_wo', 'L0_attn_bo', 'L0_xattn_Wq', 'L0_xattn_Wkv', 'L0_xattn_Wout',
        'L0_xattn_bout', 'L0_ffn_w_router', 'L0_ffn_w_gate', 'L0_ffn_w_up', 'L0_ffn_w_down', 'L0_ffn_amplitudes',
        'L0_ffn_expert_scale', 'L0_ffn_shared_w_gate', 'L0_ffn_shared_w_up', 'L0_ffn_shared_w_down', 'L1_attn_w_qkv',
        'L1_attn_w_o', 'L1_xattn_Wq', 'L1_xattn_Wk', 'L1_xattn_Wv', 'L1_xattn_Wo', 'L1_ffn_gate_w', 'L1_ffn_W1',
        'L1_ffn_W2', 'L1_ffn_W3', 'L1_ffn_Ws1', 'L1_ffn_Ws2', 'L1_ffn_Ws3']


def kernel(**inputs):
    import numpy as _np
    import concourse.bacc as _bacc
    from concourse import mybir as _mybir
    from concourse.bass_utils import run_bass_kernel_spmd as _run

    nc = _bacc.Bacc("TRN2", target_bir_lowering=False, num_devices=1)
    laid = _layouts({n: _np.asarray(inputs[n]) for n in _INS})
    arrays, aps = {}, {}
    for name, a in laid.items():
        a = _np.ascontiguousarray(a)
        arrays[f"in_{name}"] = a
        aps[name] = nc.dram_tensor(f"in_{name}", a.shape, _mybir.dt.from_np(a.dtype), kind="ExternalInput").ap()
    out = nc.dram_tensor("out", _OUT, _mybir.dt.float32, kind="ExternalOutput").ap()
    decoder(nc, aps, out)
    r = _run(nc, [arrays], core_ids=[0])
    return r.results[0]["out"].reshape(B, S, D)
```

```python
from contextlib import ExitStack

import concourse.bass as bass
from concourse import mybir

F32 = mybir.dt.float32
F32R = mybir.dt.float32r
BF16 = mybir.dt.bfloat16
I32 = mybir.dt.int32
U32 = mybir.dt.uint32
U8 = mybir.dt.uint8
U16 = mybir.dt.uint16
ALU = mybir.AluOpType
ACT = mybir.ActivationFunctionType
AX_X = mybir.AxisListType.X

P = 128
B, S, D = 16, 64, 256
T = B * S
NT = T // P
KC = D // P
HALF = T // 2
PAIRS = HALF // P
EPS_LN = 1e-5
EPS_MIX = 1e-8
HEADS_D, GROUPS_E = 16, 8
STEPS_D, STEPS_E = 2 * HEADS_D, 2 * GROUPS_E
K_MIX, E_MIX, TOPK = 8, 128, 4
E_MOE = 16
CHUNKS_F = 25
STEPS_F = 2 * CHUNKS_F
STAGES = 4
SLOTS = 6
WORDS = 1280
PI = 3.141592653589793
TWO_PI_A = 6.28125
TWO_PI_B = 2 * PI - TWO_PI_A
PI_BELOW = 3.1415925
ROUND = 12582912.0
RSQRT_SEED = float(0x5F3759DF)

BLOCKS_ABC = [
    ("a_qk", 0, 1024), ("a_vo", 1, 1024), ("ctx", None, T), ("b_q", 2, 1024), ("b_kv", 3, 768), ("b_o", 4, 512),
    ("c_router_down", 5, 1024), ("c_shared", 0, 1024), ("c_mix0", 1, 1024), ("c_mix1", 2, 1024),
    ("c_mix2", 3, 1024), ("c_mix3", 4, 1024),
]
BLOCK = {name: n for n, (name, _, _) in enumerate(BLOCKS_ABC)}
NB_ABC = len(BLOCKS_ABC)
PART_D = NB_ABC
PART_E = PART_D + 2 * HEADS_D
PART_F = PART_E + 2 * GROUPS_E


class Heads:

    def __init__(self, name, width):
        self.name, self.width = name, width
        self.variants = 32 // width
        self.pairs = self.variants // 2
        self.chunks = KC // self.pairs
        self.steps = B * self.pairs
        self.batches = B if self.pairs == 1 else B // 2
        self.quad = 4 * self.pairs

    def batch(self, n):
        return n // self.pairs

    def products(self, n):
        return [(c, 0) for c in range(KC)] if self.pairs == 1 else [(n % 2, vh) for vh in range(2)]


HA, HB = Heads("a", 16), Heads("b", 8)
PROJ_BANK = [0, 1, 6, 7]
TR_LAG, AV_LAG = 3, 4
OUT_LAG = AV_LAG + 1

USES_A = [(kind, i, half) for half in range(2) for kind, i in
          [("q", 0), ("q", 1), ("k", 0), ("k", 1), ("v", 0), ("v", 1)]]
USES_B = [(kind, i, half) for half in range(2) for kind, i in
          [(k + r, c) for k in "kq" for c in range(KC) for r in ("", "r")] + [("v", 0), ("v", 1)]]


def steps(eng, count, unroll, lag, body, peel_last=False):
    for s in range(unroll):
        body(s, s)
    turns = count // unroll - int(peel_last)
    with eng.Fori(1, turns) as i:
        for u in range(unroll):
            body(i * unroll + u, u)
    for s in range(turns * unroll, count + lag):
        body(s, s % unroll)


def has(s, lag, count):
    return not isinstance(s, int) or 0 <= s - lag < count


def at_least(eng, semaphore, value):
    if not isinstance(value, int) or value > 0:
        eng.wait_ge(semaphore, value)


def decoder(nc, A, out):
    ctx = ExitStack()
    with ctx:
        def sb(name, shape, dt=F32):
            return ctx.enter_context(nc.sbuf_tensor(name, shape, dt))

        def sem(name):
            return ctx.enter_context(nc.semaphore(name))

        ps = ctx.enter_context(nc.psum_tensor("ps", [P, 8, 512], F32))

        x = sb("x_sb", [P, NT, D])
        normed = sb("normed", [P, NT, D])
        nT_hi, nT_lo = sb("nT_hi", [P, KC, T], F32R), sb("nT_lo", [P, KC, T], F32R)
        ctx_hi, ctx_lo = sb("ctx_hi", [P, T], F32R), sb("ctx_lo", [P, T], F32R)
        ident, iota = sb("ident", [P, P]), sb("iota", [P, P])
        ones, ones_r = sb("ones", [P, P]), sb("ones_r", [P, P], F32R)
        stage = sb("stage", [P, STAGES, WORDS])
        w_hi, w_lo = sb("w_hi", [P, SLOTS, WORDS], F32R), sb("w_lo", [P, SLOTS, WORDS], F32R)
        stats, mean_var = sb("stats", [P, NT, 6]), sb("mean_var", [P, NT, 2])
        var, rstd, newton = sb("var", [P, NT]), sb("rstd", [P, NT]), sb("newton", [P, NT])
        gate_raw = sb("gate_raw", [P, KC * E_MOE])
        gate_hi, gate_lo = sb("gate_hi", [P, KC * E_MOE], F32R), sb("gate_lo", [P, KC * E_MOE], F32R)
        amps, amp_sq = sb("amps", [P, K_MIX, 2]), sb("amp_sq", [P, K_MIX, 2])
        mix, mix_sum, e_scale = sb("mix", [P, K_MIX]), sb("mix_sum", [P, 2]), sb("e_scale", [P, 1])
        lower = sb("lower", [P, 4, 4])

        areas = ExitStack()

        def ar(name, shape, dt=F32):
            return areas.enter_context(nc.sbuf_tensor(name, shape, dt))

        q_var = ar("q_var", [P, 2 * B * P])
        probs, probsT = ar("probs", [P, 4, 512]), ar("probsT", [P, 2, 512])
        smax, ssum, srec = (ar(n, [P, 4, 8]) for n in ("smax", "ssum", "srec"))
        head_mask, bias_col = ar("head_mask", [P, 6]), ar("bias_col", [P, 4])
        bias_rows = ar("bias_rows", [P, 3, D])
        pos, freqs = ar("pos", [P, NT, 2]), ar("freqs", [P, 2, 8])
        angle, turn_count, turn_part = (ar(n, [P, NT, 2, 8]) for n in ("angle", "turn_count", "turn_part"))
        v_diag = ar("v_diag", [P, B * 256])
        k_diag = ar("k_diag", [P, KC * B * 4 * S])
        areas.close()
        rotary = k_diag[:, KC * (B // 2) * 4 * S:]
        sin_t, cos_t = rotary[:, 0:T], rotary[:, T:2 * T]
        rot_sum = rotary[:, 2 * T:2 * T + 1024].rearrange("p (a n) -> p a n", a=2)
        sines = rotary[:, 2 * T:4 * T].rearrange("p (t c n) -> p t c n", t=NT, c=2)
        rot = normed[:, :, :].rearrange("p (a b c) n -> p a b (c n)", a=2, b=2)

        c_silu, c_t1, c_t2 = ar("c_silu", [P, 2, 512]), ar("c_t1", [P, 2, 512]), ar("c_t2", [P, 2, 512])
        basis = ar("basis", [P, T])
        basis_hi, basis_lo = ar("basis_hi", [P, T], F32R), ar("basis_lo", [P, T], F32R)
        sh_hi, sh_lo = ar("sh_hi", [P, 2, T], F32R), ar("sh_lo", [P, 2, T], F32R)
        r_exp, r_pick = ar("r_exp", [P, NT, E_MIX]), ar("r_pick", [P, NT, E_MIX])
        coefT, mix_rows = ar("coefT", [P, T]), ar("mix_rows", [P, K_MIX, P])
        top8, top_idx, top_idx_f = ar("top8", [P, NT, 8]), ar("top_idx", [P, NT, 8], U32), ar("top_idx_f", [P, NT, 8])
        z_all, z_top, z_rec = ar("z_all", [P, NT]), ar("z_top", [P, NT]), ar("z_rec", [P, NT])
        areas.close()

        dq, dk, d_p = ar("dq", [P, 2, 512]), ar("dk", [P, 2, 512]), ar("d_p", [P, 2, 256])
        d_phi, d_plo = ar("d_phi", [P, 2, 256], F32R), ar("d_plo", [P, 2, 256], F32R)
        d_max, d_sum, d_rec = ar("d_max", [P, 2, 4]), ar("d_sum", [P, 2, 4]), ar("d_rec", [P, 2, 4])
        d_cs, d_val = ar("d_cs", [P, 2, 512]), ar("d_val", [P, 2, 512])
        d_vhi, d_vlo = ar("d_vhi", [P, 2, 512], F32R), ar("d_vlo", [P, 2, 512], F32R)
        areas.close()

        eq = ar("eq", [P, 2, 8, 2 * S])
        ek, ev = ar("ek", [P, 2, 512]), ar("ev", [P, 2, 512])
        v_all = ar("v_all", [P, GROUPS_E * T])
        e_p, e_pT = ar("e_p", [P, 2, 512]), ar("e_pT", [P, 512])
        e_max, e_sum, e_rec = ar("e_max", [P, 2, 8]), ar("e_sum", [P, 2, 8]), ar("e_rec", [P, 2, 8])
        ea_hi, ea_lo = ar("ea_hi", [P, 2, 2, 512], F32R), ar("ea_lo", [P, 2, 2, 512], F32R)
        mask_u8, mask_bias, any_key = ar("mask_u8", [P, T], U8), ar("mask_bias", [P, T]), ar("any_key", [P, B])
        areas.close()

        f_silu, f_t1, f_t2 = ar("f_silu", [P, 2, 512]), ar("f_t1", [P, 2, 512]), ar("f_t2", [P, 2, 512])
        g_hi, g_lo = ar("g_hi", [P, 2, 512], F32R), ar("g_lo", [P, 2, 512], F32R)
        g_score, g_mask, g_pick = (ar(n, [P, NT, E_MOE]) for n in ("g_score", "g_mask", "g_pick"))
        g_top, g_rank = ar("g_top", [P, NT, 4]), ar("g_rank", [P, NT, 4])
        g_cmp, g_eq = ar("g_cmp", [P, NT, 4, 4]), ar("g_eq", [P, NT, 4, 4])
        g_top8, g_idx, g_idx_f = ar("g_top8", [P, NT, 8]), ar("g_idx", [P, NT, 8], U32), ar("g_idx_f", [P, NT, 8])
        g_sum, g_rec = ar("g_sum", [P, NT]), ar("g_rec", [P, NT])
        comb, comb_b = ar("comb", [P, NT, 96]), ar("comb_b", [P, NT, E_MOE], BF16)
        combT, select = ar("combT", [96, T], BF16), ar("select", [96, CHUNKS_F, P], BF16)
        areas.close()

        loaded = sem("loaded")
        x_in = sem("x_in")
        late_in = sem("late_in")
        gate_in = sem("gate_in")
        w_in = [sem(f"w_in{i}") for i in range(STAGES)]
        wd_in = [sem(f"wd_in{i}") for i in range(2)]
        w_hi_done, w_lo_done = sem("w_hi_done"), sem("w_lo_done")
        gate_split = sem("gate_split")
        resid = sem("resid")
        ln_chain = sem("ln_chain")
        normed_done = sem("normed_done")
        ln_tr = sem("ln_tr")
        nT_hi_done, nT_done = sem("nT_hi_done"), sem("nT_done")
        y_full = sem("y_full")
        pool_x = sem("pool_x")
        stored = sem("stored")
        consts = sem("consts")

        angles, sined = sem("angles"), sem("sined")
        trig_tr, trig_out = sem("trig_tr"), sem("trig_out")
        zeroed = sem("zeroed")
        a_mm, b_mm = sem("a_mm"), sem("b_mm")
        a_q, a_k, a_v = sem("a_q"), sem("a_k"), sem("a_v")
        b_rot, b_v = sem("b_rot"), sem("b_v")
        b_sum, b_var, b_k = sem("b_sum"), sem("b_var"), sem("b_k")
        hs = {h.name: {k: sem(f"heads_{h.name}_{k}") for k in
                       ("score", "max", "sub", "exp", "sum", "rec", "norm", "tr", "probsT", "av", "out_hi", "out_lo")}
              for h in (HA, HB)}

        c_router, c_top, c_sub, c_exp, c_chain, c_coef, c_coefT, c_coef_out = (
            sem("c_" + n) for n in ("router", "top", "sub", "exp", "chain", "coef", "coefT", "coef_out"))
        c_gate, c_up, c_cb = sem("c_gate"), sem("c_up"), sem("c_cb")
        c_silued, c_m1, c_m2, c_acc, c_hi, c_lo = (sem("c_" + n) for n in ("silued", "m1", "m2", "acc", "hi", "lo"))

        (d_qk, d_qk_out, d_score, d_maxed, d_subbed, d_exped, d_summed, d_recd, d_pd, d_csum, d_cs_out, d_v,
         d_vd, d_vhid, d_vlod, d_o, d_phid, d_plod) = (sem("d_" + n) for n in
                                     ("qk", "qk_out", "score", "maxed", "subbed", "exped", "summed", "recd", "pd",
                                      "csum", "cs_out", "v", "vd", "vhid", "vlod", "o", "phid", "plod"))
        (e_q, e_v_mm, e_v_in, e_v_split, e_v_all, e_qk_out, e_v_out, e_score, e_masked, e_maxed, e_subbed, e_exped, e_summed, e_recd, e_pd, e_tr,
         e_pT_out, e_av, e_ahi, e_alo, e_o, e_mask) = (sem("e_" + n) for n in
                                               ("q", "v_mm", "v_in", "v_split", "v_all", "qk_out", "v_out", "score", "masked", "maxed", "subbed",
                                                "exped", "summed", "recd", "pd", "tr", "pT_out", "av", "ahi", "alo",
                                                "o", "mask"))
        (f_gate, f_sig, f_chain, f_comb, f_combT, f_comb_out, f_h1, f_h3, f_cb, f_silued, f_m1, f_m2, f_ghi, f_glo,
         f_down) = (sem("f_" + n) for n in
                    ("gate", "sig", "chain", "comb", "combT", "comb_out", "h1", "h3", "cb", "silued", "m1", "m2",
                     "ghi", "glo", "down"))

        def f32(ap):
            return ap.bitcast(F32)

        def use_done(uses, n):
            kind = uses[n][0]
            if uses is USES_A:
                s = {"q": a_q, "k": a_k, "v": a_v}[kind]
                return s, sum(u[0] == kind for u in uses[:n + 1])
            if kind == "v":
                return b_v, sum(u[0] == "v" for u in uses[:n + 1])
            return b_rot, sum(u[0] != "v" for u in uses[:n + 1])

        def b_bank(n):
            half_uses = len(USES_B) // 2
            return (6, 7, 0, 1)[n % half_uses % 4]

        def q_view(h):
            return q_var[:].rearrange("p (c b n) -> p c b n", c=KC, b=h.batches)

        def k_view(h):
            return k_diag[:, 0:KC * h.batches * 4 * S].rearrange("p (c b g k) -> p c b g k", c=KC, b=h.batches, g=4)

        def v_view(h):
            return v_diag[:].rearrange("p (b c j v w n) -> p b c j v w n", b=h.batches, c=KC, j=2, v=2, w=h.pairs)

        def v_slots(h, r, row, i):
            rows = v_diag[64 * r:64 * r + 64, i * 4 * 8 * 32 * h.pairs:(i + 1) * 4 * 8 * 32 * h.pairs]
            slots = rows.rearrange("p (t o n w m) -> p t o n w m", t=2, o=2, w=h.pairs, m=32)[:, :, row]
            d = h.width
            return [slots[:, :, :, w, 16 * w + d * r:16 * w + d * r + d] for w in range(h.pairs)]

        def v_source(h, bank, r, row):
            tiles = ps[64 * row:64 * row + 64, bank, :].rearrange("p (t n) -> p t n", t=2)[:, :, r * P:(r + 1) * P]
            per_width = tiles.rearrange("p t (n w m) -> p t n w m", w=h.pairs, m=h.width)
            return [per_width[:, :, :, w, :] for w in range(h.pairs)]

        def ea_view(dst, buf, par):
            return dst[:, buf, :, :].rearrange("p j (i r q) -> p r i j q", r=2, q=S)[:, par]

        WORDS_D, WORDS_E, WORDS_F = [(0, 768), (768, 1024)], [(0, 640), (640, 1152)], [(0, 512), (512, 768)]

        T_BANK = [2, 4, 4, 0, 0, 0]
        Y_BANK = [0, 0, 4, 4, 4, 4]

        def y_of(block, t):
            return ps[:, Y_BANK[block] + t // 2, (t % 2) * D:(t % 2 + 1) * D]

        block = ctx.enter_context(nc.Block())

        @block.sync
        def _(sp):
            x_tiles = A["x"].rearrange("(t p) d -> p t d", p=P)
            for half in range(2):
                ts = slice(half * PAIRS, (half + 1) * PAIRS)
                sp.dma_start(x[:, ts, :], x_tiles[:, ts, :]).then_inc(x_in, 16)

            def load(n, src, words, freed=None):
                if freed is not None:
                    sp.wait_ge(w_lo_done, freed)
                i = n % STAGES if isinstance(n, int) else None
                sp.dma_start(stage[:, i, 0:words], src).then_inc(w_in[i], 16)

            def load_abc(n):
                name, _, words = BLOCKS_ABC[n]
                load(n, A["w_" + name], words, n - STAGES + 1 if n >= STAGES else None)

            load_abc(0)
            sp.dma_start(ident[:], A["ident"]).then_inc(loaded, 16)
            sp.dma_start(head_mask[:], A["head_mask"]).then_inc(loaded, 16)
            sp.dma_start(bias_col[:], A["bias_col"]).then_inc(loaded, 16)
            sp.dma_start(bias_rows[:], A["bias_rows"].rearrange("(o r) d -> o r d", o=1).to_broadcast([P, 3, D])
                         ).then_inc(loaded, 16)
            sp.dma_start(pos[:], A["pos"]).then_inc(loaded, 16)
            sp.dma_start(freqs[:], A["freqs"]).then_inc(loaded, 16)
            load_abc(1)
            sp.dma_start(amps[:], A["amps"]).then_inc(loaded, 16)
            sp.dma_start(e_scale[:], A["e_scale"]).then_inc(loaded, 16)
            sp.dma_start(iota[:], A["iota"]).then_inc(loaded, 16)
            sp.dma_start(lower[:], A["lower"]).then_inc(loaded, 16)
            sp.dma_start(gate_raw[:], A["gate"]).then_inc(gate_in, 16)
            for n in range(2, NB_ABC):
                load_abc(n)

            def load_def(src, q, i, stage_i, words):
                peeled = isinstance(q, int)
                sp.wait_ge(w_lo_done, NB_ABC - STAGES + 1 + q if peeled and q < 2 else PART_D + 2 * q - 2)
                sp.dma_start(stage[:, stage_i, 0:words], src[bass.ds(i, 1), :, :].rearrange("o p n -> p (o n)")
                             ).then_inc(wd_in[stage_i], 16)

            sp.wait_ge(w_lo_done, max(n for n in range(NB_ABC) if n % STAGES == 2) + 1)
            sp.dma_start(stage[:, 2, 0:T], A["w_e_v"]).then_inc(e_v_in, 16)

            def load_d(h, u):
                load_def(A["w_d"], h, h, u, 1024)

            steps(sp, HEADS_D, 2, 0, load_d)

            def load_e(g, u):
                load_def(A["w_e"], HEADS_D + g, g, u, WORDS_E[1][1])

            for g in range(2):
                load_e(g, g)
            sp.wait_ge(resid, 4 * NT)
            sp.dma_start(mask_u8[:], A["mask"].to_broadcast([P, T])).then_inc(late_in, 16)
            with sp.Fori(1, GROUPS_E // 2) as i:
                for u in range(2):
                    load_e(i * 2 + u, u)

            def load_f(j, u):
                load_def(A["w_f"], HEADS_D + GROUPS_E + j, j, u, 768)

            for j in range(2):
                load_f(j, j)
            sp.wait_ge(resid, 5 * NT)
            sp.dma_start(select[:].bitcast(U16), A["select"]).then_inc(late_in, 16)
            with sp.Fori(1, CHUNKS_F // 2) as i:
                for u in range(2):
                    load_f(i * 2 + u, u)
            load_f(CHUNKS_F - 1, 0)

            out_tiles = out.rearrange("(t p) d -> p t d", p=P)
            for t in range(0, NT, 2):
                sp.wait_ge(resid, 5 * NT + t + 2)
                sp.dma_start(out_tiles[:, t:t + 2, :], x[:, t:t + 2, :]).then_inc(stored, 16)
            sp.wait_ge(stored, 16 * NT // 2)

        N_LOADED = 16 * 10

        @block.tensor
        def _(pe):
            def mm(o, lhsT, rhs, start, stop):
                return pe.matmul(o, lhsT, rhs, start=start, stop=stop, skip_group_check=True)

            def mm3(o, l_hi, l_lo, r_hi, r_lo, start, stop):
                mm(o, l_hi, r_hi, start, False)
                mm(o, l_hi, r_lo, False, False)
                return mm(o, l_lo, r_hi, False, stop)

            def w(slot, lo, hi):
                return w_hi[:, slot, lo:hi], w_lo[:, slot, lo:hi]

            def weights(part):
                pe.wait_ge(w_lo_done, part + 1)

            def feature_major(o, slot, at, width, c, half):
                for k in range(KC):
                    lo = at + k * width + c * P
                    cols = slice(half * HALF, (half + 1) * HALF)
                    last = mm3(o, *w(slot, lo, lo + P), nT_hi[:, k, cols], nT_lo[:, k, cols], k == 0, k == KC - 1)
                return last

            def transposes(blk, tiles):
                for t in tiles:
                    pe.wait_ge(normed_done, blk * NT + t + 1)
                    if t >= 4:
                        pe.wait_ge(nT_done, blk * NT + t - 3)
                    for k in range(KC):
                        last = pe.transpose(ps[:, T_BANK[blk] + t % 4, k * P:(k + 1) * P],
                                            normed[:, t, k * P:(k + 1) * P], ident[:])
                    last.then_inc(ln_tr, 1)

            def narrow_heads(h, blk, wo_slot, wo_at, wo_part, second_half=None):
                z, q, k, v = hs[h.name], q_view(h), k_view(h), v_view(h)
                for n in range(h.steps + AV_LAG):
                    if n == h.steps // 2 and second_half:
                        second_half()
                    if n < h.steps:
                        if n >= 2:
                            pe.wait_ge(z["sub"], n - 1)
                        b = h.batch(n) % h.batches
                        for i, (c, w_pair) in enumerate(h.products(n)):
                            last = mm(ps[:, n % 2, i * 256:(i + 1) * 256], q[:, c, b, w_pair * P:(w_pair + 1) * P],
                                      k[:, c, b].rearrange("p g k -> p (g k)"), True, True)
                        last.then_inc(z["score"], 1)
                    m = n - TR_LAG
                    if 0 <= m < h.steps:
                        pe.wait_ge(z["norm"], m + 1)
                        if m >= 2:
                            pe.wait_ge(z["probsT"], m - 1)
                        for i in range(4):
                            last = pe.transpose(ps[:, 2 + m % 2, i * P:(i + 1) * P], probs[:, m % 4, i * P:(i + 1) * P], ident[:])
                        last.then_inc(z["tr"], 1)
                    m = n - AV_LAG
                    if 0 <= m < h.steps:
                        full = m // h.quad
                        pe.wait_ge(z["probsT"], m + 1)
                        if m % h.quad == 0 and full >= 2:
                            pe.wait_ge(z["out_lo"], full - 1)
                        if h is HB:
                            pe.wait_ge(b_v, 2 + 2 * (m // (h.steps // 2)))
                        b = h.batch(m)
                        for j in range(2):
                            for var in range(2):
                                rows = slice(32 * (2 * j + var), 32 * (2 * j + var) + 32)
                                for i, (c, w_pair) in enumerate(h.products(m)):
                                    at = c * 256 + (b % 4) * S
                                    last = mm(ps[rows, 4 + full % 2, at:at + S], v[:, b % h.batches, c, j, var, w_pair, :],
                                              probsT[:, m % 2, (2 * i + j) * P + var * S:(2 * i + j) * P + (var + 1) * S],
                                              w_pair == 0, w_pair == h.pairs - 1)
                        last.then_inc(z["av"], 1)
                weights(wo_part)
                pe.wait_ge(z["out_lo"], B // 4)
                pe.wait_ge(z["sub"], h.steps)
                pe.wait_ge(z["probsT"], h.steps)
                for t in range(NT):
                    cols = slice(t * P, (t + 1) * P)
                    for c in range(KC):
                        r = w(wo_slot, wo_at + c * D, wo_at + (c + 1) * D)
                        last = mm3(y_of(blk, t), nT_hi[:, c, cols], nT_lo[:, c, cols], *r, c == 0 and t % 2 == 0, c == 1)
                    if t % 2:
                        last.then_inc(y_full, 1)

            def values(bank, slot, at, hi, lo, chunks, i, half):
                for j in range(2):
                    tokens = slice((half * 4 + 2 * i + j) * P, (half * 4 + 2 * i + j + 1) * P)
                    for k in range(chunks):
                        last = mm3(ps[:, bank, j * D:(j + 1) * D], hi(k)[:, tokens], lo(k)[:, tokens],
                                   *w(slot, at + k * D, at + (k + 1) * D), k == 0 and j == 0, k == chunks - 1)
                return last

            pe.wait_ge(loaded, N_LOADED)
            n = 0
            for half in range(2):
                transposes(0, range(half * 4, half * 4 + 4))
                pe.wait_ge(nT_done, half * 4 + 4)
                for kind, i, _ in USES_A[6 * half:6 * half + 6]:
                    weights(BLOCK["a_vo"] if kind == "v" else BLOCK["a_qk"])
                    if n >= 4:
                        pe.wait_ge(*use_done(USES_A, n - 4))
                    bank = PROJ_BANK[n % 4]
                    if kind == "v":
                        last = values(bank, 1, 0, lambda k: nT_hi[:, k], lambda k: nT_lo[:, k], KC, i, half)
                    else:
                        last = feature_major(ps[:, bank, :], 0, 0 if kind == "q" else 512, D, i, half)
                    last.then_inc(a_mm, 1)
                    n += 1
            for read in (a_q, a_k, a_v):
                pe.wait_ge(read, 4)
            narrow_heads(HA, 0, 1, 512, BLOCK["a_vo"])

            transposes(1, range(NT))
            pe.wait_ge(nT_done, 2 * NT)
            pe.wait_ge(sined, 1)
            for i in range(4):
                table, half = divmod(i, 2)
                for j in range(PAIRS):
                    last = pe.transpose(ps[:, 2 + i, j * P:(j + 1) * P],
                                        sines[:, half * PAIRS + j, table, :], ident[:])
                last.then_inc(trig_tr, 1)
            weights(BLOCK["ctx"])
            weights(BLOCK["b_kv"])

            def project_b(half):
                first = half * len(USES_B) // 2
                for n in range(first, first + len(USES_B) // 2):
                    kind, i, _ = USES_B[n]
                    in_half = n - first
                    if in_half >= 4 or (half and in_half < 2):
                        pe.wait_ge(*use_done(USES_B, n - (4 if in_half >= 4 else 2)))
                    if half and in_half == 2:
                        pe.wait_ge(hs["b"]["sub"], HB.steps // 2)
                    bank, cols = b_bank(n), slice(half * HALF, (half + 1) * HALF)
                    if kind == "v":
                        last = values(bank, 3, 512, lambda k: ctx_hi, lambda k: ctx_lo, 1, i, half)
                    elif kind in ("k", "kr"):
                        lo = (D if kind == "kr" else 0) + i * P
                        last = mm3(ps[:, bank, :], *w(3, lo, lo + P), ctx_hi[:, cols], ctx_lo[:, cols], True, True)
                    else:
                        last = feature_major(ps[:, bank, :], 2, 512 if kind == "qr" else 0, D, i, half)
                    last.then_inc(b_mm, 1)
                pe.wait_ge(b_k, 2 * half + 2)
                pe.wait_ge(b_var, 2 * half + 2)

            project_b(0)
            pe.wait_ge(trig_out, 4)
            narrow_heads(HB, 1, 4, 0, BLOCK["b_o"], lambda: project_b(1))

            transposes(2, range(NT))
            weights(BLOCK["c_router_down"])
            for t in range(NT):
                pe.wait_ge(nT_done, 2 * NT + t + 1)
                if t % 4 == 0:
                    pe.wait_ge(nT_done, 3 * NT)
                for k in range(KC):
                    last = mm3(ps[:, 4 + t // 4, (t % 4) * P:(t % 4 + 1) * P], nT_hi[:, k, t * P:(t + 1) * P],
                               nT_lo[:, k, t * P:(t + 1) * P], *w(5, k * P, (k + 1) * P), k == 0 and t % 4 == 0, k == 1)
                if t % 4 == 3:
                    last.then_inc(c_router, 1)
            readers = []

            def c_bank(reader):
                if len(readers) >= 4:
                    pe.wait_ge(*readers[-4])
                readers.append(reader)
                return ps[:, (len(readers) - 1) % 4, :]

            for s in range(20):
                if s < 4:
                    j, half = divmod(s, 2)
                    slot, at = 0, 512 * j
                    weights(BLOCK["c_shared"])
                else:
                    k_mix, half = divmod(s - 4, 2)
                    slot, at = 1 + k_mix // 2, 512 * (k_mix % 2)
                    weights(BLOCK["c_mix0"] + k_mix // 2)
                feature_major(c_bank((c_silued, s + 1)), slot, at, P, 0, half).then_inc(c_gate, 1)
                feature_major(c_bank((c_m1, s + 1)), slot, at + D, P, 0, half).then_inc(c_up, 1)
                if s == 3:
                    for t in range(NT):
                        if t % 4 == 0:
                            pe.wait_ge(c_coef, t // 4 + 1)
                        last = pe.transpose(ps[:, 6 + t // 4, (t % 4) * P:(t % 4 + 1) * P], r_pick[:, t, :], ident[:])
                        if t % 4 == 3:
                            last.then_inc(c_coefT, 1)
                if s >= 4:
                    pe.wait_ge(c_coef_out, half + 1)
                    pe.wait_ge(consts, 1)
                    mm(c_bank((c_m2, s - 3)), mix_rows[:, k_mix, :], coefT[:, half * HALF:(half + 1) * HALF],
                       True, True).then_inc(c_cb, 1)
            pe.wait_ge(c_lo, 6)
            for t in range(NT):
                cols = slice(t * P, (t + 1) * P)
                mm3(y_of(2, t), basis_hi[:, cols], basis_lo[:, cols], *w(5, 768, 1024), t % 2 == 0, False)
                for j in range(2):
                    last = mm3(y_of(2, t), sh_hi[:, j, cols], sh_lo[:, j, cols],
                               *w(5, 256 + j * D, 256 + (j + 1) * D), False, j == 1)
                if t % 2:
                    last.then_inc(y_full, 1)

            transposes(3, range(NT))
            pe.wait_ge(nT_done, 4 * NT)

            def step_d(s, u):
                half, hp = u % 2, u // 2
                base = 0 if u % 2 == 0 else 2
                if has(s, 0, STEPS_D):
                    if half == 0:
                        pe.wait_ge(w_lo_done, PART_D + s + 1)
                    at_least(pe, d_cs_out, 2 * s - 3)
                    feature_major(ps[:, base, :], hp, 0, P, 0, half).then_inc(d_qk, 1)
                    at_least(pe, d_cs_out, 2 * s - 2)
                    feature_major(ps[:, base + 1, :], hp, 256, P, 0, half).then_inc(d_qk, 1)
                if has(s, 2, STEPS_D):
                    o_head = ((u - 2) % 4) // 2
                    pe.wait_ge(d_vlod, s - 1)
                    if half == 0:
                        pe.wait_ge(w_lo_done, PART_D + s)
                    for i in range(PAIRS):
                        t = half * PAIRS + i
                        last = mm3(y_of(3, t), d_vhi[:, u % 2, i * P:(i + 1) * P], d_vlo[:, u % 2, i * P:(i + 1) * P],
                                   *w(o_head, 768, 1024), isinstance(s, int) and s < 4 and t % 2 == 0,
                                   isinstance(s, int) and s >= STEPS_D)
                        if isinstance(s, int) and s >= STEPS_D and i % 2:
                            last.then_inc(y_full, 1)
                    if not (isinstance(s, int) and s >= STEPS_D):
                        last.then_inc(d_o, 1)
                if has(s, 1, STEPS_D):
                    pe.wait_ge(d_plod, s)
                    p_half, p_head, p_buf = (u + 1) % 2, ((u - 1) % 4) // 2, (u - 1) % 2
                    at_least(pe, d_vd, s - 1)
                    for par in range(2):
                        rows = slice(64 * par, 64 * par + 64)
                        sums = ps[:, (base + 2 + par) % 4, 0:256]
                        mm(sums, ones_r[rows, :], d_phi[rows, p_buf, :], True, False)
                        last = mm(sums, ones_r[rows, :], d_plo[rows, p_buf, :], False, True)
                    last.then_inc(d_csum, 1)
                if has(s, 0, STEPS_D):
                    pe.wait_ge(d_qk_out, 2 * s + 2)
                    buf = u % 2
                    for i in range(PAIRS):
                        pair = slice(i * P, (i + 1) * P)
                        last = mm(ps[:, base + 1, pair], dq[:, buf, pair], dk[:, buf, pair], True, True)
                    last.then_inc(d_score, 1)
                if has(s, 1, STEPS_D):
                    feature_major(ps[:, base, :], p_head, 512, P, 0, p_half).then_inc(d_v, 1)

            steps(pe, STEPS_D, 4, 2, step_d)

            pe.wait_ge(e_v_split, 2)
            pe.wait_ge(d_vd, STEPS_D)
            for n in range(2 * NT):
                t, i = n // 2, n % 2
                if n >= 4:
                    pe.wait_ge(e_v_all, n - 3)
                tokens = slice(t * P, (t + 1) * P)
                mm3(ps[:, n % 4, :], ctx_hi[:, tokens], ctx_lo[:, tokens], *w(4, i * 512, (i + 1) * 512),
                    True, True).then_inc(e_v_mm, 1)
            pe.wait_ge(e_v_all, 2 * NT)
            transposes(4, range(NT))
            pe.wait_ge(nT_done, 5 * NT)

            def out_e(s, u, part):
                half, buf, o_slot = u % 2, u % 2, 2 + ((u - 2) % 4) // 2
                final = isinstance(s, int) and s >= STEPS_E
                for i in part:
                    t = half * PAIRS + i
                    for j in range(2):
                        last = mm3(y_of(4, t), ea_hi[:, buf, j, i * P:(i + 1) * P], ea_lo[:, buf, j, i * P:(i + 1) * P],
                                   *w(o_slot, 640 + j * D, 640 + (j + 1) * D),
                                   isinstance(s, int) and s < 4 and t % 2 == 0 and j == 0, final and j == 1)
                    if final and i % 2:
                        last.then_inc(y_full, 1)
                if not final and 3 in part:
                    last.then_inc(e_o, 1)

            def step_e(s, u):
                half, slot, buf = u % 2, 2 + u // 2, u % 2
                prev = (u - 1) % 2
                if has(s, 0, STEPS_E):
                    if half == 0:
                        pe.wait_ge(w_lo_done, PART_E + s + 1)
                    at_least(pe, e_pT_out, s - 1)
                    feature_major(ps[:, 0, :], slot, 0, P, 0, half).then_inc(e_q, 1)
                    at_least(pe, e_alo, 2 * s - 3)
                    feature_major(ps[:, 1, :], slot, 256, P, 0, half).then_inc(e_q, 1)
                    at_least(pe, e_alo, 2 * s - 2)
                    cols = slice(half * HALF, (half + 1) * HALF)
                    mm3(ps[:, 2, :], *w(slot, 512, 640), ctx_hi[:, cols], ctx_lo[:, cols], True, True).then_inc(e_q, 1)
                if has(s, 1, STEPS_E):
                    if has(s, 0, STEPS_E):
                        pe.wait_ge(e_qk_out, 3 * s + 1)
                    else:
                        pe.wait_ge(e_pT_out, s - 1)
                    pe.wait_ge(e_pd, s)
                    for i in range(PAIRS):
                        last = pe.transpose(ps[:, 0, i * P:(i + 1) * P], e_p[:, prev, i * P:(i + 1) * P], ident[:])
                    last.then_inc(e_tr, 1)
                if has(s, 2, STEPS_E):
                    pe.wait_ge(e_alo, 2 * s - 2)
                    if half == 0:
                        pe.wait_ge(w_lo_done, PART_E + s)
                    out_e(s, u, (0, 1))
                if has(s, 0, STEPS_E):
                    pe.wait_ge(e_qk_out, 3 * s + 3)
                    at_least(pe, e_masked, s)
                    for b in reversed(range(8)):
                        keys = slice(max(b - 1, 0) * S, (b + 1) * S)
                        last = mm(ps[:, 3, keys], eq[:, buf, b, :], ek[:, buf, keys], True, True)
                    last.then_inc(e_score, 1)
                if has(s, 1, STEPS_E):
                    if not has(s, 0, STEPS_E):
                        pe.wait_ge(e_alo, 2 * s - 2)
                    pe.wait_ge(e_pT_out, s)
                    pe.wait_ge(e_v_out, s)
                    for par in range(2):
                        rows = slice(64 * par, 64 * par + 64)
                        for i in range(PAIRS):
                            last = mm(ps[:, 1 + par, i * P:(i + 1) * P], ev[rows, prev, i * P:(i + 1) * P],
                                      e_pT[rows, i * P:(i + 1) * P], True, True)
                        last.then_inc(e_av, 1)
                if has(s, 2, STEPS_E):
                    out_e(s, u, (2, 3))

            steps(pe, STEPS_E, 4, 2, step_e)

            transposes(5, range(NT))
            pe.wait_ge(nT_done, 6 * NT)
            pe.wait_ge(gate_split, 2)
            for t in range(NT):
                for k in range(KC):
                    last = mm3(ps[:, 2, t * E_MOE:(t + 1) * E_MOE], nT_hi[:, k, t * P:(t + 1) * P],
                               nT_lo[:, k, t * P:(t + 1) * P], gate_hi[:, k * E_MOE:(k + 1) * E_MOE],
                               gate_lo[:, k * E_MOE:(k + 1) * E_MOE], k == 0 and t == 0, k == 1)
            last.then_inc(f_gate, 1)

            def step_f(s, u):
                half, slot, buf = u % 2, 4 + u // 2, u % 2
                peeled = isinstance(s, int)
                if has(s, 0, STEPS_F):
                    if half == 0:
                        pe.wait_ge(w_lo_done, PART_F + s + 1)
                    at_least(pe, f_m2, s - 1)
                    feature_major(ps[:, (3 * u) % 4, :], slot, 0, P, 0, half).then_inc(f_h1, 1)
                if has(s, 2, STEPS_F):
                    d_slot = 4 + ((u - 2) % 4) // 2
                    pe.wait_ge(f_glo, s - 1)
                    if half == 0:
                        pe.wait_ge(w_lo_done, PART_F + s)
                    final = peeled and s >= STEPS_F
                    for i in range(PAIRS):
                        t = half * PAIRS + i
                        last = mm3(y_of(5, t), g_hi[:, buf, i * P:(i + 1) * P], g_lo[:, buf, i * P:(i + 1) * P],
                                   *w(d_slot, 512, 768), peeled and s < 4 and t % 2 == 0, final)
                        if final and i % 2:
                            last.then_inc(y_full, 1)
                    if not final:
                        last.then_inc(f_down, 1)
                if has(s, 0, STEPS_F):
                    at_least(pe, f_silued, s)
                    feature_major(ps[:, (3 * u + 1) % 4, :], slot, 256, P, 0, half).then_inc(f_h3, 1)
                    if peeled and s == 0:
                        for t in range(NT):
                            if t % 4 == 0:
                                pe.wait_ge(f_comb, 1)
                            last = pe.transpose(ps[0:96, 4 + t // 4, (t % 4) * P:(t % 4 + 1) * P], comb[:, t, :], ident[:])
                        last.then_inc(f_combT, 1)
                        pe.wait_ge(f_comb_out, 2)
                        pe.wait_ge(late_in, 32)
                    at_least(pe, f_m1, s)
                    chunk = (s // 2) if peeled else None
                    cols = slice(half * HALF, (half + 1) * HALF)
                    sel = select[:, chunk, :] if peeled else sel_view(s, u)
                    mm(ps[:, (3 * u + 2) % 4, :], sel, combT[:, cols], True, True).then_inc(f_cb, 1)

            def sel_view(s, u):
                return select[:, :, :].rearrange("p c m -> p (c m)")[:, bass.ds((s - u) * (P // 2) + (u // 2) * P, P)]

            steps(pe, STEPS_F, 4, 2, step_f)

        @block.scalar
        def _(act):
            def split_hi(part, src_block, slot, lo, hi, dst=None, stage_i=None, value=None):
                act.wait_ge(w_in[stage_i], value)
                d = w_hi[:, slot, lo:hi] if dst is None else dst
                act.activation(d, stage[:, stage_i, lo:hi], ACT.Copy).then_inc(w_hi_done, 1)

            def split_abc(name):
                n = BLOCK[name]
                _, slot, words = BLOCKS_ABC[n]
                if slot is None:
                    split_hi(n, n, 0, 0, T, ctx_hi[:], n % STAGES, 16 * (n // STAGES + 1))
                else:
                    split_hi(n, n, slot, 0, words, None, n % STAGES, 16 * (n // STAGES + 1))

            def round_nT(blk, tiles):
                for t in tiles:
                    act.wait_ge(ln_tr, blk * NT + t + 1)
                    act.activation(nT_hi[:, :, t * P:(t + 1) * P],
                                   ps[:, T_BANK[blk] + t % 4, 0:D].rearrange("p (k n) -> p k n", k=KC),
                                   ACT.Copy).then_inc(nT_hi_done, 1)

            def narrow_heads(h, second_half=None):
                z = hs[h.name]
                scale = float(h.width) ** -0.5
                for n in range(h.steps + OUT_LAG):
                    if n == h.steps // 2 and second_half:
                        second_half()
                    m = n - TR_LAG
                    if 0 <= m < h.steps:
                        act.wait_ge(z["tr"], m + 1)
                        if m >= 2:
                            act.wait_ge(z["av"], m - 1)
                        act.activation(probsT[:, m % 2, :], ps[:, 2 + m % 2, :], ACT.Copy).then_inc(z["probsT"], 1)
                    if n < h.steps:
                        act.wait_ge(z["sub"], n + 1)
                        act.activation(probs[:, n % 4, :], probs[:, n % 4, :], ACT.Exp, scale=scale).then_inc(z["exp"], 1)
                    if h is HB and n == h.steps // 2 + AV_LAG - 1:
                        act.wait_ge(z["av"], h.steps // 2)
                        values_b(1)
                    m = n - OUT_LAG
                    if m >= 0 and (m + 1) % h.quad == 0:
                        i = m // h.quad
                        act.wait_ge(z["av"], m + 1)
                        act.activation(nT_hi[:, :, i * 256:(i + 1) * 256], ps[:, 4 + i % 2, :].rearrange("p (c n) -> p c n", c=KC),
                                       ACT.Copy).then_inc(z["out_hi"], 1)

            def diagonal(dst, src, **kwargs):
                for g in range(4):
                    rows = slice(32 * g, 32 * g + 32)
                    bias = {k: v[rows] for k, v in kwargs.items()}
                    last = act.activation(dst[rows, :, g, :], src[rows].rearrange("p (b k) -> p b k", k=S),
                                          ACT.Identity if bias else ACT.Copy, **bias)
                return last

            act.wait_ge(loaded, N_LOADED)
            split_abc("a_qk")
            split_abc("a_vo")
            for half in range(2):
                round_nT(0, range(half * 4, half * 4 + 4))
                for c in range(KC):
                    n = 6 * half + 2 + c
                    act.wait_ge(a_mm, n + 1)
                    act.wait_ge(zeroed, 1)
                    diagonal(k_view(HA)[:, c, half * 8:half * 8 + 8], ps[:, PROJ_BANK[n % 4], :],
                             bias=bias_col[:, 2 + c:3 + c]).then_inc(a_k, 1)
            for name in ("ctx", "b_q", "b_kv", "b_o", "c_router_down"):
                split_abc(name)
            act.wait_ge(gate_in, 16)
            act.activation(gate_hi[:], gate_raw[:], ACT.Copy).then_inc(gate_split, 1)
            narrow_heads(HA)
            act.wait_ge(angles, 1)
            act.wait_ge(hs["a"]["score"], HA.steps)
            act.activation(sines.rearrange("p t c (r m) -> p (t c) r m", m=8),
                           angle[:].rearrange("p t c m -> p (t c) m").unsqueeze(2).to_broadcast([P, 2 * NT, P // 8, 8]),
                           ACT.Sin).then_inc(sined, 1)
            round_nT(1, range(NT))
            for i in range(4):
                table, half = divmod(i, 2)
                act.wait_ge(trig_tr, i + 1)
                act.activation((sin_t, cos_t)[table][:, half * HALF:(half + 1) * HALF], ps[:, 2 + i, :],
                               ACT.Copy).then_inc(trig_out, 1)

            def keys_b(half):
                for c in range(KC):
                    act.wait_ge(b_sum, 4 * half + c + 1)
                    if half:
                        act.wait_ge(hs["b"]["score"], HB.steps // 2)
                    diagonal(k_view(HB)[:, c], rot_sum[:, c, :]).then_inc(b_k, 1)

            def values_b(half):
                for i in range(2):
                    n = (half + 1) * len(USES_B) // 2 - 2 + i
                    act.wait_ge(b_mm, n + 1)
                    act.wait_ge(zeroed, 2)
                    for r in range(2):
                        for row in range(2):
                            for dst, src in zip(v_slots(HB, r, row, i), v_source(HB, b_bank(n), r, row)):
                                last = act.activation(dst, src, ACT.Copy)
                    last.then_inc(b_v, 1)

            keys_b(0)
            values_b(0)
            act.wait_ge(y_full, 4)
            split_abc("c_shared")
            split_abc("c_mix0")
            narrow_heads(HB, lambda: keys_b(1))
            round_nT(2, range(NT))
            act.wait_ge(b_mm, len(USES_B))
            split_abc("c_mix1")
            split_abc("c_mix2")
            act.wait_ge(y_full, 8)
            split_abc("c_mix3")
            for half in range(2):
                act.wait_ge(c_sub, half + 1)
                v = r_exp[:, half * 4:half * 4 + 4, :]
                act.activation(v, v, ACT.Exp).then_inc(c_exp, 1)
            for s in range(20):
                half = s % 2
                act.wait_ge(c_gate, s + 1)
                if s >= 2:
                    act.wait_ge(c_m1, s - 1)
                use = 2 * s if s < 4 else 8 + 3 * (s - 4)
                act.activation(c_silu[:, s % 2, :], ps[:, use % 4, :], ACT.Silu).then_inc(c_silued, 1)
                if 1 <= s <= 4:
                    j, h2 = divmod(s - 1, 2)
                    act.wait_ge(c_m1, s)
                    act.activation(sh_hi[:, j, h2 * HALF:(h2 + 1) * HALF], c_t1[:, (s - 1) % 2, :],
                                   ACT.Copy).then_inc(c_hi, 1)
                if s == 3:
                    for h2 in range(2):
                        act.wait_ge(c_coefT, h2 + 1)
                        act.activation(coefT[:, h2 * HALF:(h2 + 1) * HALF], ps[:, 6 + h2, :], ACT.Copy).then_inc(c_coef_out, 1)
            for half in range(2):
                act.wait_ge(c_acc, 13 + half)
                cols = slice(half * HALF, (half + 1) * HALF)
                act.activation(basis_hi[:, cols], basis[:, cols], ACT.Copy).then_inc(c_hi, 1)

            def split_next(s, u, count, q0, slot0, words, used):
                odd = u % 2
                if not has(s, 2 + odd, count - 4):
                    return
                if odd:
                    act.wait_ge(used, s - 1)
                stage_i = (u // 2 + 1) % 2
                act.wait_ge(wd_in[stage_i], 16 * (q0 // 2 + (u // 2 + 1) // 2 + 1) + 4 * (s - u))
                lo, hi = words[odd]
                slot = slot0 + stage_i
                act.activation(w_hi[:, slot, lo:hi], stage[:, stage_i, lo:hi], ACT.Copy).then_inc(w_hi_done, 1)

            def split_first(q, slot, words):
                act.wait_ge(wd_in[q % 2], 16 * (q // 2 + 1))
                for lo, hi in words:
                    act.activation(w_hi[:, slot, lo:hi], stage[:, q % 2, lo:hi], ACT.Copy).then_inc(w_hi_done, 1)

            act.wait_ge(c_up, 8)
            for q in range(2):
                split_first(q, q, WORDS_D)
            round_nT(3, range(NT))
            act.wait_ge(e_v_in, 16)
            act.wait_ge(y_full, 4 * 3)
            act.activation(w_hi[:, 4, 0:T], stage[:, 2, 0:T], ACT.Copy).then_inc(e_v_split, 1)

            def step_d(s, u):
                buf = u % 2
                base = 2 * (u % 2)
                prev = (u - 1) % 2

                def copy_qk(i, dst):
                    act.wait_ge(d_qk, 2 * s + i + 1)
                    at_least(act, d_score, s - 1)
                    act.activation(dst[:, buf, :], ps[:, base + i, :], ACT.Copy).then_inc(d_qk_out, 1)

                if has(s, 0, STEPS_D):
                    copy_qk(0, dq)
                if has(s, 1, STEPS_D):
                    act.wait_ge(d_pd, s)
                    at_least(act, d_csum, s - 2)
                    act.activation(d_phi[:, prev, :], d_p[:, prev, :], ACT.Copy).then_inc(d_phid, 1)
                if has(s, 0, STEPS_D):
                    copy_qk(1, dk)
                if has(s, 1, STEPS_D):
                    act.wait_ge(d_csum, s)
                    at_least(act, d_vd, s - 2)
                    cs = d_cs[:, prev, :].rearrange("p (i r k) -> p r i k", r=2, k=S)
                    for par in range(2):
                        act.activation(cs[:, par], ps[:, (base + 2 + par) % 4, 0:256].rearrange("p (i k) -> p i k", k=S),
                                       ACT.Copy).then_inc(d_cs_out, 1)
                if has(s, 0, STEPS_D):
                    act.wait_ge(d_subbed, s + 1)
                    act.activation(d_p[:, buf, :], d_p[:, buf, :], ACT.Exp, scale=float(P) ** -0.5).then_inc(d_exped, 1)
                if has(s, 1, STEPS_D):
                    act.wait_ge(d_vd, s)
                    at_least(act, d_o, s - 2)
                    act.activation(d_vhi[:, prev, :], d_val[:, prev, :], ACT.Copy).then_inc(d_vhid, 1)
                split_next(s, u, STEPS_D, 0, 0, WORDS_D, d_o)
                if isinstance(s, int) and s >= STEPS_D - 2 and s < STEPS_D:
                    q = HEADS_D + s - STEPS_D + 2
                    split_first(q, 2 + q % 2, WORDS_E)

            steps(act, STEPS_D, 4, 2, step_d, peel_last=True)

            act.wait_ge(y_full, 4 * 4)
            by_group = v_all[:].rearrange("p (g t f) -> p g t f", g=GROUPS_E, t=NT)
            for n in range(2 * NT):
                t, i = n // 2, n % 2
                act.wait_ge(e_v_mm, n + 1)
                act.activation(by_group[:, 4 * i:4 * i + 4, t, :], ps[:, n % 4, :].rearrange("p (g f) -> p g f", g=4),
                               ACT.Copy).then_inc(e_v_all, 1)
            round_nT(4, range(NT))

            def step_e(s, u):
                buf, prev = u % 2, (u - 1) % 2
                if has(s, 0, STEPS_E):
                    at_least(act, e_score, s - 1)
                    for j in range(2):
                        act.wait_ge(e_q, 3 * s + j + 1)
                        act.activation(eq[:, buf, :, j * S:(j + 1) * S], ps[:, j, :].rearrange("p (b n) -> p b n", b=8),
                                       ACT.Copy).then_inc(e_qk_out, 1)
                    act.wait_ge(e_q, 3 * s + 3)
                    act.activation(ek[:, buf, :], ps[:, 2, :], ACT.Copy).then_inc(e_qk_out, 1)
                if has(s, 1, STEPS_E):
                    act.wait_ge(e_tr, s)
                    at_least(act, e_av, 2 * s - 2)
                    act.activation(e_pT[:], ps[:, 0, :], ACT.Copy).then_inc(e_pT_out, 1)
                if u % 2 == 0:
                    split_next(s, u, STEPS_E, HEADS_D, 2, WORDS_E, e_o)
                if has(s, 1, STEPS_E):
                    at_least(act, e_o, s - 2)
                    for par in range(2):
                        act.wait_ge(e_av, 2 * s - 1 + par)
                        act.activation(ea_view(ea_hi, prev, par), ps[:, 1 + par, :].rearrange("p (i j q) -> p i j q", j=2, q=S),
                                       ACT.Copy).then_inc(e_ahi, 1)
                if has(s, 0, STEPS_E):
                    act.wait_ge(e_subbed, s + 1)
                    act.activation(e_p[:, buf, :], e_p[:, buf, :], ACT.Exp, scale=float(P) ** -0.5).then_inc(e_exped, 1)
                if u % 2:
                    split_next(s, u, STEPS_E, HEADS_D, 2, WORDS_E, e_o)
                if isinstance(s, int) and s >= STEPS_E - 2 and s < STEPS_E:
                    q = HEADS_D + GROUPS_E + s - STEPS_E + 2
                    split_first(q, 4 + q % 2, WORDS_F)

            steps(act, STEPS_E, 4, 2, step_e, peel_last=True)

            round_nT(5, range(NT))
            act.wait_ge(f_gate, 1)
            act.activation(g_score[:].rearrange("p t e -> p (t e)"), ps[:, 2, 0:NT * E_MOE], ACT.Sigmoid).then_inc(f_sig, 1)

            def step_f(s, u):
                buf, prev = u % 2, (u - 1) % 2
                if has(s, 0, STEPS_F):
                    act.wait_ge(f_h1, s + 1)
                    at_least(act, f_m1, s - 1)
                    act.activation(f_silu[:, buf, :], ps[:, (3 * u) % 4, :], ACT.Silu).then_inc(f_silued, 1)
                if has(s, 1, STEPS_F):
                    act.wait_ge(f_m2, s)
                    at_least(act, f_down, s - 2)
                    act.activation(g_hi[:, prev, :], f_t2[:, prev, :], ACT.Copy).then_inc(f_ghi, 1)
                if isinstance(s, int) and s == 0:
                    for half in range(2):
                        act.wait_ge(f_combT, 1)
                        act.activation(combT[:, half * HALF:(half + 1) * HALF], ps[0:96, 4 + half, :],
                                       ACT.Copy).then_inc(f_comb_out, 1)
                split_next(s, u, STEPS_F, HEADS_D + GROUPS_E, 4, WORDS_F, f_down)

            steps(act, STEPS_F, 4, 2, step_f)

        @block.gpsimd
        def _(pool):
            def sub_lo(part, slot, lo, hi, stage_i, dst=None, src_hi=None):
                d = w_lo[:, slot, lo:hi] if dst is None else dst
                h = w_hi[:, slot, lo:hi] if src_hi is None else src_hi
                pool.wait_ge(w_hi_done, part + 1)
                pool.tensor_tensor(d, stage[:, stage_i, lo:hi], f32(h), ALU.subtract).then_inc(w_lo_done, 1)

            def sub_abc(name):
                n = BLOCK[name]
                _, slot, words = BLOCKS_ABC[n]
                if slot is None:
                    sub_lo(n, 0, 0, T, n % STAGES, ctx_lo[:], ctx_hi[:])
                else:
                    sub_lo(n, slot, 0, words, n % STAGES)

            pool.memset(k_diag[:], 0.0)
            pool.memset(v_diag[:], 0.0).then_inc(zeroed, 1)
            sub_abc("a_qk")
            sub_abc("a_vo")
            for name in ("ctx", "b_q", "b_kv", "b_o", "c_router_down"):
                sub_abc(name)
            pool.wait_ge(gate_split, 1)
            pool.tensor_tensor(gate_lo[:], gate_raw[:], f32(gate_hi[:]), ALU.subtract).then_inc(gate_split, 1)

            def add_bias(blk, row):
                pool.wait_ge(normed_done, (blk + 1) * NT)
                pool.wait_ge(loaded, N_LOADED)
                bias = bias_rows[:, row:row + 1, :].to_broadcast([P, NT, D])
                pool.tensor_tensor(x[:], x[:], bias, ALU.add).then_inc(pool_x, 1)

            def narrow_heads(h, second_half=None):
                z = hs[h.name]
                for n in range(h.steps):
                    if n == h.steps // 2 - 1 and second_half:
                        second_half()
                    p3 = probs[:, n % 4, :].rearrange("p (s k) -> p s k", k=S)
                    pool.wait_ge(z["rec"], n + 1)
                    pool.tensor_tensor(p3, p3, srec[:, n % 4, :].unsqueeze(2).to_broadcast([P, 8, S]),
                                       ALU.mult).then_inc(z["norm"], 1)

            add_bias(0, 1)
            narrow_heads(HA)
            pool.wait_ge(hs["a"]["av"], HA.steps)
            pool.memset(v_diag[:], 0.0).then_inc(zeroed, 1)
            add_bias(1, 2)

            def sums_b(half):
                for i in range(4 * half, 4 * half + 4):
                    pool.wait_ge(b_rot, 2 * i + 2)
                    if i >= 2:
                        pool.wait_ge(*((b_k, 2 * half + i % 4 - 1) if i % 4 >= 2 else (b_var, 2 * half - 1 + i % 4)))
                    pool.tensor_tensor(rot_sum[:, i % 2, :], rot[:, i % 2, 0, :], rot[:, i % 2, 1, :], ALU.add).then_inc(b_sum, 1)

            sums_b(0)
            narrow_heads(HB, lambda: sums_b(1))
            sub_abc("c_shared")
            sub_abc("c_mix0")
            sub_abc("c_mix1")
            sub_abc("c_mix2")
            sub_abc("c_mix3")
            for s in range(20):
                half = s % 2
                cols = slice(half * HALF, (half + 1) * HALF)
                if s < 4:
                    j = s // 2
                    pool.wait_ge(c_hi, s + 1)
                    pool.tensor_tensor(sh_lo[:, j, cols], c_t1[:, s % 2, :], f32(sh_hi[:, j, cols]),
                                       ALU.subtract).then_inc(c_lo, 1)
                elif s >= 6:
                    pool.wait_ge(c_m2, s - 3)
                    if s >= 8:
                        pool.wait_ge(c_acc, s - 7)
                    pool.tensor_tensor(basis[:, cols], basis[:, cols], c_t2[:, s % 2, :], ALU.add).then_inc(c_acc, 1)
            for half in range(2):
                cols = slice(half * HALF, (half + 1) * HALF)
                pool.wait_ge(c_hi, 5 + half)
                pool.tensor_tensor(basis_lo[:, cols], basis[:, cols], f32(basis_hi[:, cols]), ALU.subtract).then_inc(c_lo, 1)

            def sub_next(s, u, count, part0, slot0, words):
                odd = u % 2
                if not has(s, 2 + odd, count - 4):
                    return
                stage_i = (u // 2 + 1) % 2
                sub_lo(part0 + s + 2, slot0 + stage_i, *words[odd], stage_i)

            def sub_first(q, slot, words):
                for i, (lo, hi) in enumerate(words):
                    sub_lo(PART_D + 2 * q + i, slot, lo, hi, q % 2)

            for q in range(2):
                sub_first(q, q, WORDS_D)
            pool.wait_ge(e_v_split, 1)
            pool.tensor_tensor(w_lo[:, 4, 0:T], stage[:, 2, 0:T], f32(w_hi[:, 4, 0:T]), ALU.subtract).then_inc(e_v_split, 1)

            def step_d(s, u):
                sub_next(s, u, STEPS_D, PART_D, 0, WORDS_D)
                if isinstance(s, int) and STEPS_D - 2 <= s < STEPS_D:
                    q = HEADS_D + s - STEPS_D + 2
                    sub_first(q, 2 + q % 2, WORDS_E)

            steps(pool, STEPS_D, 4, 0, step_d, peel_last=True)

            pool.wait_ge(e_v_all, 2 * NT)

            def step_e(s, u):
                if has(s, 0, STEPS_E):
                    at_least(pool, e_av, 2 * s - 2)
                    here = slice(s * 512, (s + 1) * 512) if isinstance(s, int) else bass.ds(s * 512, 512)
                    pool.tensor_copy(ev[:, u % 2, :], v_all[:, here]).then_inc(e_v_out, 1)
                sub_next(s, u, STEPS_E, PART_E, 2, WORDS_E)
                if isinstance(s, int) and STEPS_E - 2 <= s < STEPS_E:
                    q = HEADS_D + GROUPS_E + s - STEPS_E + 2
                    sub_first(q, 4 + q % 2, WORDS_F)

            steps(pool, STEPS_E, 4, 0, step_e, peel_last=True)

            def step_f(s, u):
                prev = (u - 1) % 2
                if has(s, 1, STEPS_F):
                    pool.wait_ge(f_ghi, s)
                    pool.tensor_tensor(g_lo[:, prev, :], f_t2[:, prev, :], f32(g_hi[:, prev, :]),
                                       ALU.subtract).then_inc(f_glo, 1)
                sub_next(s, u, STEPS_F, PART_F, 4, WORDS_F)

            steps(pool, STEPS_F, 4, 2, step_f)

        @block.vector
        def _(ve):
            chained = 0

            def small(instruction):
                nonlocal chained
                instruction.then_inc(ln_chain, 1)
                chained += 1
                ve.wait_ge(ln_chain, chained)

            def add_output(blk, tiles):
                for t in tiles:
                    ve.wait_ge(y_full, 4 * blk + t // 2 + 1)
                    if blk < 2:
                        ve.wait_ge(pool_x, blk + 1)
                    ve.tensor_tensor(x[:, t, :], x[:, t, :], y_of(blk, t), ALU.add).then_inc(resid, 1)

            def layernorm(blk, tiles):
                four = slice(tiles[0], tiles[0] + 4)
                for t in tiles:
                    if blk:
                        ve.wait_ge(resid, (blk - 1) * NT + t + 1)
                    last = ve.bn_stats(stats[:, t, :], x[:, t, :])
                small(last)
                for t in tiles:
                    last = ve.bn_aggr(mean_var[:, t, :], stats[:, t, :])
                small(last)
                v, y, a = var[:, four], rstd[:, four], newton[:, four]
                small(ve.tensor_scalar(v, mean_var[:, four, 1], EPS_LN, None, ALU.add))
                small(ve.tensor_scalar(y.bitcast(I32), v.bitcast(I32), 1, None, ALU.logical_shift_right))
                small(ve.tensor_scalar(y.bitcast(I32), y.bitcast(I32), -1.0, RSQRT_SEED, ALU.mult, ALU.add))
                for _ in range(3):
                    small(ve.tensor_tensor(a, y, y, ALU.mult))
                    small(ve.scalar_tensor_tensor(out=a, in0=a, scalar=-0.5, in1=v, op0=ALU.mult, op1=ALU.mult))
                    small(ve.scalar_tensor_tensor(out=y, in0=a, scalar=1.5, in1=y, op0=ALU.add, op1=ALU.mult))
                for t in tiles:
                    ve.tensor_scalar(normed[:, t, :], x[:, t, :], mean_var[:, t, 0:1], rstd[:, t:t + 1],
                                     ALU.subtract, ALU.mult).then_inc(normed_done, 1)

            def lo_nT(blk, tiles):
                for t in tiles:
                    ve.wait_ge(nT_hi_done, blk * NT + t + 1)
                    cols = slice(t * P, (t + 1) * P)
                    ve.tensor_tensor(nT_lo[:, :, cols], ps[:, T_BANK[blk] + t % 4, 0:D].rearrange("p (k n) -> p k n", k=KC),
                                     f32(nT_hi[:, :, cols]), ALU.subtract).then_inc(nT_done, 1)

            def next_block(blk):
                first, second = range(4), range(4, NT)
                if blk:
                    add_output(blk - 1, first)
                layernorm(blk, first)
                if blk:
                    add_output(blk - 1, second)
                layernorm(blk, second)
                lo_nT(blk, first)
                lo_nT(blk, second)

            def bcast(ap, shape):
                return ap.unsqueeze(len(ap.shape)).to_broadcast(shape)

            def narrow_heads(h, second_half=None):
                z = hs[h.name]
                for n in range(h.steps + OUT_LAG + 1):
                    if n == h.steps // 2 and second_half:
                        second_half()
                    if n < h.steps:
                        s3 = ps[:, n % 2, :].rearrange("p (s k) -> p s k", k=S)
                        ve.wait_ge(z["score"], n + 1)
                        ve.tensor_reduce(smax[:, n % 4, :], s3, AX_X, ALU.max).then_inc(z["max"], 1)
                    m = n - 1
                    if 0 <= m < h.steps:
                        ve.wait_ge(z["exp"], m + 1)
                        ve.tensor_reduce(ssum[:, m % 4, :], probs[:, m % 4, :].rearrange("p (s k) -> p s k", k=S),
                                         AX_X, ALU.add).then_inc(z["sum"], 1)
                    if n < h.steps:
                        ve.wait_ge(z["max"], n + 1)
                        if n >= 4:
                            ve.wait_ge(z["tr"], n - 3)
                        ve.tensor_tensor(probs[:, n % 4, :].rearrange("p (s k) -> p s k", k=S), s3,
                                         bcast(smax[:, n % 4, :], [P, 8, S]), ALU.subtract).then_inc(z["sub"], 1)
                    if 0 <= m < h.steps:
                        ve.wait_ge(z["sum"], m + 1)
                        if m >= 4:
                            ve.wait_ge(z["norm"], m - 3)
                        ve.reciprocal(srec[:, m % 4, :], ssum[:, m % 4, :]).then_inc(z["rec"], 1)
                    m = n - OUT_LAG - 1
                    if m >= 0 and (m + 1) % h.quad == 0:
                        i = m // h.quad
                        ve.wait_ge(z["out_hi"], i + 1)
                        cols = slice(i * 256, (i + 1) * 256)
                        ve.tensor_tensor(nT_lo[:, :, cols], ps[:, 4 + i % 2, :].rearrange("p (c n) -> p c n", c=KC),
                                         f32(nT_hi[:, :, cols]), ALU.subtract).then_inc(z["out_lo"], 1)

            small(ve.memset(ones[:], 1.0))
            small(ve.tensor_copy(ones_r[:], ones[:]))
            ve.wait_ge(loaded, N_LOADED)
            for axis in range(2):
                f = slice(4 * axis, 4 * axis + 4)
                last = ve.tensor_tensor(angle[:, :, :, f], freqs[:, :, f].unsqueeze(1).to_broadcast([P, NT, 2, 4]),
                                        pos[:, :, axis:axis + 1].unsqueeze(3).to_broadcast([P, NT, 2, 4]), ALU.mult)
            small(last)
            small(ve.tensor_scalar(angle[:, :, 1, :], angle[:, :, 1, :], PI / 2, None, ALU.add))
            small(ve.tensor_scalar(turn_count[:], angle[:], 1 / (2 * PI), ROUND, ALU.mult, ALU.add))
            small(ve.tensor_scalar(turn_count[:], turn_count[:], ROUND, None, ALU.subtract))
            for part in (TWO_PI_A, TWO_PI_B):
                small(ve.scalar_tensor_tensor(out=angle[:], in0=turn_count[:], scalar=-part, in1=angle[:],
                                              op0=ALU.mult, op1=ALU.add))
            ve.tensor_scalar(angle[:], angle[:], PI_BELOW, -PI_BELOW, ALU.min, ALU.max).then_inc(angles, 1)

            for half in range(2):
                tiles = range(half * 4, half * 4 + 4)
                ve.wait_ge(x_in, 16 * (half + 1))
                layernorm(0, tiles)
                lo_nT(0, tiles)
                for i in range(6):
                    kind, c, _ = USES_A[6 * half + i]
                    n = 6 * half + i
                    if kind == "k":
                        continue
                    ve.wait_ge(a_mm, n + 1)
                    bank = PROJ_BANK[n % 4]
                    if kind == "q":
                        for v in range(HA.variants):
                            last = ve.tensor_scalar(q_view(HA)[:, c, half * 8:half * 8 + 8, v * S:(v + 1) * S],
                                                    ps[:, bank, :].rearrange("p (b q) -> p b q", q=S),
                                                    bias_col[:, c:c + 1], head_mask[:, v:v + 1], ALU.add, ALU.mult)
                        last.then_inc(a_q, 1)
                    else:
                        ve.wait_ge(zeroed, 1)
                        for r in range(2):
                            for row in range(2):
                                bias = bias_rows[64 * row:64 * row + 64, 0, r * P:(r + 1) * P].rearrange(
                                    "p (n m) -> p n m", m=16).unsqueeze(1).to_broadcast([64, 2, 8, 16])
                                last = ve.tensor_tensor(v_slots(HA, r, row, 2 * half + c)[0], v_source(HA, bank, r, row)[0],
                                                        bias, ALU.add)
                        last.then_inc(a_v, 1)
            narrow_heads(HA)

            next_block(1)

            def rotate_b(half):
                cols = slice(half * HALF, (half + 1) * HALF)
                for i in range(4 * half, 4 * half + 4):
                    kind, c = "kkqq"[i % 4], i % 2
                    for turned in range(2):
                        n = half * len(USES_B) // 2 + 2 * (i % 4) + turned
                        ve.wait_ge(b_mm, n + 1)
                        if i >= 2:
                            ve.wait_ge(b_sum, i - 1)
                        ve.tensor_tensor(rot[:, i % 2, turned, :], ps[:, b_bank(n), :],
                                         (sin_t if turned else cos_t)[:, cols], ALU.mult).then_inc(b_rot, 1)
                for c in range(KC):
                    ve.wait_ge(b_sum, 4 * half + 2 + c + 1)
                    if half:
                        ve.wait_ge(hs["b"]["score"], HB.steps // 2)
                    for v in range(HB.variants):
                        last = ve.tensor_scalar(q_view(HB)[:, c, :, v * S:(v + 1) * S],
                                                rot_sum[:, c, :].rearrange("p (b q) -> p b q", q=S),
                                                head_mask[:, 2 + v:3 + v], None, ALU.mult)
                    last.then_inc(b_var, 1)

            ve.wait_ge(trig_out, 4)
            rotate_b(0)
            narrow_heads(HB, lambda: rotate_b(1))

            next_block(2)
            small(ve.tensor_tensor(amp_sq[:], amps[:], amps[:], ALU.mult))
            small(ve.tensor_reduce(mix[:], amp_sq[:], AX_X, ALU.add))
            small(ve.tensor_reduce(mix_sum[:, 0:1], mix[:], AX_X, ALU.add))
            small(ve.tensor_scalar(mix_sum[:, 0:1], mix_sum[:, 0:1], EPS_MIX, None, ALU.add))
            small(ve.reciprocal(mix_sum[:, 1:2], mix_sum[:, 0:1]))
            small(ve.tensor_scalar(mix[:], mix[:], mix_sum[:, 1:2], e_scale[:], ALU.mult, ALU.mult))
            ve.tensor_copy(mix_rows[:], bcast(mix[:], [P, K_MIX, P])).then_inc(consts, 1)

            def c_step(s):
                half, use = s % 2, 2 * s + 1 if s < 4 else 9 + 3 * (s - 4)
                ve.wait_ge(c_up, s + 1)
                ve.wait_ge(c_silued, s + 1)
                if 2 <= s < 6:
                    ve.wait_ge(c_lo, s - 1)
                ve.tensor_tensor(c_t1[:, s % 2, :], c_silu[:, s % 2, :], ps[:, use % 4, :], ALU.mult).then_inc(c_m1, 1)
                if s >= 4:
                    ve.wait_ge(c_m1, s + 1)
                    ve.wait_ge(c_cb, s - 3)
                    first = s < 6
                    if s >= 8:
                        ve.wait_ge(c_acc, s - 7)
                    dst = basis[:, half * HALF:(half + 1) * HALF] if first else c_t2[:, s % 2, :]
                    ve.tensor_tensor(dst, c_t1[:, s % 2, :], ps[:, (use + 1) % 4, :], ALU.mult).then_inc(c_m2, 1)

            logits = [ps[:, 4 + half, :].rearrange("p (t e) -> p t e", e=E_MIX) for half in range(2)]
            for t in range(NT):
                ve.wait_ge(c_router, t // 4 + 1)
                last = ve.max(top8[:, t, :], logits[t // 4][:, t % 4, :])
            small(last)
            for half in range(2):
                tiles = slice(half * 4, half * 4 + 4)
                ve.tensor_tensor(r_exp[:, tiles, :], logits[half], top8[:, tiles, 0:1].to_broadcast([P, 4, E_MIX]),
                                 ALU.subtract).then_inc(c_sub, 1)
            for t in range(NT):
                last = ve.max_index(top_idx[:, t, :], top8[:, t, :], logits[t // 4][:, t % 4, :])
            small(last)
            small(ve.tensor_copy(top_idx_f[:], top_idx[:]))
            c_step(0)
            c_step(1)
            for j in range(TOPK):
                for t in range(NT):
                    idx = top_idx_f[:, t, j:j + 1]
                    if j == 0:
                        last = ve.tensor_scalar(r_pick[:, t, :], iota[:], idx, None, ALU.is_equal)
                    else:
                        last = ve.scalar_tensor_tensor(out=r_pick[:, t, :], in0=iota[:], scalar=idx, in1=r_pick[:, t, :],
                                                       op0=ALU.is_equal, op1=ALU.add)
                small(last)
            ve.wait_ge(c_exp, 2)
            small(ve.tensor_reduce(z_all[:], r_exp[:], AX_X, ALU.add))
            small(ve.tensor_tensor(r_pick[:], r_pick[:], r_exp[:], ALU.mult))
            small(ve.tensor_reduce(z_top[:], r_pick[:], AX_X, ALU.add))
            small(ve.scalar_tensor_tensor(out=z_top[:], in0=z_all[:], scalar=EPS_MIX, in1=z_top[:], op0=ALU.mult, op1=ALU.add))
            small(ve.reciprocal(z_rec[:], z_top[:]))
            for half in range(2):
                tiles = slice(half * 4, half * 4 + 4)
                ve.tensor_tensor(r_pick[:, tiles, :], r_pick[:, tiles, :], bcast(z_rec[:, tiles], [P, 4, E_MIX]),
                                 ALU.mult).then_inc(c_coef, 1)
            for s in range(2, 20):
                c_step(s)

            next_block(3)

            def step_d(s, u):
                buf, prev, base = u % 2, (u - 1) % 2, 2 * (u % 2)
                if has(s, 0, STEPS_D):
                    p3 = d_p[:, buf, :].rearrange("p (i k) -> p i k", k=S)
                    ve.wait_ge(d_score, s + 1)
                    own = [(slice(64 * r, 64 * r + 64), ps[64 * r:64 * r + 64, base + 1, :].rearrange(
                        "p (i b k) -> p i b k", b=2, k=S)[:, :, r]) for r in range(2)]
                    for rows, scores in own:
                        last = ve.tensor_reduce(d_max[rows, buf, :], scores, AX_X, ALU.max)
                    last.then_inc(d_maxed, 1)
                    ve.wait_ge(d_maxed, s + 1)
                    for rows, scores in own:
                        last = ve.tensor_tensor(p3[rows], scores, bcast(d_max[rows, buf, :], [64, 4, S]), ALU.subtract)
                    last.then_inc(d_subbed, 1)
                if has(s, 1, STEPS_D):
                    ve.wait_ge(d_v, s)
                    ve.wait_ge(d_cs_out, 2 * s)
                    at_least(ve, d_vlod, s - 2)
                    ve.tensor_tensor(d_val[:, prev, :], ps[:, base, :], d_cs[:, prev, :], ALU.mult).then_inc(d_vd, 1)
                if has(s, 0, STEPS_D):
                    ve.wait_ge(d_exped, s + 1)
                    ve.tensor_reduce(d_sum[:, buf, :], p3, AX_X, ALU.add).then_inc(d_summed, 1)
                    ve.wait_ge(d_summed, s + 1)
                    ve.reciprocal(d_rec[:, buf, :], d_sum[:, buf, :]).then_inc(d_recd, 1)
                if has(s, 1, STEPS_D):
                    ve.wait_ge(d_vhid, s)
                    ve.tensor_tensor(d_vlo[:, prev, :], d_val[:, prev, :], f32(d_vhi[:, prev, :]),
                                     ALU.subtract).then_inc(d_vlod, 1)
                if has(s, 0, STEPS_D):
                    ve.wait_ge(d_recd, s + 1)
                    ve.tensor_tensor(p3, p3, bcast(d_rec[:, buf, :], [P, 4, S]), ALU.mult).then_inc(d_pd, 1)
                    ve.wait_ge(d_phid, s + 1)
                    at_least(ve, d_csum, s - 1)
                    ve.tensor_tensor(d_plo[:, buf, :], d_p[:, buf, :], f32(d_phi[:, buf, :]), ALU.subtract).then_inc(d_plod, 1)

            steps(ve, STEPS_D, 4, 1, step_d)

            next_block(4)
            ve.wait_ge(late_in, 16)
            small(ve.tensor_copy(mask_bias[:], mask_u8[:]))
            small(ve.tensor_reduce(any_key[:], mask_bias[:].rearrange("p (b k) -> p b k", k=S), AX_X, ALU.max))
            small(ve.tensor_scalar(mask_bias[:], mask_bias[:], -1.0, 1e30, ALU.add, ALU.mult))

            def step_e(s, u):
                half, buf, prev = u % 2, u % 2, (u - 1) % 2
                p3 = e_p[:, buf, :].rearrange("p (b k) -> p b k", k=S)
                if has(s, 0, STEPS_E):
                    ve.wait_ge(e_score, s + 1)
                    at_least(ve, e_tr, s - 1)
                    ve.tensor_tensor(e_p[:, buf, :], ps[:, 3, :], mask_bias[:, half * HALF:(half + 1) * HALF],
                                     ALU.add).then_inc(e_masked, 1)
                    ve.wait_ge(e_masked, s + 1)
                    ve.tensor_reduce(e_max[:, buf, :], p3, AX_X, ALU.max).then_inc(e_maxed, 1)
                    ve.wait_ge(e_maxed, s + 1)
                    ve.tensor_tensor(p3, p3, bcast(e_max[:, buf, :], [P, 8, S]), ALU.subtract).then_inc(e_subbed, 1)
                if has(s, 1, STEPS_E):
                    for par in range(2):
                        ve.wait_ge(e_ahi, 2 * s - 1 + par)
                        ve.tensor_tensor(ea_view(ea_lo, prev, par), ps[:, 1 + par, :].rearrange("p (i j q) -> p i j q", j=2, q=S),
                                         f32(ea_view(ea_hi, prev, par)), ALU.subtract).then_inc(e_alo, 1)
                if has(s, 0, STEPS_E):
                    ve.wait_ge(e_exped, s + 1)
                    ve.tensor_reduce(e_sum[:, buf, :], p3, AX_X, ALU.add).then_inc(e_summed, 1)
                    ve.wait_ge(e_summed, s + 1)
                    ve.reciprocal(e_rec[:, buf, :], e_sum[:, buf, :]).then_inc(e_recd, 1)
                    ve.wait_ge(e_recd, 2 * s + 1)
                    ve.tensor_tensor(e_rec[:, buf, :], e_rec[:, buf, :], any_key[:, half * 8:half * 8 + 8],
                                     ALU.mult).then_inc(e_recd, 1)
                    ve.wait_ge(e_recd, 2 * s + 2)
                    ve.tensor_tensor(p3, p3, bcast(e_rec[:, buf, :], [P, 8, S]), ALU.mult).then_inc(e_pd, 1)

            steps(ve, STEPS_E, 4, 1, step_e)

            next_block(5)
            small(ve.memset(comb[:], 0.0))
            ve.wait_ge(f_sig, 1)
            g4 = g_score[:].rearrange("p t (g e) -> p t g e", g=4)
            small(ve.tensor_reduce(g_top[:], g4, AX_X, ALU.max))
            top_i = g_top[:].unsqueeze(3).to_broadcast([P, NT, 4, 4])
            top_j = g_top[:].unsqueeze(2).to_broadcast([P, NT, 4, 4])
            small(ve.tensor_tensor(g_cmp[:], top_j, top_i, ALU.is_gt))
            small(ve.tensor_tensor(g_eq[:], top_j, top_i, ALU.is_equal))
            small(ve.tensor_tensor(g_eq[:], g_eq[:], lower[:].unsqueeze(1).to_broadcast([P, NT, 4, 4]), ALU.mult))
            small(ve.tensor_tensor(g_cmp[:], g_cmp[:], g_eq[:], ALU.add))
            small(ve.tensor_reduce(g_rank[:], g_cmp[:], AX_X, ALU.add))
            small(ve.tensor_scalar(g_rank[:], g_rank[:], 1.5, None, ALU.is_lt))
            small(ve.tensor_tensor(g_mask[:].rearrange("p t (g e) -> p t g e", g=4), g4,
                                   g_rank[:].unsqueeze(3).to_broadcast([P, NT, 4, 4]), ALU.mult))
            for t in range(NT):
                last = ve.max(g_top8[:, t, :], g_mask[:, t, :])
            small(last)
            for t in range(NT):
                last = ve.max_index(g_idx[:, t, :], g_top8[:, t, :], g_mask[:, t, :])
            small(last)
            small(ve.tensor_copy(g_idx_f[:], g_idx[:]))
            for j in range(TOPK):
                idx = g_idx_f[:, :, j:j + 1].to_broadcast([P, NT, E_MOE])
                ids = iota[:, 0:E_MOE].unsqueeze(1).to_broadcast([P, NT, E_MOE])
                if j == 0:
                    small(ve.tensor_tensor(g_pick[:], ids, idx, ALU.is_equal))
                else:
                    small(ve.tensor_tensor(g_mask[:], ids, idx, ALU.is_equal))
                    small(ve.tensor_tensor(g_pick[:], g_pick[:], g_mask[:], ALU.add))
            small(ve.tensor_tensor(g_pick[:], g_pick[:], g_score[:], ALU.mult))
            small(ve.tensor_reduce(g_sum[:], g_pick[:], AX_X, ALU.add))
            small(ve.reciprocal(g_rec[:], g_sum[:]))
            small(ve.tensor_tensor(g_pick[:], g_pick[:], bcast(g_rec[:], [P, NT, E_MOE]), ALU.mult))
            small(ve.memset(comb[:, :, E_MOE:E_MOE + 1], 1.0))
            for i in range(3):
                small(ve.tensor_copy(comb_b[:], g_pick[:]))
                last = ve.tensor_copy(comb[:, :, 32 * i:32 * i + E_MOE], comb_b[:])
                if i < 2:
                    small(last)
                    small(ve.tensor_tensor(g_pick[:], g_pick[:], comb[:, :, 32 * i:32 * i + E_MOE], ALU.subtract))
            last.then_inc(f_comb, 1)

            def step_f(s, u):
                buf = u % 2
                if has(s, 0, STEPS_F):
                    ve.wait_ge(f_h3, s + 1)
                    ve.wait_ge(f_silued, s + 1)
                    ve.tensor_tensor(f_t1[:, buf, :], f_silu[:, buf, :], ps[:, (3 * u + 1) % 4, :], ALU.mult).then_inc(f_m1, 1)
                    ve.wait_ge(f_m1, s + 1)
                    ve.wait_ge(f_cb, s + 1)
                    at_least(ve, f_glo, s - 1)
                    ve.tensor_tensor(f_t2[:, buf, :], f_t1[:, buf, :], ps[:, (3 * u + 2) % 4, :], ALU.mult).then_inc(f_m2, 1)

            steps(ve, STEPS_F, 4, 0, step_f)
            add_output(5, range(NT))


_OUT = (T, D)


def _chunks(w):
    k = w.shape[0] // P
    return w.reshape(k, P, w.shape[1]).transpose(1, 0, 2).reshape(P, -1)


def _out_rows(h):
    import numpy as np
    n = np.arange(D).reshape(KC, 2, 2, h.pairs, 2, h.width)
    return n.transpose(0, 1, 4, 3, 2, 5).reshape(-1)


def _value_columns(h):
    import numpy as np
    n = np.arange(D).reshape(KC, 2, 2, h.pairs, 2, h.width)
    return n.transpose(2, 0, 1, 4, 3, 5).reshape(-1)


def _layouts(i):
    import numpy as np

    def cat(*a):
        return np.ascontiguousarray(np.concatenate(a, axis=1))

    g = {}
    g["x"] = i["x"].reshape(T, D)
    g["w_a_qk"] = cat(_chunks(i["L0_attn_wq"].T), _chunks(i["L0_attn_wk"].T))
    g["w_a_vo"] = cat(_chunks(i["L0_attn_wv"].T[:, _value_columns(HA)]), _chunks(i["L0_attn_wo"].T[_out_rows(HA)]))
    g["w_ctx"] = i["ctx_1024"].reshape(T, P).T
    swap = np.arange(D).reshape(-1, 2)[:, ::-1].reshape(-1)
    wq, wk, wv = i["L0_xattn_Wq"], i["L0_xattn_Wkv"][:, :D], i["L0_xattn_Wkv"][:, D:]
    g["w_b_q"] = cat(_chunks(wq), _chunks(wq[:, swap]))
    g["w_b_kv"] = cat(wk, wk[:, swap], wv[:, _value_columns(HB)])
    g["w_b_o"] = _chunks(i["L0_xattn_Wout"][_out_rows(HB)])
    g["w_c_router_down"] = cat(_chunks(i["L0_ffn_w_router"]), _chunks(i["L0_ffn_shared_w_down"]), i["L0_ffn_w_down"])

    def gate_up(gate, up, js):
        return cat(*[_chunks(w[:, j * P:(j + 1) * P]) for j in js for w in (gate, up)])

    g["w_c_shared"] = gate_up(i["L0_ffn_shared_w_gate"], i["L0_ffn_shared_w_up"], range(2))
    for r in range(4):
        g[f"w_c_mix{r}"] = gate_up(i["L0_ffn_w_gate"], i["L0_ffn_w_up"], (2 * r, 2 * r + 1))
    qkv, wo = i["L1_attn_w_qkv"], i["L1_attn_w_o"]
    F = HEADS_D * P
    g["w_d"] = np.stack([cat(*[_chunks(qkv[:, n * F + h * P:n * F + (h + 1) * P]) for n in range(3)],
                             wo[h * P:(h + 1) * P]) for h in range(HEADS_D)])
    q, k, v, o = (i["L1_xattn_W" + n] for n in "qkvo")
    g["w_e"] = np.stack([cat(*[_chunks(q[:, h * P:(h + 1) * P]) for h in (2 * n, 2 * n + 1)],
                             k[:, n * P:(n + 1) * P],
                             o[2 * n * P:(2 * n + 1) * P], o[(2 * n + 1) * P:(2 * n + 2) * P]) for n in range(GROUPS_E)])

    g["w_e_v"] = v

    def rows(expert, shared):
        a = np.concatenate([expert, shared])
        return np.concatenate([a, np.zeros((CHUNKS_F * P - len(a), D), np.float32)])

    w1 = rows(i["L1_ffn_W1"].reshape(-1, D), i["L1_ffn_Ws1"])
    w3 = rows(i["L1_ffn_W3"].reshape(-1, D), i["L1_ffn_Ws3"])
    w2 = rows(i["L1_ffn_W2"].transpose(0, 2, 1).reshape(-1, D), i["L1_ffn_Ws2"].T)
    g["w_f"] = np.stack([cat(_chunks(w1[n * P:(n + 1) * P].T), _chunks(w3[n * P:(n + 1) * P].T),
                             w2[n * P:(n + 1) * P]) for n in range(CHUNKS_F)])
    g["gate"] = _chunks(i["L1_ffn_gate_w"].T)
    g["bias_col"] = cat(i["L0_attn_bq"].reshape(KC, P).T, i["L0_attn_bk"].reshape(KC, P).T)
    g["bias_rows"] = np.stack([i["L0_attn_bv"][_value_columns(HA)], i["L0_attn_bo"], i["L0_xattn_bout"]])
    g["pos"] = i["fside_BxSx2_0"].reshape(NT, P, 2).transpose(1, 0, 2)
    g["mask"] = i["mask_BxS2_bf1"].reshape(1, T).view(np.uint8)
    g["amps"] = i["L0_ffn_amplitudes"]
    g["e_scale"] = i["L0_ffn_expert_scale"].reshape(P, 1)

    p = np.arange(P)
    g["ident"] = np.eye(P, dtype=np.float32)
    g["iota"] = np.tile(p.astype(np.float32), (P, 1))
    g["head_mask"] = np.stack([(p // 16) % 2 == v for v in range(2)] + [(p // 8) % 4 == v for v in range(4)],
                              axis=1).astype(np.float32)
    g["lower"] = np.tile((np.arange(4)[None, :] < np.arange(4)[:, None]).astype(np.float32), (P, 1, 1))
    m = np.arange(8)
    freq = np.array([1.0, np.float32(10000.0) ** np.float32(-0.5)], np.float32)[(m % 4) // 2]
    freqs = np.stack([np.where(m % 2 == 0, -freq, freq), freq]).astype(np.float32)
    g["freqs"] = np.tile(freqs, (P, 1, 1))
    hidden = np.arange(CHUNKS_F * P)
    owner = np.where(hidden < 16 * 176, hidden // 176, 16)
    sel = np.zeros((96, CHUNKS_F * P), np.float32)
    for r in range(96):
        if r % 32 < 16 or r == 16:
            sel[r] = owner == r % 32
    g["select"] = (sel.reshape(96, CHUNKS_F, P) * 0x3F80).astype(np.uint16)
    return g


_INS = ['x', 'ctx_1024', 'fside_BxSx2_0', 'mask_BxS2_bf1', 'L0_attn_wq', 'L0_attn_bq', 'L0_attn_wk', 'L0_attn_bk',
        'L0_attn_wv', 'L0_attn_bv', 'L0_attn_wo', 'L0_attn_bo', 'L0_xattn_Wq', 'L0_xattn_Wkv', 'L0_xattn_Wout',
        'L0_xattn_bout', 'L0_ffn_w_router', 'L0_ffn_w_gate', 'L0_ffn_w_up', 'L0_ffn_w_down', 'L0_ffn_amplitudes',
        'L0_ffn_expert_scale', 'L0_ffn_shared_w_gate', 'L0_ffn_shared_w_up', 'L0_ffn_shared_w_down', 'L1_attn_w_qkv',
        'L1_attn_w_o', 'L1_xattn_Wq', 'L1_xattn_Wk', 'L1_xattn_Wv', 'L1_xattn_Wo', 'L1_ffn_gate_w', 'L1_ffn_W1',
        'L1_ffn_W2', 'L1_ffn_W3', 'L1_ffn_Ws1', 'L1_ffn_Ws2', 'L1_ffn_Ws3']


def kernel(**inputs):
    import numpy as _np
    import concourse.bacc as _bacc
    from concourse import mybir as _mybir
    from concourse.bass_utils import run_bass_kernel_spmd as _run

    nc = _bacc.Bacc("TRN2", target_bir_lowering=False, num_devices=1)
    laid = _layouts({n: _np.asarray(inputs[n]) for n in _INS})
    arrays, aps = {}, {}
    for name, a in laid.items():
        a = _np.ascontiguousarray(a)
        arrays[f"in_{name}"] = a
        aps[name] = nc.dram_tensor(f"in_{name}", a.shape, _mybir.dt.from_np(a.dtype), kind="ExternalInput").ap()
    out = nc.dram_tensor("out", _OUT, _mybir.dt.float32, kind="ExternalOutput").ap()
    decoder(nc, aps, out)
    r = _run(nc, [arrays], core_ids=[0])
    return r.results[0]["out"].reshape(B, S, D)
```

```python
from contextlib import ExitStack

import concourse.bass as bass
from concourse import mybir

F32 = mybir.dt.float32
F32R = mybir.dt.float32r
BF16 = mybir.dt.bfloat16
I32 = mybir.dt.int32
U32 = mybir.dt.uint32
U8 = mybir.dt.uint8
U16 = mybir.dt.uint16
ALU = mybir.AluOpType
ACT = mybir.ActivationFunctionType
AX_X = mybir.AxisListType.X

P = 128
B, S, D = 16, 64, 256
T = B * S
NT = T // P
KC = D // P
HALF = T // 2
PAIRS = HALF // P
EPS_LN = 1e-5
EPS_MIX = 1e-8
HEADS_D, GROUPS_E = 16, 8
STEPS_D, STEPS_E = 2 * HEADS_D, 2 * GROUPS_E
K_MIX, E_MIX, TOPK = 8, 128, 4
E_MOE = 16
CHUNKS_F = 25
STEPS_F = 2 * CHUNKS_F
STAGES = 4
SLOTS = 6
WORDS = 1280
PI = 3.141592653589793
TWO_PI_A = 6.28125
TWO_PI_B = 2 * PI - TWO_PI_A
PI_BELOW = 3.1415925
ROUND = 12582912.0
RSQRT_SEED = float(0x5F3759DF)

BLOCKS_ABC = [
    ("a_qk", 0, 1024), ("a_vo", 1, 1024), ("ctx", None, T), ("b_q", 2, 1024), ("b_kv", 3, 768), ("b_o", 4, 512),
    ("c_router_down", 5, 1024), ("c_shared", 0, 1024), ("c_mix0", 1, 1024), ("c_mix1", 2, 1024),
    ("c_mix2", 3, 1024), ("c_mix3", 4, 1024),
]
BLOCK = {name: n for n, (name, _, _) in enumerate(BLOCKS_ABC)}
NB_ABC = len(BLOCKS_ABC)
PART_D = NB_ABC
PART_E = PART_D + 2 * HEADS_D
PART_F = PART_E + 2 * GROUPS_E


class Heads:

    def __init__(self, name, width):
        self.name, self.width = name, width
        self.variants = 32 // width
        self.pairs = self.variants // 2
        self.chunks = KC // self.pairs
        self.steps = B * self.pairs
        self.batches = B if self.pairs == 1 else B // 2
        self.quad = 4 * self.pairs

    def batch(self, n):
        return n // self.pairs

    def products(self, n):
        return [(c, 0) for c in range(KC)] if self.pairs == 1 else [(n % 2, vh) for vh in range(2)]


HA, HB = Heads("a", 16), Heads("b", 8)
PROJ_BANK = [0, 1, 6, 7]
TR_LAG, AV_LAG = 3, 4
OUT_LAG = AV_LAG + 1

USES_A = [(kind, i, half) for half in range(2) for kind, i in
          [("q", 0), ("q", 1), ("k", 0), ("k", 1), ("v", 0), ("v", 1)]]
USES_B = [(kind, i, half) for half in range(2) for kind, i in
          [(k + r, c) for k in "kq" for c in range(KC) for r in ("", "r")] + [("v", 0), ("v", 1)]]


USES_C = ([(kind, s) for s in range(6) for kind in ("gate", "up")] + [("coef", 4), ("coef", 5)]
          + [(kind, s) for s in range(6, 20) for kind in ("gate", "up", "coef")])


def steps(eng, count, unroll, lag, body, peel_last=False):
    for s in range(unroll):
        body(s, s)
    turns = count // unroll - int(peel_last)
    with eng.Fori(1, turns) as i:
        for u in range(unroll):
            body(i * unroll + u, u)
    for s in range(turns * unroll, count + lag):
        body(s, s % unroll)


def has(s, lag, count):
    return not isinstance(s, int) or 0 <= s - lag < count


def at_least(eng, semaphore, value):
    if not isinstance(value, int) or value > 0:
        eng.wait_ge(semaphore, value)


def decoder(nc, A, out):
    ctx = ExitStack()
    with ctx:
        def sb(name, shape, dt=F32):
            return ctx.enter_context(nc.sbuf_tensor(name, shape, dt))

        def sem(name):
            return ctx.enter_context(nc.semaphore(name))

        ps = ctx.enter_context(nc.psum_tensor("ps", [P, 8, 512], F32))

        x = sb("x_sb", [P, NT, D])
        normed = sb("normed", [P, NT, D])
        nT_hi, nT_lo = sb("nT_hi", [P, KC, T], F32R), sb("nT_lo", [P, KC, T], F32R)
        ctx_hi, ctx_lo = sb("ctx_hi", [P, T], F32R), sb("ctx_lo", [P, T], F32R)
        ident, iota = sb("ident", [P, P]), sb("iota", [P, P])
        ones, ones_r = sb("ones", [P, P]), sb("ones_r", [P, P], F32R)
        stage = sb("stage", [P, STAGES, WORDS])
        w_hi, w_lo = sb("w_hi", [P, SLOTS, WORDS], F32R), sb("w_lo", [P, SLOTS, WORDS], F32R)
        stats, mean_var = sb("stats", [P, NT, 6]), sb("mean_var", [P, NT, 2])
        var, rstd, newton = sb("var", [P, NT]), sb("rstd", [P, NT]), sb("newton", [P, NT])
        gate_raw = sb("gate_raw", [P, KC * E_MOE])
        gate_hi, gate_lo = sb("gate_hi", [P, KC * E_MOE], F32R), sb("gate_lo", [P, KC * E_MOE], F32R)
        amps, amp_sq = sb("amps", [P, K_MIX, 2]), sb("amp_sq", [P, K_MIX, 2])
        mix, mix_sum, e_scale = sb("mix", [P, K_MIX]), sb("mix_sum", [P, 2]), sb("e_scale", [P, 1])
        lower = sb("lower", [P, 4, 4])

        areas = ExitStack()

        def ar(name, shape, dt=F32):
            return areas.enter_context(nc.sbuf_tensor(name, shape, dt))

        q_var = ar("q_var", [P, 2 * B * P])
        probs, probsT = ar("probs", [P, 4, 512]), ar("probsT", [P, 2, 512])
        smax, ssum, srec = (ar(n, [P, 4, 8]) for n in ("smax", "ssum", "srec"))
        head_mask, bias_col = ar("head_mask", [P, 6]), ar("bias_col", [P, 4])
        bias_rows = ar("bias_rows", [P, 3, D])
        pos, freqs = ar("pos", [P, NT, 2]), ar("freqs", [P, 2, 8])
        angle, turn_count, turn_part = (ar(n, [P, NT, 2, 8]) for n in ("angle", "turn_count", "turn_part"))
        v_diag = ar("v_diag", [P, B * 256])
        k_diag = ar("k_diag", [P, KC * B * 4 * S])
        areas.close()
        rotary = k_diag[:, KC * (B // 2) * 4 * S:]
        sin_t, cos_t = rotary[:, 0:T], rotary[:, T:2 * T]
        rot_sum = rotary[:, 2 * T:2 * T + 1024].rearrange("p (a n) -> p a n", a=2)
        sines = rotary[:, 2 * T:4 * T].rearrange("p (t c n) -> p t c n", t=NT, c=2)
        def rotated(i):
            room = q_var[:, 0:2048] if i < 2 else normed[:].rearrange("p t n -> p (t n)")
            return room.rearrange("p (a b n) -> p a b n", a=2, b=2)[:, i % 2]


        c_silu, c_t1, c_t2 = ar("c_silu", [P, 2, 512]), ar("c_t1", [P, 2, 512]), ar("c_t2", [P, 2, 512])
        basis = ar("basis", [P, T])
        basis_hi, basis_lo = ar("basis_hi", [P, T], F32R), ar("basis_lo", [P, T], F32R)
        sh_hi, sh_lo = ar("sh_hi", [P, 2, T], F32R), ar("sh_lo", [P, 2, T], F32R)
        r_exp, r_pick = ar("r_exp", [P, NT, E_MIX]), ar("r_pick", [P, NT, E_MIX])
        coefT, mix_rows = ar("coefT", [P, T]), ar("mix_rows", [P, K_MIX, P])
        top8, top_idx, top_idx_f = ar("top8", [P, NT, 8]), ar("top_idx", [P, NT, 8], U32), ar("top_idx_f", [P, NT, 8])
        z_all, z_top, z_rec = ar("z_all", [P, NT]), ar("z_top", [P, NT]), ar("z_rec", [P, NT])
        areas.close()

        dq, dk, d_p = ar("dq", [P, 2, 512]), ar("dk", [P, 2, 512]), ar("d_p", [P, 2, 256])
        d_phi, d_plo = ar("d_phi", [P, 2, 256], F32R), ar("d_plo", [P, 2, 256], F32R)
        d_max, d_sum, d_rec = ar("d_max", [P, 2, 4]), ar("d_sum", [P, 2, 4]), ar("d_rec", [P, 2, 4])
        d_cs, d_val = ar("d_cs", [P, 2, 512]), ar("d_val", [P, 2, 512])
        d_vhi, d_vlo = ar("d_vhi", [P, 2, 512], F32R), ar("d_vlo", [P, 2, 512], F32R)
        areas.close()

        eq = ar("eq", [P, 2, 8, 2 * S])
        ek, ev = ar("ek", [P, 2, 512]), ar("ev", [P, 2, 512])
        v_all = ar("v_all", [P, GROUPS_E * T])
        e_p, e_pT = ar("e_p", [P, 2, 512]), ar("e_pT", [P, 512])
        e_max, e_sum, e_rec = ar("e_max", [P, 2, 8]), ar("e_sum", [P, 2, 8]), ar("e_rec", [P, 2, 8])
        ea_hi, ea_lo = ar("ea_hi", [P, 2, 2, 512], F32R), ar("ea_lo", [P, 2, 2, 512], F32R)
        mask_u8, mask_bias, any_key = ar("mask_u8", [P, T], U8), ar("mask_bias", [P, T]), ar("any_key", [P, B])
        areas.close()

        f_silu, f_t1, f_t2 = ar("f_silu", [P, 2, 512]), ar("f_t1", [P, 2, 512]), ar("f_t2", [P, 2, 512])
        g_hi, g_lo = ar("g_hi", [P, 2, 512], F32R), ar("g_lo", [P, 2, 512], F32R)
        g_score, g_mask, g_pick = (ar(n, [P, NT, E_MOE]) for n in ("g_score", "g_mask", "g_pick"))
        g_top, g_rank = ar("g_top", [P, NT, 4]), ar("g_rank", [P, NT, 4])
        g_cmp, g_eq = ar("g_cmp", [P, NT, 4, 4]), ar("g_eq", [P, NT, 4, 4])
        g_top8, g_idx, g_idx_f = ar("g_top8", [P, NT, 8]), ar("g_idx", [P, NT, 8], U32), ar("g_idx_f", [P, NT, 8])
        g_sum, g_rec = ar("g_sum", [P, NT]), ar("g_rec", [P, NT])
        comb, comb_b = ar("comb", [P, NT, 96]), ar("comb_b", [P, NT, E_MOE], BF16)
        gateT = ar("gateT", [E_MOE, T])
        combT, select = ar("combT", [96, T], BF16), ar("select", [96, CHUNKS_F, P], BF16)
        areas.close()

        loaded = sem("loaded")
        x_in = [sem(f"x_in{i}") for i in range(2)]
        ident_in = sem("ident_in")
        late_in = sem("late_in")
        gate_in = sem("gate_in")
        w_in = [sem(f"w_in{i}") for i in range(STAGES)]
        wd_in = [sem(f"wd_in{i}") for i in range(2)]
        w_hi_done, w_lo_done = sem("w_hi_done"), sem("w_lo_done")
        gate_split = sem("gate_split")
        resid = sem("resid")
        ln_chain = sem("ln_chain")
        normed_done = sem("normed_done")
        ln_tr = sem("ln_tr")
        nT_hi_done, nT_done = sem("nT_hi_done"), sem("nT_done")
        y_full = sem("y_full")
        pool_x = sem("pool_x")
        stored = sem("stored")
        consts = sem("consts")

        angles, sined = sem("angles"), sem("sined")
        trig_tr, trig_out = sem("trig_tr"), sem("trig_out")
        zeroed = sem("zeroed")
        a_mm, b_mm = sem("a_mm"), sem("b_mm")
        a_q, a_k, a_v = sem("a_q"), sem("a_k"), sem("a_v")
        b_rot, b_v = sem("b_rot"), sem("b_v")
        b_sum, b_var, b_k = sem("b_sum"), sem("b_var"), sem("b_k")
        hs = {h.name: {k: sem(f"heads_{h.name}_{k}") for k in
                       ("score", "max", "sub", "exp", "sum", "rec", "norm", "tr", "probsT", "av", "out_hi", "out_lo")}
              for h in (HA, HB)}

        c_logit, c_logit_out, c_router, c_sub, c_exp, c_coef, c_coefT, c_coef_out = (
            sem("c_" + n) for n in ("logit", "logit_out", "router", "sub", "exp", "coef", "coefT", "coef_out"))
        c_gate, c_up, c_cb = sem("c_gate"), sem("c_up"), sem("c_cb")
        c_silued, c_m1, c_m2, c_acc, c_hi, c_lo = (sem("c_" + n) for n in ("silued", "m1", "m2", "acc", "hi", "lo"))

        (d_qk, d_qk_out, d_score, d_maxed, d_subbed, d_exped, d_summed, d_recd, d_pd, d_csum, d_cs_out, d_v,
         d_vd, d_vhid, d_vlod, d_o, d_phid, d_plod) = (sem("d_" + n) for n in
                                     ("qk", "qk_out", "score", "maxed", "subbed", "exped", "summed", "recd", "pd",
                                      "csum", "cs_out", "v", "vd", "vhid", "vlod", "o", "phid", "plod"))
        (e_q, e_v_mm, e_v_in, e_v_split, e_v_all, e_qk_out, e_v_out, e_score, e_masked, e_maxed, e_subbed, e_exped, e_summed, e_recd, e_pd, e_tr,
         e_pT_out, e_av, e_ahi, e_alo, e_o) = (sem("e_" + n) for n in
                                               ("q", "v_mm", "v_in", "v_split", "v_all", "qk_out", "v_out", "score", "masked", "maxed", "subbed",
                                                "exped", "summed", "recd", "pd", "tr", "pT_out", "av", "ahi", "alo",
                                                "o"))
        (f_gate, f_gate_out, f_sig, f_comb, f_combT, f_comb_out, f_h1, f_h3, f_cb, f_silued, f_m1, f_m2, f_ghi, f_glo,
         f_down) = (sem("f_" + n) for n in
                    ("gate", "gate_out", "sig", "comb", "combT", "comb_out", "h1", "h3", "cb", "silued", "m1", "m2",
                     "ghi", "glo", "down"))

        def f32(ap):
            return ap.bitcast(F32)

        def c_bank(kind, s):
            return ps[:, USES_C.index((kind, s)) % 4, :]

        def use_done(uses, n):
            kind = uses[n][0]
            if uses is USES_A:
                s = {"q": a_q, "k": a_k, "v": a_v}[kind]
                return s, sum(u[0] == kind for u in uses[:n + 1])
            if kind == "v":
                return b_v, sum(u[0] == "v" for u in uses[:n + 1])
            return b_rot, sum(u[0] != "v" for u in uses[:n + 1])

        def b_bank(n):
            return (4, 5, 6, 7, 0, 1, 2, 3, 6, 7, 6, 7, 0, 1, 6, 7, 0, 1, 6, 7)[n]

        def q_view(h):
            return q_var[:].rearrange("p (c b n) -> p c b n", c=KC, b=h.batches)

        def k_view(h):
            return k_diag[:, 0:KC * h.batches * 4 * S].rearrange("p (c b g k) -> p c b g k", c=KC, b=h.batches, g=4)

        def v_view(h):
            return v_diag[:].rearrange("p (b c j v w n) -> p b c j v w n", b=h.batches, c=KC, j=2, v=2, w=h.pairs)

        def v_slots(h, r, row, i):
            rows = v_diag[64 * r:64 * r + 64, i * 4 * 8 * 32 * h.pairs:(i + 1) * 4 * 8 * 32 * h.pairs]
            slots = rows.rearrange("p (t o n w m) -> p t o n w m", t=2, o=2, w=h.pairs, m=32)[:, :, row]
            d = h.width
            return [slots[:, :, :, w, 16 * w + d * r:16 * w + d * r + d] for w in range(h.pairs)]

        def v_source(h, bank, r, row):
            tiles = ps[64 * row:64 * row + 64, bank, :].rearrange("p (t n) -> p t n", t=2)[:, :, r * P:(r + 1) * P]
            per_width = tiles.rearrange("p t (n w m) -> p t n w m", w=h.pairs, m=h.width)
            return [per_width[:, :, :, w, :] for w in range(h.pairs)]

        def ea_view(dst, buf, par):
            return dst[:, buf, :, :].rearrange("p j (i r q) -> p r i j q", r=2, q=S)[:, par]

        WORDS_D, WORDS_E, WORDS_F = [(0, 768), (768, 1024)], [(0, 640), (640, 1152)], [(0, 512), (512, 768)]

        T_BANK = [2, 4, 4, 0, 0, 0]
        Y_BANK = [0, 0, 4, 4, 4, 4]

        def t_bank(block, t):
            return T_BANK[block] + t % 4 if block == 0 else (T_BANK[block] + t) % 8

        FIRST, SECOND = range(4), range(4, NT)

        def y_of(block, t):
            return ps[:, Y_BANK[block] + t // 2, (t % 2) * D:(t % 2 + 1) * D]

        block = ctx.enter_context(nc.Block())

        @block.sync
        def _(sp):
            x_tiles = A["x"].rearrange("(t p) d -> p t d", p=P)
            for half in range(2):
                ts = slice(half * PAIRS, (half + 1) * PAIRS)
                sp.dma_start(x[:, ts, :], x_tiles[:, ts, :]).then_inc(x_in[half], 16)

            def load_abc(n):
                name, _, words = BLOCKS_ABC[n]
                if n >= STAGES:
                    sp.wait_ge(w_lo_done, n - STAGES + 1)
                sp.dma_start(stage[:, n % STAGES, 0:words], A["w_" + name]).then_inc(w_in[n % STAGES], 16)

            load_abc(0)
            sp.dma_start(ident[:], A["ident"]).then_inc(ident_in, 16)
            sp.dma_start(head_mask[:], A["head_mask"]).then_inc(loaded, 16)
            sp.dma_start(bias_col[:], A["bias_col"]).then_inc(loaded, 16)
            sp.dma_start(bias_rows[:], A["bias_rows"].rearrange("(o r) d -> o r d", o=1).to_broadcast([P, 3, D])
                         ).then_inc(loaded, 16)
            sp.dma_start(pos[:], A["pos"]).then_inc(loaded, 16)
            sp.dma_start(freqs[:], A["freqs"]).then_inc(loaded, 16)
            load_abc(1)
            sp.dma_start(amps[:], A["amps"]).then_inc(loaded, 16)
            sp.dma_start(e_scale[:], A["e_scale"]).then_inc(loaded, 16)
            sp.dma_start(iota[:], A["iota"]).then_inc(loaded, 16)
            sp.dma_start(lower[:], A["lower"]).then_inc(loaded, 16)
            sp.dma_start(gate_raw[:], A["gate"]).then_inc(gate_in, 16)
            for n in range(2, NB_ABC):
                load_abc(n)

            def load_def(src, q, i, stage_i, words):
                peeled = isinstance(q, int)
                sp.wait_ge(w_lo_done, NB_ABC - STAGES + 1 + q if peeled and q < 2 else PART_D + 2 * q - 2)
                sp.dma_start(stage[:, stage_i, 0:words], src[bass.ds(i, 1), :, :].rearrange("o p n -> p (o n)")
                             ).then_inc(wd_in[stage_i], 16)

            sp.wait_ge(w_lo_done, max(n for n in range(NB_ABC) if n % STAGES == 2) + 1)
            sp.dma_start(stage[:, 2, 0:T], A["w_e_v"]).then_inc(e_v_in, 16)

            def load_d(h, u):
                load_def(A["w_d"], h, h, u, 1024)

            steps(sp, HEADS_D, 2, 0, load_d)

            def load_e(g, u):
                load_def(A["w_e"], HEADS_D + g, g, u, WORDS_E[1][1])

            for g in range(2):
                load_e(g, g)
            sp.wait_ge(resid, 4 * NT)
            sp.dma_start(mask_u8[:], A["mask"].to_broadcast([P, T])).then_inc(late_in, 16)
            with sp.Fori(1, GROUPS_E // 2) as i:
                for u in range(2):
                    load_e(i * 2 + u, u)

            def load_f(j, u):
                load_def(A["w_f"], HEADS_D + GROUPS_E + j, j, u, 768)

            for j in range(2):
                load_f(j, j)
            sp.wait_ge(resid, 5 * NT)
            sp.dma_start(select[:].bitcast(U16), A["select"]).then_inc(late_in, 16)
            with sp.Fori(1, CHUNKS_F // 2) as i:
                for u in range(2):
                    load_f(i * 2 + u, u)
            load_f(CHUNKS_F - 1, 0)

            out_tiles = out.rearrange("(t p) d -> p t d", p=P)
            for t in range(0, NT, 2):
                sp.wait_ge(resid, 5 * NT + t + 2)
                sp.dma_start(out_tiles[:, t:t + 2, :], x[:, t:t + 2, :]).then_inc(stored, 16)
            sp.wait_ge(stored, 16 * NT // 2)

        N_LOADED = 16 * 9

        @block.tensor
        def _(pe):
            def mm(o, lhsT, rhs, start, stop):
                return pe.matmul(o, lhsT, rhs, start=start, stop=stop, skip_group_check=True)

            def mm3(o, l_hi, l_lo, r_hi, r_lo, start, stop):
                mm(o, l_hi, r_hi, start, False)
                mm(o, l_hi, r_lo, False, False)
                return mm(o, l_lo, r_hi, False, stop)

            def w(slot, lo, hi):
                return w_hi[:, slot, lo:hi], w_lo[:, slot, lo:hi]

            def weights(part):
                pe.wait_ge(w_lo_done, part + 1)

            def feature_major(o, slot, at, width, c, half):
                for k in range(KC):
                    lo = at + k * width + c * P
                    cols = slice(half * HALF, (half + 1) * HALF)
                    last = mm3(o, *w(slot, lo, lo + P), nT_hi[:, k, cols], nT_lo[:, k, cols], k == 0, k == KC - 1)
                return last

            def transposes(blk, tiles):
                for t in tiles:
                    pe.wait_ge(normed_done, blk * NT + t + 1)
                    if t >= 4 and blk == 0:
                        pe.wait_ge(nT_done, t - 3)
                    for k in range(KC):
                        last = pe.transpose(ps[:, t_bank(blk, t), k * P:(k + 1) * P],
                                            normed[:, t, k * P:(k + 1) * P], ident[:])
                    last.then_inc(ln_tr, 1)

            def narrow_heads(h, blk, wo_slot, wo_at, wo_part, second_half=None):
                z, q, k, v = hs[h.name], q_view(h), k_view(h), v_view(h)
                for n in range(h.steps + AV_LAG):
                    if n == h.steps // 2 and second_half:
                        second_half()
                    if n < h.steps:
                        if n >= 2:
                            pe.wait_ge(z["sub"], n - 1)
                        b = h.batch(n) % h.batches
                        for i, (c, w_pair) in enumerate(h.products(n)):
                            last = mm(ps[:, n % 2, i * 256:(i + 1) * 256], q[:, c, b, w_pair * P:(w_pair + 1) * P],
                                      k[:, c, b].rearrange("p g k -> p (g k)"), True, True)
                        last.then_inc(z["score"], 1)
                    m = n - TR_LAG
                    if 0 <= m < h.steps:
                        pe.wait_ge(z["norm"], m + 1)
                        if m >= 2:
                            pe.wait_ge(z["probsT"], m - 1)
                        for i in range(4):
                            last = pe.transpose(ps[:, 2 + m % 2, i * P:(i + 1) * P], probs[:, m % 4, i * P:(i + 1) * P], ident[:])
                        last.then_inc(z["tr"], 1)
                    m = n - AV_LAG
                    if 0 <= m < h.steps:
                        full = m // h.quad
                        pe.wait_ge(z["probsT"], m + 1)
                        if m % h.quad == 0 and full >= 2:
                            pe.wait_ge(z["out_lo"], full - 1)
                        if h is HB:
                            pe.wait_ge(b_v, 2 + 2 * (m // (h.steps // 2)))
                        b = h.batch(m)
                        for j in range(2):
                            for var in range(2):
                                rows = slice(32 * (2 * j + var), 32 * (2 * j + var) + 32)
                                for i, (c, w_pair) in enumerate(h.products(m)):
                                    at = c * 256 + (b % 4) * S
                                    last = mm(ps[rows, 4 + full % 2, at:at + S], v[:, b % h.batches, c, j, var, w_pair, :],
                                              probsT[:, m % 2, (2 * i + j) * P + var * S:(2 * i + j) * P + (var + 1) * S],
                                              w_pair == 0, w_pair == h.pairs - 1)
                        last.then_inc(z["av"], 1)
                weights(wo_part)
                pe.wait_ge(z["out_lo"], B // 4)
                pe.wait_ge(z["sub"], h.steps)
                pe.wait_ge(z["probsT"], h.steps)
                for t in range(NT):
                    cols = slice(t * P, (t + 1) * P)
                    for c in range(KC):
                        r = w(wo_slot, wo_at + c * D, wo_at + (c + 1) * D)
                        last = mm3(y_of(blk, t), nT_hi[:, c, cols], nT_lo[:, c, cols], *r, c == 0 and t % 2 == 0, c == 1)
                    if t % 2:
                        last.then_inc(y_full, 1)

            def values(bank, slot, at, hi, lo, chunks, i, half):
                for j in range(2):
                    tokens = slice((half * 4 + 2 * i + j) * P, (half * 4 + 2 * i + j + 1) * P)
                    for k in range(chunks):
                        last = mm3(ps[:, bank, j * D:(j + 1) * D], hi(k)[:, tokens], lo(k)[:, tokens],
                                   *w(slot, at + k * D, at + (k + 1) * D), k == 0 and j == 0, k == chunks - 1)
                return last

            pe.wait_ge(ident_in, 16)
            n = 0
            for half in range(2):
                if half == 0:
                    transposes(0, FIRST)
                pe.wait_ge(nT_done, half * 4 + 4)
                for kind, i, _ in USES_A[6 * half:6 * half + 6]:
                    if n == 4:
                        transposes(0, SECOND)
                    weights(BLOCK["a_vo"] if kind == "v" else BLOCK["a_qk"])
                    if n >= 4:
                        pe.wait_ge(*use_done(USES_A, n - 4))
                    bank = PROJ_BANK[n % 4]
                    if kind == "v":
                        last = values(bank, 1, 0, lambda k: nT_hi[:, k], lambda k: nT_lo[:, k], KC, i, half)
                    else:
                        last = feature_major(ps[:, bank, :], 0, 0 if kind == "q" else 512, D, i, half)
                    last.then_inc(a_mm, 1)
                    n += 1
            for read in (a_q, a_k, a_v):
                pe.wait_ge(read, 4)
            narrow_heads(HA, 0, 1, 512, BLOCK["a_vo"])

            transposes(1, FIRST)
            pe.wait_ge(nT_done, NT + 4)
            pe.wait_ge(sined, 1)
            for i in range(4):
                half, table = divmod(i, 2)
                for j in range(PAIRS):
                    last = pe.transpose(ps[:, 4 + i, j * P:(j + 1) * P],
                                        sines[:, half * PAIRS + j, table, :], ident[:])
                last.then_inc(trig_tr, 1)
            transposes(1, SECOND)
            weights(BLOCK["ctx"])
            weights(BLOCK["b_kv"])

            def project_b(half):
                first = half * len(USES_B) // 2
                for n in range(first, first + len(USES_B) // 2):
                    kind, i, _ = USES_B[n]
                    in_half = n - first
                    if half == 0 and in_half < 4:
                        pe.wait_ge(trig_out, in_half + 1)
                    elif half == 0 and in_half < 8:
                        pe.wait_ge(nT_done, 2 * NT)
                    elif half and in_half < 2:
                        pe.wait_ge(*use_done(USES_B, n - 2))
                    else:
                        pe.wait_ge(*use_done(USES_B, n - (6 if half == 0 else 4)))
                    if half and in_half == 2:
                        pe.wait_ge(hs["b"]["sub"], HB.steps // 2)
                    bank, cols = b_bank(n), slice(half * HALF, (half + 1) * HALF)
                    if kind == "v":
                        last = values(bank, 3, 512, lambda k: ctx_hi, lambda k: ctx_lo, 1, i, half)
                    elif kind in ("k", "kr"):
                        lo = (D if kind == "kr" else 0) + i * P
                        last = mm3(ps[:, bank, :], *w(3, lo, lo + P), ctx_hi[:, cols], ctx_lo[:, cols], True, True)
                    else:
                        last = feature_major(ps[:, bank, :], 2, 512 if kind == "qr" else 0, D, i, half)
                    last.then_inc(b_mm, 1)
                pe.wait_ge(b_k, 2 * half + 2)
                pe.wait_ge(b_var, 2 * half + 2)

            project_b(0)
            narrow_heads(HB, 1, 4, 0, BLOCK["b_o"], lambda: project_b(1))

            weights(BLOCK["c_router_down"])
            for half, tiles in enumerate((FIRST, SECOND)):
                transposes(2, tiles)
                pe.wait_ge(nT_done, 2 * NT + 4 * (half + 1))
                cols = slice(half * HALF, (half + 1) * HALF)
                for k in range(KC):
                    last = mm3(ps[:, 4 + half, :], *w(5, k * P, (k + 1) * P), nT_hi[:, k, cols], nT_lo[:, k, cols],
                               k == 0, k == KC - 1)
                last.then_inc(c_logit, 1)
            for t in range(NT):
                pe.wait_ge(c_logit_out, t // 4 + 1)
                last = pe.transpose(ps[:, 6 + t // 4, (t % 4) * P:(t % 4 + 1) * P], coefT[:, t * P:(t + 1) * P], ident[:])
                if t % 4 == 3:
                    last.then_inc(c_router, 1)
            c_reader = {"gate": lambda s: (c_silued, s + 1), "up": lambda s: (c_m1, s + 1), "coef": lambda s: (c_m2, s - 3)}
            for n, (kind, s) in enumerate(USES_C):
                k_mix, half = (s - 4) // 2, s % 2
                if s < 4:
                    slot, at = 0, 512 * (s // 2)
                    weights(BLOCK["c_shared"])
                else:
                    slot, at = 1 + k_mix // 2, 512 * (k_mix % 2)
                    weights(BLOCK["c_mix0"] + k_mix // 2)
                if kind == "coef":
                    if s == 4:
                        for t in range(NT):
                            if t % 4 == 0:
                                pe.wait_ge(c_coef, t // 4 + 1)
                            last = pe.transpose(ps[:, 4 + t // 4, (t % 4) * P:(t % 4 + 1) * P], r_pick[:, t, :], ident[:])
                            if t % 4 == 3:
                                last.then_inc(c_coefT, 1)
                    pe.wait_ge(c_coef_out, half + 1)
                    pe.wait_ge(consts, 1)
                if n >= 4:
                    before, s_before = USES_C[n - 4]
                    pe.wait_ge(*c_reader[before](s_before))
                bank = ps[:, n % 4, :]
                if kind == "gate":
                    feature_major(bank, slot, at, P, 0, half).then_inc(c_gate, 1)
                elif kind == "up":
                    feature_major(bank, slot, at + D, P, 0, half).then_inc(c_up, 1)
                else:
                    mm(bank, mix_rows[:, k_mix, :], coefT[:, half * HALF:(half + 1) * HALF], True, True).then_inc(c_cb, 1)
            pe.wait_ge(c_lo, 4)
            for t in range(NT):
                cols = slice(t * P, (t + 1) * P)
                for j in range(2):
                    mm3(y_of(2, t), sh_hi[:, j, cols], sh_lo[:, j, cols],
                        *w(5, 256 + j * D, 256 + (j + 1) * D), j == 0 and t % 2 == 0, False)
            for t in range(NT):
                pe.wait_ge(c_lo, 5 + t // 4)
                cols = slice(t * P, (t + 1) * P)
                last = mm3(y_of(2, t), basis_hi[:, cols], basis_lo[:, cols], *w(5, 768, 1024), False, True)
                if t % 2:
                    last.then_inc(y_full, 1)

            transposes(3, FIRST)
            pe.wait_ge(nT_done, 3 * NT + 4)

            def step_d(s, u):
                half, hp = u % 2, u // 2
                base = 0 if u % 2 == 0 else 2
                if has(s, 0, STEPS_D):
                    if half == 0:
                        pe.wait_ge(w_lo_done, PART_D + s + 1)
                    at_least(pe, d_cs_out, 2 * s - 3)
                    feature_major(ps[:, base, :], hp, 0, P, 0, half).then_inc(d_qk, 1)
                    at_least(pe, d_cs_out, 2 * s - 2)
                    feature_major(ps[:, base + 1, :], hp, 256, P, 0, half).then_inc(d_qk, 1)
                if isinstance(s, int) and s == 0:
                    transposes(3, SECOND)
                    pe.wait_ge(nT_done, 4 * NT)
                if has(s, 2, STEPS_D):
                    o_head = ((u - 2) % 4) // 2
                    pe.wait_ge(d_vlod, s - 1)
                    if half == 0:
                        pe.wait_ge(w_lo_done, PART_D + s)
                    for i in range(PAIRS):
                        t = half * PAIRS + i
                        last = mm3(y_of(3, t), d_vhi[:, u % 2, i * P:(i + 1) * P], d_vlo[:, u % 2, i * P:(i + 1) * P],
                                   *w(o_head, 768, 1024), isinstance(s, int) and s < 4 and t % 2 == 0,
                                   isinstance(s, int) and s >= STEPS_D)
                        if isinstance(s, int) and s >= STEPS_D and i % 2:
                            last.then_inc(y_full, 1)
                    if not (isinstance(s, int) and s >= STEPS_D):
                        last.then_inc(d_o, 1)
                if has(s, 1, STEPS_D):
                    pe.wait_ge(d_plod, s)
                    p_half, p_head, p_buf = (u + 1) % 2, ((u - 1) % 4) // 2, (u - 1) % 2
                    at_least(pe, d_vd, s - 1)
                    for par in range(2):
                        rows = slice(64 * par, 64 * par + 64)
                        sums = ps[:, (base + 2 + par) % 4, 0:256]
                        mm(sums, ones_r[rows, :], d_phi[rows, p_buf, :], True, False)
                        last = mm(sums, ones_r[rows, :], d_plo[rows, p_buf, :], False, True)
                    last.then_inc(d_csum, 1)
                if has(s, 0, STEPS_D):
                    pe.wait_ge(d_qk_out, 2 * s + 2)
                    buf = u % 2
                    for i in range(PAIRS):
                        pair = slice(i * P, (i + 1) * P)
                        last = mm(ps[:, base + 1, pair], dq[:, buf, pair], dk[:, buf, pair], True, True)
                    last.then_inc(d_score, 1)
                if has(s, 1, STEPS_D):
                    feature_major(ps[:, base, :], p_head, 512, P, 0, p_half).then_inc(d_v, 1)

            steps(pe, STEPS_D, 4, 2, step_d)

            pe.wait_ge(e_v_split, 2)
            pe.wait_ge(d_vd, STEPS_D)
            def values_e(part):
                for n in part:
                    t, i = n // 2, n % 2
                    if n >= 4:
                        pe.wait_ge(e_v_all, n - 3)
                    tokens = slice(t * P, (t + 1) * P)
                    mm3(ps[:, n % 4, :], ctx_hi[:, tokens], ctx_lo[:, tokens], *w(4, i * 512, (i + 1) * 512),
                        True, True).then_inc(e_v_mm, 1)

            values_e(range(NT))
            pe.wait_ge(e_v_all, NT)
            transposes(4, FIRST)
            pe.wait_ge(nT_done, 4 * NT + 4)
            values_e(range(NT, 2 * NT))
            transposes(4, SECOND)
            pe.wait_ge(e_v_all, 2 * NT)

            def out_e(s, u, part):
                half, buf, o_slot = u % 2, u % 2, 2 + ((u - 2) % 4) // 2
                final = isinstance(s, int) and s >= STEPS_E
                for i in part:
                    t = half * PAIRS + i
                    for j in range(2):
                        last = mm3(y_of(4, t), ea_hi[:, buf, j, i * P:(i + 1) * P], ea_lo[:, buf, j, i * P:(i + 1) * P],
                                   *w(o_slot, 640 + j * D, 640 + (j + 1) * D),
                                   isinstance(s, int) and s < 4 and t % 2 == 0 and j == 0, final and j == 1)
                    if final and i % 2:
                        last.then_inc(y_full, 1)
                if not final and 3 in part:
                    last.then_inc(e_o, 1)

            def step_e(s, u):
                half, slot, buf = u % 2, 2 + u // 2, u % 2
                prev = (u - 1) % 2
                if has(s, 0, STEPS_E):
                    if half == 0:
                        pe.wait_ge(w_lo_done, PART_E + s + 1)
                    at_least(pe, e_pT_out, s - 1)
                    feature_major(ps[:, 0, :], slot, 0, P, 0, half).then_inc(e_q, 1)
                    at_least(pe, e_alo, 2 * s - 3)
                    feature_major(ps[:, 1, :], slot, 256, P, 0, half).then_inc(e_q, 1)
                    at_least(pe, e_alo, 2 * s - 2)
                    cols = slice(half * HALF, (half + 1) * HALF)
                    mm3(ps[:, 2, :], *w(slot, 512, 640), ctx_hi[:, cols], ctx_lo[:, cols], True, True).then_inc(e_q, 1)
                if isinstance(s, int) and s == 0:
                    pe.wait_ge(nT_done, 5 * NT)
                if has(s, 1, STEPS_E):
                    if has(s, 0, STEPS_E):
                        pe.wait_ge(e_qk_out, 3 * s + 1)
                    else:
                        pe.wait_ge(e_pT_out, s - 1)
                    pe.wait_ge(e_pd, s)
                    for i in range(PAIRS):
                        last = pe.transpose(ps[:, 0, i * P:(i + 1) * P], e_p[:, prev, i * P:(i + 1) * P], ident[:])
                    last.then_inc(e_tr, 1)
                if has(s, 2, STEPS_E):
                    pe.wait_ge(e_alo, 2 * s - 2)
                    if half == 0:
                        pe.wait_ge(w_lo_done, PART_E + s)
                    out_e(s, u, (0, 1))
                if has(s, 0, STEPS_E):
                    pe.wait_ge(e_qk_out, 3 * s + 3)
                    at_least(pe, e_masked, s)
                    for b in reversed(range(8)):
                        keys = slice(max(b - 1, 0) * S, (b + 1) * S)
                        last = mm(ps[:, 3, keys], eq[:, buf, b, :], ek[:, buf, keys], True, True)
                    last.then_inc(e_score, 1)
                if has(s, 1, STEPS_E):
                    if not has(s, 0, STEPS_E):
                        pe.wait_ge(e_alo, 2 * s - 2)
                    pe.wait_ge(e_pT_out, s)
                    pe.wait_ge(e_v_out, s)
                    for par in range(2):
                        rows = slice(64 * par, 64 * par + 64)
                        for i in range(PAIRS):
                            last = mm(ps[:, 1 + par, i * P:(i + 1) * P], ev[rows, prev, i * P:(i + 1) * P],
                                      e_pT[rows, i * P:(i + 1) * P], True, True)
                        last.then_inc(e_av, 1)
                if has(s, 2, STEPS_E):
                    out_e(s, u, (2, 3))

            steps(pe, STEPS_E, 4, 2, step_e)

            transposes(5, FIRST)
            pe.wait_ge(gate_split, 2)
            for half in range(2):
                pe.wait_ge(nT_done, 5 * NT + 4 * (half + 1))
                cols = slice(half * HALF, (half + 1) * HALF)
                for k in range(KC):
                    last = mm3(ps[0:E_MOE, half, :], gate_hi[:, k * E_MOE:(k + 1) * E_MOE], gate_lo[:, k * E_MOE:(k + 1) * E_MOE],
                               nT_hi[:, k, cols], nT_lo[:, k, cols], k == 0, k == KC - 1)
                last.then_inc(f_gate, 1)
                if half == 0:
                    transposes(5, SECOND)
            for t in range(NT):
                pe.wait_ge(f_gate_out, t // 4 + 1)
                last = pe.transpose(ps[:, 2, t * E_MOE:(t + 1) * E_MOE], gateT[:, t * P:(t + 1) * P],
                                    ident[0:E_MOE, 0:E_MOE])
            last.then_inc(f_gate, 1)

            def step_f(s, u):
                half, slot, buf = u % 2, 4 + u // 2, u % 2
                peeled = isinstance(s, int)
                if has(s, 0, STEPS_F):
                    if half == 0:
                        pe.wait_ge(w_lo_done, PART_F + s + 1)
                    if not (peeled and s == 1):
                        at_least(pe, f_m2, s - 1)
                        feature_major(ps[:, (3 * u) % 4, :], slot, 0, P, 0, half).then_inc(f_h1, 1)
                if has(s, 2, STEPS_F):
                    d_slot = 4 + ((u - 2) % 4) // 2
                    pe.wait_ge(f_glo, s - 1)
                    if half == 0:
                        pe.wait_ge(w_lo_done, PART_F + s)
                    final = peeled and s >= STEPS_F
                    for i in range(PAIRS):
                        t = half * PAIRS + i
                        last = mm3(y_of(5, t), g_hi[:, buf, i * P:(i + 1) * P], g_lo[:, buf, i * P:(i + 1) * P],
                                   *w(d_slot, 512, 768), peeled and s < 4 and t % 2 == 0, final)
                        if final and i % 2:
                            last.then_inc(y_full, 1)
                    if not final:
                        last.then_inc(f_down, 1)
                if has(s, 0, STEPS_F):
                    if not (peeled and s == 1):
                        at_least(pe, f_silued, s)
                        feature_major(ps[:, (3 * u + 1) % 4, :], slot, 256, P, 0, half).then_inc(f_h3, 1)
                    if peeled and s == 0:
                        pe.wait_ge(f_sig, 1)
                        feature_major(ps[:, 3, :], slot, 0, P, 0, 1).then_inc(f_h1, 1)
                        pe.wait_ge(f_silued, 1)
                        feature_major(ps[:, 0, :], slot, 256, P, 0, 1).then_inc(f_h3, 1)
                        for t in range(NT):
                            if t % 4 == 0:
                                pe.wait_ge(f_comb, 1)
                            last = pe.transpose(ps[0:96, 4 + t // 4, (t % 4) * P:(t % 4 + 1) * P], comb[:, t, :], ident[:])
                        last.then_inc(f_combT, 1)
                        pe.wait_ge(f_comb_out, 2)
                        pe.wait_ge(late_in, 32)
                    at_least(pe, f_m1, s)
                    chunk = (s // 2) if peeled else None
                    cols = slice(half * HALF, (half + 1) * HALF)
                    sel = select[:, chunk, :] if peeled else sel_view(s, u)
                    mm(ps[:, (3 * u + 2) % 4, :], sel, combT[:, cols], True, True).then_inc(f_cb, 1)

            def sel_view(s, u):
                return select[:, :, :].rearrange("p c m -> p (c m)")[:, bass.ds((s - u) * (P // 2) + (u // 2) * P, P)]

            steps(pe, STEPS_F, 4, 2, step_f)

        @block.scalar
        def _(act):
            def split_abc(name):
                n = BLOCK[name]
                _, slot, words = BLOCKS_ABC[n]
                act.wait_ge(w_in[n % STAGES], 16 * (n // STAGES + 1))
                dst = ctx_hi[:] if slot is None else w_hi[:, slot, 0:words]
                act.activation(dst, stage[:, n % STAGES, 0:words], ACT.Copy).then_inc(w_hi_done, 1)

            def round_nT(blk, tiles):
                for t in tiles:
                    act.wait_ge(ln_tr, blk * NT + t + 1)
                    act.activation(nT_hi[:, :, t * P:(t + 1) * P],
                                   ps[:, t_bank(blk, t), 0:D].rearrange("p (k n) -> p k n", k=KC),
                                   ACT.Copy).then_inc(nT_hi_done, 1)

            def narrow_heads(h, second_half=None):
                z = hs[h.name]
                scale = float(h.width) ** -0.5
                for n in range(h.steps + OUT_LAG):
                    if n == h.steps // 2 and second_half:
                        second_half()
                    m = n - TR_LAG
                    if 0 <= m < h.steps:
                        act.wait_ge(z["tr"], m + 1)
                        if m >= 2:
                            act.wait_ge(z["av"], m - 1)
                        act.activation(probsT[:, m % 2, :], ps[:, 2 + m % 2, :], ACT.Copy).then_inc(z["probsT"], 1)
                    if n < h.steps:
                        act.wait_ge(z["sub"], n + 1)
                        act.activation(probs[:, n % 4, :], probs[:, n % 4, :], ACT.Exp, scale=scale).then_inc(z["exp"], 1)
                    if h is HB and n == h.steps // 2 + AV_LAG - 1:
                        act.wait_ge(z["av"], h.steps // 2)
                        values_b(1)
                    m = n - OUT_LAG
                    if m >= 0 and (m + 1) % h.quad == 0:
                        i = m // h.quad
                        act.wait_ge(z["av"], m + 1)
                        act.activation(nT_hi[:, :, i * 256:(i + 1) * 256], ps[:, 4 + i % 2, :].rearrange("p (c n) -> p c n", c=KC),
                                       ACT.Copy).then_inc(z["out_hi"], 1)

            def diagonal(dst, src, **kwargs):
                for g in range(4):
                    rows = slice(32 * g, 32 * g + 32)
                    bias = {k: v[rows] for k, v in kwargs.items()}
                    last = act.activation(dst[rows, :, g, :], src[rows].rearrange("p (b k) -> p b k", k=S),
                                          ACT.Identity if bias else ACT.Copy, **bias)
                return last

            split_abc("a_qk")
            split_abc("a_vo")
            round_nT(0, FIRST)
            act.wait_ge(loaded, N_LOADED)
            split_abc("ctx")
            split_abc("b_q")
            for half in range(2):
                for c in range(KC):
                    n = 6 * half + 2 + c
                    act.wait_ge(a_mm, n + 1)
                    act.wait_ge(zeroed, 2)
                    diagonal(k_view(HA)[:, c, half * 8:half * 8 + 8], ps[:, PROJ_BANK[n % 4], :],
                             bias=bias_col[:, 2 + c:3 + c]).then_inc(a_k, 1)
                    if half == 0 and c == 0:
                        round_nT(0, SECOND)
                if half == 0:
                    for name in ("b_kv", "b_o", "c_router_down"):
                        split_abc(name)
            act.wait_ge(gate_in, 16)
            act.activation(gate_hi[:], gate_raw[:], ACT.Copy).then_inc(gate_split, 1)
            narrow_heads(HA)
            act.wait_ge(angles, 1)
            act.wait_ge(hs["a"]["score"], HA.steps)
            act.activation(sines.rearrange("p t c (r m) -> p (t c) r m", m=8),
                           angle[:].rearrange("p t c m -> p (t c) m").unsqueeze(2).to_broadcast([P, 2 * NT, P // 8, 8]),
                           ACT.Sin).then_inc(sined, 1)
            round_nT(1, FIRST)
            for i in range(4):
                half, table = divmod(i, 2)
                act.wait_ge(trig_tr, i + 1)
                act.activation((sin_t, cos_t)[table][:, half * HALF:(half + 1) * HALF], ps[:, 4 + i, :],
                               ACT.Copy).then_inc(trig_out, 1)
            round_nT(1, SECOND)

            def keys_b(half):
                for c in range(KC):
                    act.wait_ge(b_sum, 4 * half + c + 1)
                    if half:
                        act.wait_ge(hs["b"]["score"], HB.steps // 2)
                    diagonal(k_view(HB)[:, c], rot_sum[:, c, :]).then_inc(b_k, 1)

            def values_b(half):
                for i in range(2):
                    n = (half + 1) * len(USES_B) // 2 - 2 + i
                    act.wait_ge(b_mm, n + 1)
                    act.wait_ge(zeroed, 3)
                    for r in range(2):
                        for row in range(2):
                            for dst, src in zip(v_slots(HB, r, row, i), v_source(HB, b_bank(n), r, row)):
                                last = act.activation(dst, src, ACT.Copy)
                    last.then_inc(b_v, 1)

            keys_b(0)
            values_b(0)
            act.wait_ge(y_full, 4)
            split_abc("c_shared")
            split_abc("c_mix0")
            narrow_heads(HB, lambda: keys_b(1))
            for half, tiles in enumerate((FIRST, SECOND)):
                round_nT(2, tiles)
                act.wait_ge(c_logit, half + 1)
                act.activation(coefT[:, half * HALF:(half + 1) * HALF], ps[:, 4 + half, :], ACT.Copy).then_inc(c_logit_out, 1)
            act.wait_ge(b_mm, len(USES_B))
            split_abc("c_mix1")
            split_abc("c_mix2")
            act.wait_ge(y_full, 8)
            split_abc("c_mix3")
            for half in range(2):
                act.wait_ge(c_sub, half + 1)
                v = r_exp[:, half * 4:half * 4 + 4, :]
                act.activation(v, v, ACT.Exp).then_inc(c_exp, 1)
            for s in range(20):
                half = s % 2
                act.wait_ge(c_gate, s + 1)
                if s >= 2:
                    act.wait_ge(c_m1, s - 1)
                act.activation(c_silu[:, s % 2, :], c_bank("gate", s), ACT.Silu).then_inc(c_silued, 1)
                if 1 <= s <= 4:
                    j, h2 = divmod(s - 1, 2)
                    act.wait_ge(c_m1, s)
                    act.activation(sh_hi[:, j, h2 * HALF:(h2 + 1) * HALF], c_t1[:, (s - 1) % 2, :],
                                   ACT.Copy).then_inc(c_hi, 1)
                if s == 5:
                    for h2 in range(2):
                        act.wait_ge(c_coefT, h2 + 1)
                        act.activation(coefT[:, h2 * HALF:(h2 + 1) * HALF], ps[:, 4 + h2, :], ACT.Copy).then_inc(c_coef_out, 1)
            for half in range(2):
                act.wait_ge(c_acc, 13 + half)
                cols = slice(half * HALF, (half + 1) * HALF)
                act.activation(basis_hi[:, cols], basis[:, cols], ACT.Copy).then_inc(c_hi, 1)

            def split_next(s, u, count, q0, slot0, words, used):
                odd = u % 2
                if not has(s, 2 + odd, count - 4):
                    return
                if odd:
                    act.wait_ge(used, s - 1)
                stage_i = (u // 2 + 1) % 2
                act.wait_ge(wd_in[stage_i], 16 * (q0 // 2 + (u // 2 + 1) // 2 + 1) + 4 * (s - u))
                lo, hi = words[odd]
                slot = slot0 + stage_i
                act.activation(w_hi[:, slot, lo:hi], stage[:, stage_i, lo:hi], ACT.Copy).then_inc(w_hi_done, 1)

            def split_first(q, slot, words):
                act.wait_ge(wd_in[q % 2], 16 * (q // 2 + 1))
                for lo, hi in words:
                    act.activation(w_hi[:, slot, lo:hi], stage[:, q % 2, lo:hi], ACT.Copy).then_inc(w_hi_done, 1)

            act.wait_ge(c_up, 8)
            for q in range(2):
                split_first(q, q, WORDS_D)
            round_nT(3, FIRST)
            act.wait_ge(e_v_in, 16)
            act.wait_ge(y_full, 4 * 3)
            act.activation(w_hi[:, 4, 0:T], stage[:, 2, 0:T], ACT.Copy).then_inc(e_v_split, 1)

            def step_d(s, u):
                buf = u % 2
                base = 2 * (u % 2)
                prev = (u - 1) % 2

                def copy_qk(i, dst):
                    act.wait_ge(d_qk, 2 * s + i + 1)
                    at_least(act, d_score, s - 1)
                    act.activation(dst[:, buf, :], ps[:, base + i, :], ACT.Copy).then_inc(d_qk_out, 1)

                if has(s, 0, STEPS_D):
                    copy_qk(0, dq)
                if has(s, 1, STEPS_D):
                    act.wait_ge(d_pd, s)
                    at_least(act, d_csum, s - 2)
                    act.activation(d_phi[:, prev, :], d_p[:, prev, :], ACT.Copy).then_inc(d_phid, 1)
                if has(s, 0, STEPS_D):
                    copy_qk(1, dk)
                if isinstance(s, int) and s == 0:
                    round_nT(3, SECOND)
                if has(s, 1, STEPS_D):
                    act.wait_ge(d_csum, s)
                    at_least(act, d_vd, s - 2)
                    cs = d_cs[:, prev, :].rearrange("p (i r k) -> p r i k", r=2, k=S)
                    for par in range(2):
                        act.activation(cs[:, par], ps[:, (base + 2 + par) % 4, 0:256].rearrange("p (i k) -> p i k", k=S),
                                       ACT.Copy).then_inc(d_cs_out, 1)
                if has(s, 0, STEPS_D):
                    act.wait_ge(d_subbed, s + 1)
                    act.activation(d_p[:, buf, :], d_p[:, buf, :], ACT.Exp, scale=float(P) ** -0.5).then_inc(d_exped, 1)
                if has(s, 1, STEPS_D):
                    act.wait_ge(d_vd, s)
                    at_least(act, d_o, s - 2)
                    act.activation(d_vhi[:, prev, :], d_val[:, prev, :], ACT.Copy).then_inc(d_vhid, 1)
                split_next(s, u, STEPS_D, 0, 0, WORDS_D, d_o)
                if isinstance(s, int) and s >= STEPS_D - 2 and s < STEPS_D:
                    q = HEADS_D + s - STEPS_D + 2
                    split_first(q, 2 + q % 2, WORDS_E)

            steps(act, STEPS_D, 4, 2, step_d, peel_last=True)

            act.wait_ge(y_full, 4 * 4)
            by_group = v_all[:].rearrange("p (g t f) -> p g t f", g=GROUPS_E, t=NT)

            def copy_values_e(part):
                for n in part:
                    t, i = n // 2, n % 2
                    act.wait_ge(e_v_mm, n + 1)
                    act.activation(by_group[:, 4 * i:4 * i + 4, t, :], ps[:, n % 4, :].rearrange("p (g f) -> p g f", g=4),
                                   ACT.Copy).then_inc(e_v_all, 1)

            copy_values_e(range(NT))
            round_nT(4, FIRST)
            copy_values_e(range(NT, 2 * NT))
            round_nT(4, SECOND)

            def step_e(s, u):
                buf, prev = u % 2, (u - 1) % 2
                if has(s, 0, STEPS_E):
                    at_least(act, e_score, s - 1)
                    for j in range(2):
                        act.wait_ge(e_q, 3 * s + j + 1)
                        act.activation(eq[:, buf, :, j * S:(j + 1) * S], ps[:, j, :].rearrange("p (b n) -> p b n", b=8),
                                       ACT.Copy).then_inc(e_qk_out, 1)
                    act.wait_ge(e_q, 3 * s + 3)
                    act.activation(ek[:, buf, :], ps[:, 2, :], ACT.Copy).then_inc(e_qk_out, 1)
                if has(s, 1, STEPS_E):
                    act.wait_ge(e_tr, s)
                    at_least(act, e_av, 2 * s - 2)
                    act.activation(e_pT[:], ps[:, 0, :], ACT.Copy).then_inc(e_pT_out, 1)
                if u % 2 == 0:
                    split_next(s, u, STEPS_E, HEADS_D, 2, WORDS_E, e_o)
                if has(s, 1, STEPS_E):
                    at_least(act, e_o, s - 2)
                    for par in range(2):
                        act.wait_ge(e_av, 2 * s - 1 + par)
                        act.activation(ea_view(ea_hi, prev, par), ps[:, 1 + par, :].rearrange("p (i j q) -> p i j q", j=2, q=S),
                                       ACT.Copy).then_inc(e_ahi, 1)
                if has(s, 0, STEPS_E):
                    act.wait_ge(e_subbed, s + 1)
                    act.activation(e_p[:, buf, :], e_p[:, buf, :], ACT.Exp, scale=float(P) ** -0.5).then_inc(e_exped, 1)
                if u % 2:
                    split_next(s, u, STEPS_E, HEADS_D, 2, WORDS_E, e_o)
                if isinstance(s, int) and s >= STEPS_E - 2 and s < STEPS_E:
                    q = HEADS_D + GROUPS_E + s - STEPS_E + 2
                    split_first(q, 4 + q % 2, WORDS_F)

            steps(act, STEPS_E, 4, 2, step_e, peel_last=True)

            round_nT(5, FIRST)
            for half in range(2):
                act.wait_ge(f_gate, half + 1)
                act.activation(gateT[:, half * HALF:(half + 1) * HALF], ps[0:E_MOE, half, :], ACT.Copy).then_inc(f_gate_out, 1)
                if half == 0:
                    round_nT(5, SECOND)
            act.wait_ge(f_gate, 3)
            act.activation(g_score[:].rearrange("p t e -> p (t e)"), ps[:, 2, 0:NT * E_MOE], ACT.Sigmoid).then_inc(f_sig, 1)

            def step_f(s, u):
                buf, prev = u % 2, (u - 1) % 2
                if has(s, 0, STEPS_F):
                    act.wait_ge(f_h1, s + 1)
                    at_least(act, f_m1, s - 1)
                    act.activation(f_silu[:, buf, :], ps[:, (3 * u) % 4, :], ACT.Silu).then_inc(f_silued, 1)
                if has(s, 1, STEPS_F):
                    act.wait_ge(f_m2, s)
                    at_least(act, f_down, s - 2)
                    act.activation(g_hi[:, prev, :], f_t2[:, prev, :], ACT.Copy).then_inc(f_ghi, 1)
                if isinstance(s, int) and s == 0:
                    for half in range(2):
                        act.wait_ge(f_combT, 1)
                        act.activation(combT[:, half * HALF:(half + 1) * HALF], ps[0:96, 4 + half, :],
                                       ACT.Copy).then_inc(f_comb_out, 1)
                split_next(s, u, STEPS_F, HEADS_D + GROUPS_E, 4, WORDS_F, f_down)

            steps(act, STEPS_F, 4, 2, step_f)

        @block.gpsimd
        def _(pool):
            def sub_lo(part, stage_i, lo, hi, dst, src_hi):
                pool.wait_ge(w_hi_done, part + 1)
                pool.tensor_tensor(dst, stage[:, stage_i, lo:hi], f32(src_hi), ALU.subtract).then_inc(w_lo_done, 1)

            def sub_slot(part, slot, lo, hi, stage_i):
                sub_lo(part, stage_i, lo, hi, w_lo[:, slot, lo:hi], w_hi[:, slot, lo:hi])

            def sub_abc(name):
                n = BLOCK[name]
                _, slot, words = BLOCKS_ABC[n]
                if slot is None:
                    sub_lo(n, n % STAGES, 0, words, ctx_lo[:], ctx_hi[:])
                else:
                    sub_slot(n, slot, 0, words, n % STAGES)

            pool.memset(k_diag[:], 0.0).then_inc(zeroed, 1)
            sub_abc("a_qk")
            sub_abc("a_vo")
            pool.memset(v_diag[:], 0.0).then_inc(zeroed, 1)
            for name in ("ctx", "b_q", "b_kv", "b_o", "c_router_down"):
                sub_abc(name)
            pool.wait_ge(gate_split, 1)
            pool.tensor_tensor(gate_lo[:], gate_raw[:], f32(gate_hi[:]), ALU.subtract).then_inc(gate_split, 1)

            def add_bias(blk, row):
                pool.wait_ge(normed_done, (blk + 1) * NT)
                pool.wait_ge(loaded, N_LOADED)
                bias = bias_rows[:, row:row + 1, :].to_broadcast([P, NT, D])
                pool.tensor_tensor(x[:], x[:], bias, ALU.add).then_inc(pool_x, 1)

            def narrow_heads(h, second_half=None):
                z = hs[h.name]
                for n in range(h.steps):
                    if n == h.steps // 2 - 1 and second_half:
                        second_half()
                    p3 = probs[:, n % 4, :].rearrange("p (s k) -> p s k", k=S)
                    pool.wait_ge(z["rec"], n + 1)
                    pool.tensor_tensor(p3, p3, srec[:, n % 4, :].unsqueeze(2).to_broadcast([P, 8, S]),
                                       ALU.mult).then_inc(z["norm"], 1)

            add_bias(0, 1)
            narrow_heads(HA)
            pool.wait_ge(hs["a"]["av"], HA.steps)
            pool.memset(v_diag[:], 0.0).then_inc(zeroed, 1)
            add_bias(1, 2)

            def sums_b(half):
                for i in range(4 * half, 4 * half + 4):
                    pool.wait_ge(b_rot, 2 * i + 2)
                    if i >= 2:
                        pool.wait_ge(*((b_k, 2 * half + i % 4 - 1) if i % 4 >= 2 else (b_var, 2 * half - 1 + i % 4)))
                    pool.tensor_tensor(rot_sum[:, i % 2, :], rotated(i)[:, 0, :], rotated(i)[:, 1, :], ALU.add).then_inc(b_sum, 1)

            sums_b(0)
            narrow_heads(HB, lambda: sums_b(1))
            sub_abc("c_shared")
            sub_abc("c_mix0")
            sub_abc("c_mix1")
            sub_abc("c_mix2")
            sub_abc("c_mix3")
            for s in range(20):
                half = s % 2
                cols = slice(half * HALF, (half + 1) * HALF)
                if s < 4:
                    j = s // 2
                    pool.wait_ge(c_hi, s + 1)
                    pool.tensor_tensor(sh_lo[:, j, cols], c_t1[:, s % 2, :], f32(sh_hi[:, j, cols]),
                                       ALU.subtract).then_inc(c_lo, 1)
                elif s >= 6:
                    pool.wait_ge(c_m2, s - 3)
                    if s >= 8:
                        pool.wait_ge(c_acc, s - 7)
                    pool.tensor_tensor(basis[:, cols], basis[:, cols], c_t2[:, s % 2, :], ALU.add).then_inc(c_acc, 1)
            for half in range(2):
                cols = slice(half * HALF, (half + 1) * HALF)
                pool.wait_ge(c_hi, 5 + half)
                pool.tensor_tensor(basis_lo[:, cols], basis[:, cols], f32(basis_hi[:, cols]), ALU.subtract).then_inc(c_lo, 1)

            def sub_next(s, u, count, part0, slot0, words):
                odd = u % 2
                if not has(s, 2 + odd, count - 4):
                    return
                stage_i = (u // 2 + 1) % 2
                sub_slot(part0 + s + 2, slot0 + stage_i, *words[odd], stage_i)

            def sub_first(q, slot, words):
                for i, (lo, hi) in enumerate(words):
                    sub_slot(PART_D + 2 * q + i, slot, lo, hi, q % 2)

            for q in range(2):
                sub_first(q, q, WORDS_D)
            pool.wait_ge(e_v_split, 1)
            pool.tensor_tensor(w_lo[:, 4, 0:T], stage[:, 2, 0:T], f32(w_hi[:, 4, 0:T]), ALU.subtract).then_inc(e_v_split, 1)

            def step_d(s, u):
                sub_next(s, u, STEPS_D, PART_D, 0, WORDS_D)
                if isinstance(s, int) and STEPS_D - 2 <= s < STEPS_D:
                    q = HEADS_D + s - STEPS_D + 2
                    sub_first(q, 2 + q % 2, WORDS_E)

            steps(pool, STEPS_D, 4, 0, step_d, peel_last=True)

            pool.wait_ge(e_v_all, 2 * NT)

            def step_e(s, u):
                if has(s, 0, STEPS_E):
                    at_least(pool, e_av, 2 * s - 2)
                    here = slice(s * 512, (s + 1) * 512) if isinstance(s, int) else bass.ds(s * 512, 512)
                    pool.tensor_copy(ev[:, u % 2, :], v_all[:, here]).then_inc(e_v_out, 1)
                sub_next(s, u, STEPS_E, PART_E, 2, WORDS_E)
                if isinstance(s, int) and STEPS_E - 2 <= s < STEPS_E:
                    q = HEADS_D + GROUPS_E + s - STEPS_E + 2
                    sub_first(q, 4 + q % 2, WORDS_F)

            steps(pool, STEPS_E, 4, 0, step_e, peel_last=True)

            def step_f(s, u):
                prev = (u - 1) % 2
                if has(s, 1, STEPS_F):
                    pool.wait_ge(f_ghi, s)
                    pool.tensor_tensor(g_lo[:, prev, :], f_t2[:, prev, :], f32(g_hi[:, prev, :]),
                                       ALU.subtract).then_inc(f_glo, 1)
                sub_next(s, u, STEPS_F, PART_F, 4, WORDS_F)

            steps(pool, STEPS_F, 4, 2, step_f)

        @block.vector
        def _(ve):
            chained = 0

            def small(instruction):
                nonlocal chained
                instruction.then_inc(ln_chain, 1)
                chained += 1
                ve.wait_ge(ln_chain, chained)

            def add_output(blk, tiles):
                for t in tiles:
                    ve.wait_ge(y_full, 4 * blk + t // 2 + 1)
                    if blk < 2:
                        ve.wait_ge(pool_x, blk + 1)
                    ve.tensor_tensor(x[:, t, :], x[:, t, :], y_of(blk, t), ALU.add).then_inc(resid, 1)

            def layernorm(blk, tiles):
                four = slice(tiles[0], tiles[0] + 4)
                for t in tiles:
                    if blk:
                        ve.wait_ge(resid, (blk - 1) * NT + t + 1)
                    last = ve.bn_stats(stats[:, t, :], x[:, t, :])
                small(last)
                for t in tiles:
                    last = ve.bn_aggr(mean_var[:, t, :], stats[:, t, :])
                small(last)
                v, y, a = var[:, four], rstd[:, four], newton[:, four]
                small(ve.tensor_scalar(v, mean_var[:, four, 1], EPS_LN, None, ALU.add))
                small(ve.tensor_scalar(y.bitcast(I32), v.bitcast(I32), 1, None, ALU.logical_shift_right))
                small(ve.tensor_scalar(y.bitcast(I32), y.bitcast(I32), -1.0, RSQRT_SEED, ALU.mult, ALU.add))
                for _ in range(3):
                    small(ve.tensor_tensor(a, y, y, ALU.mult))
                    small(ve.scalar_tensor_tensor(out=a, in0=a, scalar=-0.5, in1=v, op0=ALU.mult, op1=ALU.mult))
                    small(ve.scalar_tensor_tensor(out=y, in0=a, scalar=1.5, in1=y, op0=ALU.add, op1=ALU.mult))
                for t in tiles:
                    ve.tensor_scalar(normed[:, t, :], x[:, t, :], mean_var[:, t, 0:1], rstd[:, t:t + 1],
                                     ALU.subtract, ALU.mult).then_inc(normed_done, 1)

            def lo_nT(blk, tiles):
                for t in tiles:
                    ve.wait_ge(nT_hi_done, blk * NT + t + 1)
                    cols = slice(t * P, (t + 1) * P)
                    ve.tensor_tensor(nT_lo[:, :, cols], ps[:, t_bank(blk, t), 0:D].rearrange("p (k n) -> p k n", k=KC),
                                     f32(nT_hi[:, :, cols]), ALU.subtract).then_inc(nT_done, 1)

            def next_block(blk, between=None):
                if blk:
                    add_output(blk - 1, FIRST)
                layernorm(blk, FIRST)
                if blk:
                    add_output(blk - 1, SECOND)
                lo_nT(blk, FIRST)
                layernorm(blk, SECOND)
                if between:
                    between()
                lo_nT(blk, SECOND)

            def bcast(ap, shape):
                return ap.unsqueeze(len(ap.shape)).to_broadcast(shape)

            def narrow_heads(h, second_half=None):
                z = hs[h.name]
                for n in range(h.steps + OUT_LAG + 1):
                    if n == h.steps // 2 and second_half:
                        second_half()
                    if n < h.steps:
                        s3 = ps[:, n % 2, :].rearrange("p (s k) -> p s k", k=S)
                        ve.wait_ge(z["score"], n + 1)
                        ve.tensor_reduce(smax[:, n % 4, :], s3, AX_X, ALU.max).then_inc(z["max"], 1)
                    m = n - 1
                    if 0 <= m < h.steps:
                        ve.wait_ge(z["exp"], m + 1)
                        ve.tensor_reduce(ssum[:, m % 4, :], probs[:, m % 4, :].rearrange("p (s k) -> p s k", k=S),
                                         AX_X, ALU.add).then_inc(z["sum"], 1)
                    if n < h.steps:
                        ve.wait_ge(z["max"], n + 1)
                        if n >= 4:
                            ve.wait_ge(z["tr"], n - 3)
                        ve.tensor_tensor(probs[:, n % 4, :].rearrange("p (s k) -> p s k", k=S), s3,
                                         bcast(smax[:, n % 4, :], [P, 8, S]), ALU.subtract).then_inc(z["sub"], 1)
                    if 0 <= m < h.steps:
                        ve.wait_ge(z["sum"], m + 1)
                        if m >= 4:
                            ve.wait_ge(z["norm"], m - 3)
                        ve.reciprocal(srec[:, m % 4, :], ssum[:, m % 4, :]).then_inc(z["rec"], 1)
                    m = n - OUT_LAG - 1
                    if m >= 0 and (m + 1) % h.quad == 0:
                        i = m // h.quad
                        ve.wait_ge(z["out_hi"], i + 1)
                        cols = slice(i * 256, (i + 1) * 256)
                        ve.tensor_tensor(nT_lo[:, :, cols], ps[:, 4 + i % 2, :].rearrange("p (c n) -> p c n", c=KC),
                                         f32(nT_hi[:, :, cols]), ALU.subtract).then_inc(z["out_lo"], 1)

            def rotary_angles():
                for axis in range(2):
                    f = slice(4 * axis, 4 * axis + 4)
                    last = ve.tensor_tensor(angle[:, :, :, f], freqs[:, :, f].unsqueeze(1).to_broadcast([P, NT, 2, 4]),
                                            pos[:, :, axis:axis + 1].unsqueeze(3).to_broadcast([P, NT, 2, 4]), ALU.mult)
                small(last)
                small(ve.tensor_scalar(angle[:, :, 1, :], angle[:, :, 1, :], PI / 2, None, ALU.add))
                small(ve.tensor_scalar(turn_count[:], angle[:], 1 / (2 * PI), ROUND, ALU.mult, ALU.add))
                small(ve.tensor_scalar(turn_count[:], turn_count[:], ROUND, None, ALU.subtract))
                for part in (TWO_PI_A, TWO_PI_B):
                    small(ve.scalar_tensor_tensor(out=angle[:], in0=turn_count[:], scalar=-part, in1=angle[:],
                                                  op0=ALU.mult, op1=ALU.add))
                ve.tensor_scalar(angle[:], angle[:], PI_BELOW, -PI_BELOW, ALU.min, ALU.max).then_inc(angles, 1)

            small(ve.memset(ones[:], 1.0))
            small(ve.tensor_copy(ones_r[:], ones[:]))
            for half in range(2):
                if half == 0:
                    ve.wait_ge(x_in[0], 16)
                    layernorm(0, FIRST)
                    lo_nT(0, FIRST)
                    ve.wait_ge(x_in[1], 16)
                    layernorm(0, SECOND)
                    ve.wait_ge(loaded, N_LOADED)
                    ve.wait_ge(zeroed, 2)
                for i in range(6):
                    kind, c, _ = USES_A[6 * half + i]
                    n = 6 * half + i
                    if kind == "k":
                        continue
                    if n == 4:
                        lo_nT(0, SECOND)
                    ve.wait_ge(a_mm, n + 1)
                    bank = PROJ_BANK[n % 4]
                    if kind == "q":
                        for v in range(HA.variants):
                            last = ve.tensor_scalar(q_view(HA)[:, c, half * 8:half * 8 + 8, v * S:(v + 1) * S],
                                                    ps[:, bank, :].rearrange("p (b q) -> p b q", q=S),
                                                    bias_col[:, c:c + 1], head_mask[:, v:v + 1], ALU.add, ALU.mult)
                        last.then_inc(a_q, 1)
                    else:
                        for r in range(2):
                            for row in range(2):
                                bias = bias_rows[64 * row:64 * row + 64, 0, r * P:(r + 1) * P].rearrange(
                                    "p (n m) -> p n m", m=16).unsqueeze(1).to_broadcast([64, 2, 8, 16])
                                last = ve.tensor_tensor(v_slots(HA, r, row, 2 * half + c)[0], v_source(HA, bank, r, row)[0],
                                                        bias, ALU.add)
                        last.then_inc(a_v, 1)
            rotary_angles()
            narrow_heads(HA)

            def rotate_b(half, pieces=None):
                cols = slice(half * HALF, (half + 1) * HALF)
                for i in pieces or range(4 * half, 4 * half + 4):
                    for turned in range(2):
                        n = half * len(USES_B) // 2 + 2 * (i % 4) + turned
                        ve.wait_ge(b_mm, n + 1)
                        if i >= 4:
                            ve.wait_ge(b_sum, i - 1)
                        ve.tensor_tensor(rotated(i)[:, turned, :], ps[:, b_bank(n), :],
                                         (sin_t if turned else cos_t)[:, cols], ALU.mult).then_inc(b_rot, 1)
                if pieces and 3 not in pieces:
                    return
                for c in range(KC):
                    ve.wait_ge(b_sum, 4 * half + 2 + c + 1)
                    if half:
                        ve.wait_ge(hs["b"]["score"], HB.steps // 2)
                    for v in range(HB.variants):
                        last = ve.tensor_scalar(q_view(HB)[:, c, :, v * S:(v + 1) * S],
                                                rot_sum[:, c, :].rearrange("p (b q) -> p b q", q=S),
                                                head_mask[:, 2 + v:3 + v], None, ALU.mult)
                    last.then_inc(b_var, 1)

            def rotate_first_keys():
                ve.wait_ge(trig_out, 4)
                rotate_b(0, (0, 1))

            next_block(1, rotate_first_keys)
            rotate_b(0, (2, 3))
            narrow_heads(HB, lambda: rotate_b(1))

            next_block(2)
            small(ve.tensor_tensor(amp_sq[:], amps[:], amps[:], ALU.mult))
            small(ve.tensor_reduce(mix[:], amp_sq[:], AX_X, ALU.add))
            small(ve.tensor_reduce(mix_sum[:, 0:1], mix[:], AX_X, ALU.add))
            small(ve.tensor_scalar(mix_sum[:, 0:1], mix_sum[:, 0:1], EPS_MIX, None, ALU.add))
            small(ve.reciprocal(mix_sum[:, 1:2], mix_sum[:, 0:1]))
            small(ve.tensor_scalar(mix[:], mix[:], mix_sum[:, 1:2], e_scale[:], ALU.mult, ALU.mult))
            ve.tensor_copy(mix_rows[:], bcast(mix[:], [P, K_MIX, P])).then_inc(consts, 1)

            def c_m1_step(s):
                ve.wait_ge(c_up, s + 1)
                ve.wait_ge(c_silued, s + 1)
                if 2 <= s < 6:
                    ve.wait_ge(c_lo, s - 1)
                if s >= 6:
                    ve.wait_ge(c_m2, s - 5)
                ve.tensor_tensor(c_t1[:, s % 2, :], c_silu[:, s % 2, :], c_bank("up", s), ALU.mult).then_inc(c_m1, 1)

            def c_m2_step(s):
                half = s % 2
                ve.wait_ge(c_m1, s + 1)
                ve.wait_ge(c_cb, s - 3)
                if s >= 8:
                    ve.wait_ge(c_acc, s - 7)
                dst = basis[:, half * HALF:(half + 1) * HALF] if s < 6 else c_t2[:, s % 2, :]
                ve.tensor_tensor(dst, c_t1[:, s % 2, :], c_bank("coef", s), ALU.mult).then_inc(c_m2, 1)

            logits = [ps[:, 6 + half, :].rearrange("p (t e) -> p t e", e=E_MIX) for half in range(2)]
            for t in range(NT):
                ve.wait_ge(c_router, t // 4 + 1)
                last = ve.max(top8[:, t, :], logits[t // 4][:, t % 4, :])
            small(last)
            for half in range(2):
                tiles = slice(half * 4, half * 4 + 4)
                ve.tensor_tensor(r_exp[:, tiles, :], logits[half], top8[:, tiles, 0:1].to_broadcast([P, 4, E_MIX]),
                                 ALU.subtract).then_inc(c_sub, 1)
            for t in range(NT):
                last = ve.max_index(top_idx[:, t, :], top8[:, t, :], logits[t // 4][:, t % 4, :])
            small(last)
            small(ve.tensor_copy(top_idx_f[:], top_idx[:]))
            c_m1_step(0)
            c_m1_step(1)
            for t in range(NT):
                last = ve.tensor_scalar(r_pick[:, t, :], iota[:], top_idx_f[:, t, 3:4], None, ALU.is_le)
            small(last)
            for op0, op1 in ((ALU.is_ge, ALU.mult), (ALU.is_gt, ALU.max)):
                for t in range(NT):
                    last = ve.scalar_tensor_tensor(out=r_pick[:, t, :], in0=logits[t // 4][:, t % 4, :],
                                                   scalar=top8[:, t, 3:4], in1=r_pick[:, t, :], op0=op0, op1=op1)
                small(last)
            c_m1_step(2)
            c_m1_step(3)
            ve.wait_ge(c_exp, 2)
            small(ve.tensor_reduce(z_all[:], r_exp[:], AX_X, ALU.add))
            small(ve.tensor_tensor(r_pick[:], r_pick[:], r_exp[:], ALU.mult))
            small(ve.tensor_reduce(z_top[:], r_pick[:], AX_X, ALU.add))
            small(ve.scalar_tensor_tensor(out=z_top[:], in0=z_all[:], scalar=EPS_MIX, in1=z_top[:], op0=ALU.mult, op1=ALU.add))
            small(ve.reciprocal(z_rec[:], z_top[:]))
            c_m1_step(4)
            c_m1_step(5)
            for half in range(2):
                tiles = slice(half * 4, half * 4 + 4)
                ve.tensor_tensor(r_pick[:, tiles, :], r_pick[:, tiles, :], bcast(z_rec[:, tiles], [P, 4, E_MIX]),
                                 ALU.mult).then_inc(c_coef, 1)
            for s in range(4, 20):
                if s >= 6:
                    c_m1_step(s)
                c_m2_step(s)

            next_block(3)

            def step_d(s, u):
                buf, prev, base = u % 2, (u - 1) % 2, 2 * (u % 2)
                if has(s, 0, STEPS_D):
                    p3 = d_p[:, buf, :].rearrange("p (i k) -> p i k", k=S)
                    ve.wait_ge(d_score, s + 1)
                    own = [(slice(64 * r, 64 * r + 64), ps[64 * r:64 * r + 64, base + 1, :].rearrange(
                        "p (i b k) -> p i b k", b=2, k=S)[:, :, r]) for r in range(2)]
                    for rows, scores in own:
                        last = ve.tensor_reduce(d_max[rows, buf, :], scores, AX_X, ALU.max)
                    last.then_inc(d_maxed, 1)
                    ve.wait_ge(d_maxed, s + 1)
                    for rows, scores in own:
                        last = ve.tensor_tensor(p3[rows], scores, bcast(d_max[rows, buf, :], [64, 4, S]), ALU.subtract)
                    last.then_inc(d_subbed, 1)
                if has(s, 1, STEPS_D):
                    ve.wait_ge(d_v, s)
                    ve.wait_ge(d_cs_out, 2 * s)
                    at_least(ve, d_vlod, s - 2)
                    ve.tensor_tensor(d_val[:, prev, :], ps[:, base, :], d_cs[:, prev, :], ALU.mult).then_inc(d_vd, 1)
                if has(s, 0, STEPS_D):
                    ve.wait_ge(d_exped, s + 1)
                    ve.tensor_reduce(d_sum[:, buf, :], p3, AX_X, ALU.add).then_inc(d_summed, 1)
                    ve.wait_ge(d_summed, s + 1)
                    ve.reciprocal(d_rec[:, buf, :], d_sum[:, buf, :]).then_inc(d_recd, 1)
                if has(s, 1, STEPS_D):
                    ve.wait_ge(d_vhid, s)
                    ve.tensor_tensor(d_vlo[:, prev, :], d_val[:, prev, :], f32(d_vhi[:, prev, :]),
                                     ALU.subtract).then_inc(d_vlod, 1)
                if has(s, 0, STEPS_D):
                    ve.wait_ge(d_recd, s + 1)
                    ve.tensor_tensor(p3, p3, bcast(d_rec[:, buf, :], [P, 4, S]), ALU.mult).then_inc(d_pd, 1)
                    ve.wait_ge(d_phid, s + 1)
                    at_least(ve, d_csum, s - 1)
                    ve.tensor_tensor(d_plo[:, buf, :], d_p[:, buf, :], f32(d_phi[:, buf, :]), ALU.subtract).then_inc(d_plod, 1)

            steps(ve, STEPS_D, 4, 1, step_d)

            next_block(4)
            ve.wait_ge(late_in, 16)
            small(ve.tensor_copy(mask_bias[:], mask_u8[:]))
            small(ve.tensor_reduce(any_key[:], mask_bias[:].rearrange("p (b k) -> p b k", k=S), AX_X, ALU.max))
            small(ve.tensor_scalar(mask_bias[:], mask_bias[:], -1.0, 1e30, ALU.add, ALU.mult))

            def step_e(s, u):
                half, buf, prev = u % 2, u % 2, (u - 1) % 2
                p3 = e_p[:, buf, :].rearrange("p (b k) -> p b k", k=S)
                if has(s, 0, STEPS_E):
                    ve.wait_ge(e_score, s + 1)
                    at_least(ve, e_tr, s - 1)
                    ve.tensor_tensor(e_p[:, buf, :], ps[:, 3, :], mask_bias[:, half * HALF:(half + 1) * HALF],
                                     ALU.add).then_inc(e_masked, 1)
                    ve.wait_ge(e_masked, s + 1)
                    ve.tensor_reduce(e_max[:, buf, :], p3, AX_X, ALU.max).then_inc(e_maxed, 1)
                    ve.wait_ge(e_maxed, s + 1)
                    ve.tensor_tensor(p3, p3, bcast(e_max[:, buf, :], [P, 8, S]), ALU.subtract).then_inc(e_subbed, 1)
                if has(s, 1, STEPS_E):
                    for par in range(2):
                        ve.wait_ge(e_ahi, 2 * s - 1 + par)
                        ve.tensor_tensor(ea_view(ea_lo, prev, par), ps[:, 1 + par, :].rearrange("p (i j q) -> p i j q", j=2, q=S),
                                         f32(ea_view(ea_hi, prev, par)), ALU.subtract).then_inc(e_alo, 1)
                if has(s, 0, STEPS_E):
                    ve.wait_ge(e_exped, s + 1)
                    ve.tensor_reduce(e_sum[:, buf, :], p3, AX_X, ALU.add).then_inc(e_summed, 1)
                    ve.wait_ge(e_summed, s + 1)
                    ve.reciprocal(e_rec[:, buf, :], e_sum[:, buf, :]).then_inc(e_recd, 1)
                    ve.wait_ge(e_recd, 2 * s + 1)
                    ve.tensor_tensor(e_rec[:, buf, :], e_rec[:, buf, :], any_key[:, half * 8:half * 8 + 8],
                                     ALU.mult).then_inc(e_recd, 1)
                    ve.wait_ge(e_recd, 2 * s + 2)
                    ve.tensor_tensor(p3, p3, bcast(e_rec[:, buf, :], [P, 8, S]), ALU.mult).then_inc(e_pd, 1)

            steps(ve, STEPS_E, 4, 1, step_e)

            next_block(5)
            small(ve.memset(comb[:], 0.0))
            ve.wait_ge(f_sig, 1)
            g4 = g_score[:].rearrange("p t (g e) -> p t g e", g=4)
            small(ve.tensor_reduce(g_top[:], g4, AX_X, ALU.max))
            top_i = g_top[:].unsqueeze(3).to_broadcast([P, NT, 4, 4])
            top_j = g_top[:].unsqueeze(2).to_broadcast([P, NT, 4, 4])
            small(ve.tensor_tensor(g_cmp[:], top_j, top_i, ALU.is_gt))
            small(ve.tensor_tensor(g_eq[:], top_j, top_i, ALU.is_equal))
            small(ve.tensor_tensor(g_eq[:], g_eq[:], lower[:].unsqueeze(1).to_broadcast([P, NT, 4, 4]), ALU.mult))
            small(ve.tensor_tensor(g_cmp[:], g_cmp[:], g_eq[:], ALU.add))
            small(ve.tensor_reduce(g_rank[:], g_cmp[:], AX_X, ALU.add))
            small(ve.tensor_scalar(g_rank[:], g_rank[:], 1.5, None, ALU.is_lt))
            small(ve.tensor_tensor(g_mask[:].rearrange("p t (g e) -> p t g e", g=4), g4,
                                   g_rank[:].unsqueeze(3).to_broadcast([P, NT, 4, 4]), ALU.mult))
            for t in range(NT):
                last = ve.max(g_top8[:, t, :], g_mask[:, t, :])
            small(last)
            for t in range(NT):
                last = ve.max_index(g_idx[:, t, :], g_top8[:, t, :], g_mask[:, t, :])
            small(last)
            small(ve.tensor_copy(g_idx_f[:], g_idx[:]))
            for j in range(TOPK):
                idx = g_idx_f[:, :, j:j + 1].to_broadcast([P, NT, E_MOE])
                ids = iota[:, 0:E_MOE].unsqueeze(1).to_broadcast([P, NT, E_MOE])
                if j == 0:
                    small(ve.tensor_tensor(g_pick[:], ids, idx, ALU.is_equal))
                else:
                    small(ve.tensor_tensor(g_mask[:], ids, idx, ALU.is_equal))
                    small(ve.tensor_tensor(g_pick[:], g_pick[:], g_mask[:], ALU.add))
            small(ve.tensor_tensor(g_pick[:], g_pick[:], g_score[:], ALU.mult))
            small(ve.tensor_reduce(g_sum[:], g_pick[:], AX_X, ALU.add))
            small(ve.reciprocal(g_rec[:], g_sum[:]))
            small(ve.tensor_tensor(g_pick[:], g_pick[:], bcast(g_rec[:], [P, NT, E_MOE]), ALU.mult))
            small(ve.memset(comb[:, :, E_MOE:E_MOE + 1], 1.0))
            for i in range(3):
                small(ve.tensor_copy(comb_b[:], g_pick[:]))
                last = ve.tensor_copy(comb[:, :, 32 * i:32 * i + E_MOE], comb_b[:])
                if i < 2:
                    small(last)
                    small(ve.tensor_tensor(g_pick[:], g_pick[:], comb[:, :, 32 * i:32 * i + E_MOE], ALU.subtract))
            last.then_inc(f_comb, 1)

            def step_f(s, u):
                buf = u % 2
                if has(s, 0, STEPS_F):
                    ve.wait_ge(f_h3, s + 1)
                    ve.wait_ge(f_silued, s + 1)
                    ve.tensor_tensor(f_t1[:, buf, :], f_silu[:, buf, :], ps[:, (3 * u + 1) % 4, :], ALU.mult).then_inc(f_m1, 1)
                    ve.wait_ge(f_m1, s + 1)
                    ve.wait_ge(f_cb, s + 1)
                    at_least(ve, f_glo, s - 1)
                    ve.tensor_tensor(f_t2[:, buf, :], f_t1[:, buf, :], ps[:, (3 * u + 2) % 4, :], ALU.mult).then_inc(f_m2, 1)

            steps(ve, STEPS_F, 4, 0, step_f)
            add_output(5, range(NT))


_OUT = (T, D)


def _chunks(w):
    k = w.shape[0] // P
    return w.reshape(k, P, w.shape[1]).transpose(1, 0, 2).reshape(P, -1)


def _out_rows(h):
    import numpy as np
    n = np.arange(D).reshape(KC, 2, 2, h.pairs, 2, h.width)
    return n.transpose(0, 1, 4, 3, 2, 5).reshape(-1)


def _value_columns(h):
    import numpy as np
    n = np.arange(D).reshape(KC, 2, 2, h.pairs, 2, h.width)
    return n.transpose(2, 0, 1, 4, 3, 5).reshape(-1)


def _layouts(i):
    import numpy as np

    def cat(*a):
        return np.ascontiguousarray(np.concatenate(a, axis=1))

    g = {}
    g["x"] = i["x"].reshape(T, D)
    g["w_a_qk"] = cat(_chunks(i["L0_attn_wq"].T), _chunks(i["L0_attn_wk"].T))
    g["w_a_vo"] = cat(_chunks(i["L0_attn_wv"].T[:, _value_columns(HA)]), _chunks(i["L0_attn_wo"].T[_out_rows(HA)]))
    g["w_ctx"] = i["ctx_1024"].reshape(T, P).T
    swap = np.arange(D).reshape(-1, 2)[:, ::-1].reshape(-1)
    wq, wk, wv = i["L0_xattn_Wq"], i["L0_xattn_Wkv"][:, :D], i["L0_xattn_Wkv"][:, D:]
    g["w_b_q"] = cat(_chunks(wq), _chunks(wq[:, swap]))
    g["w_b_kv"] = cat(wk, wk[:, swap], wv[:, _value_columns(HB)])
    g["w_b_o"] = _chunks(i["L0_xattn_Wout"][_out_rows(HB)])
    g["w_c_router_down"] = cat(_chunks(i["L0_ffn_w_router"]), _chunks(i["L0_ffn_shared_w_down"]), i["L0_ffn_w_down"])

    def gate_up(gate, up, js):
        return cat(*[_chunks(w[:, j * P:(j + 1) * P]) for j in js for w in (gate, up)])

    g["w_c_shared"] = gate_up(i["L0_ffn_shared_w_gate"], i["L0_ffn_shared_w_up"], range(2))
    for r in range(4):
        g[f"w_c_mix{r}"] = gate_up(i["L0_ffn_w_gate"], i["L0_ffn_w_up"], (2 * r, 2 * r + 1))
    qkv, wo = i["L1_attn_w_qkv"], i["L1_attn_w_o"]
    F = HEADS_D * P
    g["w_d"] = np.stack([cat(*[_chunks(qkv[:, n * F + h * P:n * F + (h + 1) * P]) for n in range(3)],
                             wo[h * P:(h + 1) * P]) for h in range(HEADS_D)])
    q, k, v, o = (i["L1_xattn_W" + n] for n in "qkvo")
    g["w_e"] = np.stack([cat(*[_chunks(q[:, h * P:(h + 1) * P]) for h in (2 * n, 2 * n + 1)],
                             k[:, n * P:(n + 1) * P],
                             o[2 * n * P:(2 * n + 1) * P], o[(2 * n + 1) * P:(2 * n + 2) * P]) for n in range(GROUPS_E)])

    g["w_e_v"] = v

    def rows(expert, shared):
        a = np.concatenate([expert, shared])
        return np.concatenate([a, np.zeros((CHUNKS_F * P - len(a), D), np.float32)])

    w1 = rows(i["L1_ffn_W1"].reshape(-1, D), i["L1_ffn_Ws1"])
    w3 = rows(i["L1_ffn_W3"].reshape(-1, D), i["L1_ffn_Ws3"])
    w2 = rows(i["L1_ffn_W2"].transpose(0, 2, 1).reshape(-1, D), i["L1_ffn_Ws2"].T)
    g["w_f"] = np.stack([cat(_chunks(w1[n * P:(n + 1) * P].T), _chunks(w3[n * P:(n + 1) * P].T),
                             w2[n * P:(n + 1) * P]) for n in range(CHUNKS_F)])
    g["gate"] = _chunks(i["L1_ffn_gate_w"].T)
    g["bias_col"] = cat(i["L0_attn_bq"].reshape(KC, P).T, i["L0_attn_bk"].reshape(KC, P).T)
    g["bias_rows"] = np.stack([i["L0_attn_bv"][_value_columns(HA)], i["L0_attn_bo"], i["L0_xattn_bout"]])
    g["pos"] = i["fside_BxSx2_0"].reshape(NT, P, 2).transpose(1, 0, 2)
    g["mask"] = i["mask_BxS2_bf1"].reshape(1, T).view(np.uint8)
    g["amps"] = i["L0_ffn_amplitudes"]
    g["e_scale"] = i["L0_ffn_expert_scale"].reshape(P, 1)

    p = np.arange(P)
    g["ident"] = np.eye(P, dtype=np.float32)
    g["iota"] = np.tile(p.astype(np.float32), (P, 1))
    g["head_mask"] = np.stack([(p // 16) % 2 == v for v in range(2)] + [(p // 8) % 4 == v for v in range(4)],
                              axis=1).astype(np.float32)
    g["lower"] = np.tile((np.arange(4)[None, :] < np.arange(4)[:, None]).astype(np.float32), (P, 1, 1))
    m = np.arange(8)
    freq = np.array([1.0, np.float32(10000.0) ** np.float32(-0.5)], np.float32)[(m % 4) // 2]
    freqs = np.stack([np.where(m % 2 == 0, -freq, freq), freq]).astype(np.float32)
    g["freqs"] = np.tile(freqs, (P, 1, 1))
    hidden = np.arange(CHUNKS_F * P)
    owner = np.where(hidden < 16 * 176, hidden // 176, 16)
    sel = np.zeros((96, CHUNKS_F * P), np.float32)
    for r in range(96):
        if r % 32 < 16 or r == 16:
            sel[r] = owner == r % 32
    g["select"] = (sel.reshape(96, CHUNKS_F, P) * 0x3F80).astype(np.uint16)
    return g


_INS = ['x', 'ctx_1024', 'fside_BxSx2_0', 'mask_BxS2_bf1', 'L0_attn_wq', 'L0_attn_bq', 'L0_attn_wk', 'L0_attn_bk',
        'L0_attn_wv', 'L0_attn_bv', 'L0_attn_wo', 'L0_attn_bo', 'L0_xattn_Wq', 'L0_xattn_Wkv', 'L0_xattn_Wout',
        'L0_xattn_bout', 'L0_ffn_w_router', 'L0_ffn_w_gate', 'L0_ffn_w_up', 'L0_ffn_w_down', 'L0_ffn_amplitudes',
        'L0_ffn_expert_scale', 'L0_ffn_shared_w_gate', 'L0_ffn_shared_w_up', 'L0_ffn_shared_w_down', 'L1_attn_w_qkv',
        'L1_attn_w_o', 'L1_xattn_Wq', 'L1_xattn_Wk', 'L1_xattn_Wv', 'L1_xattn_Wo', 'L1_ffn_gate_w', 'L1_ffn_W1',
        'L1_ffn_W2', 'L1_ffn_W3', 'L1_ffn_Ws1', 'L1_ffn_Ws2', 'L1_ffn_Ws3']


def kernel(**inputs):
    import numpy as _np
    import concourse.bacc as _bacc
    from concourse import mybir as _mybir
    from concourse.bass_utils import run_bass_kernel_spmd as _run

    nc = _bacc.Bacc("TRN2", target_bir_lowering=False, num_devices=1)
    laid = _layouts({n: _np.asarray(inputs[n]) for n in _INS})
    arrays, aps = {}, {}
    for name, a in laid.items():
        a = _np.ascontiguousarray(a)
        arrays[f"in_{name}"] = a
        aps[name] = nc.dram_tensor(f"in_{name}", a.shape, _mybir.dt.from_np(a.dtype), kind="ExternalInput").ap()
    out = nc.dram_tensor("out", _OUT, _mybir.dt.float32, kind="ExternalOutput").ap()
    decoder(nc, aps, out)
    r = _run(nc, [arrays], core_ids=[0])
    return r.results[0]["out"].reshape(B, S, D)
```
